# Optimizing a Trainium2 kernel written in Bass

```python
import numpy as np
import jax
import jax.numpy as jnp

def _softmax(x, axis=-1):
    return jax.nn.softmax(x, axis=axis)

def _gelu(x):
    return jax.nn.gelu(x, approximate=True)

def _silu(x):
    return jax.nn.silu(x)

def _sigmoid(x):
    return jax.nn.sigmoid(x)

def _layernorm(x, axis=-1, eps=1e-05):
    m = jnp.mean(x, axis=axis, keepdims=True)
    v = jnp.var(x, axis=axis, keepdims=True)
    return (x - m) / jnp.sqrt(v + eps)

def _scatter_add(tgt, idx, src, axis=0):
    return tgt.at[idx].add(src)

def _segment_sum(src, seg, n):
    return jax.ops.segment_sum(src, seg, n)
kernel_name = 'mk_decoder_postln_d2_seqx_r8_e5da28'

def setup_inputs(seed: int=0):
    np.random.seed(seed)
    _w = jnp.asarray

    def _rec_inputs():
        import jax
        import jax.numpy as jnp
        _rk = jax.random.key(seed)
        x = -0.0005146 + 1 * jax.random.normal(jax.random.fold_in(_rk, 1), (4, 512, 128), jnp.float32)
        _lenS = 512 - jax.random.randint(jax.random.fold_in(_rk, 7), (4,), 0, max(1, 512 // 4) + 1, jnp.int32)
        _lenS2 = 154 - jax.random.randint(jax.random.fold_in(_rk, 8), (4,), 0, max(1, 154 // 4) + 1, jnp.int32)
        _ctx_1024P = jax.random.normal(jax.random.fold_in(_rk, 11), (4, 16, 128), jnp.float32)
        _ctx_1024c = jax.random.dirichlet(jax.random.fold_in(_rk, 511), 0.3 * jnp.ones((16,), jnp.float32), (4, 154))
        _ctx_1024t = jnp.einsum('bsk,bkd->bsd', _ctx_1024c, _ctx_1024P)
        _ctx_1024t = _ctx_1024t * jax.lax.rsqrt(jnp.mean(jnp.square(_ctx_1024t)) + 1e-12) * 0.953939
        ctx_1024 = -0.000392918 + 0.999932 * (_ctx_1024t + 0.3 * jax.random.normal(jax.random.fold_in(_rk, 611), (4, 154, 128), jnp.float32))
        _validS = jnp.arange(512)[None, :] < _lenS[:, None]
        _validS2 = jnp.arange(154)[None, :] < _lenS2[:, None]
        _causal = jnp.tril(jnp.ones((512, 512), dtype=bool))
        mask_BxS2_ik1 = jnp.where(jnp.broadcast_to(_validS2[:, :], (4, 154)), 1, 0).astype(jnp.int32)
        return (x, ctx_1024, mask_BxS2_ik1)
    x, ctx_1024, mask_BxS2_ik1 = _rec_inputs()

    def _L0_attn_setup():
        import jax, jax.numpy as jnp
        import numpy as np
        DIM = 128
        HEADS = 16
        THS = 0.5
        C = float(np.e) * float(np.sqrt(1.0 / DIM))

        def _pm_c(key, shape):
            return jnp.where(jax.random.bernoulli(key, 0.5, shape), C, -C).astype(jnp.float32)
        key = jax.random.key(seed)
        ks = jax.random.split(key, 7)
        b, n = (2, 256)
        return {'x': jax.random.normal(ks[0], (b, n, DIM), jnp.float32), 'qkv_weight': _pm_c(ks[1], (3 * DIM, DIM)), 'qkv_weight_mask': jax.random.normal(ks[2], (3 * DIM, DIM), jnp.float32), 'out_weight': _pm_c(ks[3], (DIM, DIM)), 'out_weight_mask': jax.random.normal(ks[4], (DIM, DIM), jnp.float32), 'out_bias': _pm_c(ks[5], (DIM,)), 'out_bias_mask': jax.random.normal(ks[6], (DIM,), jnp.float32)}
    _L0_attn_all = _L0_attn_setup()
    _L0_attn_in = {k: v for k, v in _L0_attn_all.items() if k in ('qkv_weight', 'qkv_weight_mask', 'out_weight', 'out_weight_mask', 'out_bias', 'out_bias_mask')}
    del _L0_attn_all

    def _L0_xattn_setup():
        import jax, jax.numpy as jnp
        import numpy as np
        DIM = 128
        DIM_HEAD = 64
        HEADS = 16
        INNER = DIM_HEAD * HEADS
        EPS = 1e-05

        def layer_norm(x, g, b):
            m = jnp.mean(x, axis=-1, keepdims=True)
            v = jnp.mean(jnp.square(x - m), axis=-1, keepdims=True)
            return (x - m) * jax.lax.rsqrt(v + EPS) * g + b
        key = jax.random.key(seed)
        ks = jax.random.split(key, 8)
        B, N_IMG, N_LAT = (4, 512, 64)
        std = 1.0 / np.sqrt(DIM)
        return {'image_embeds': jax.random.normal(ks[0], (B, N_IMG, DIM), dtype=jnp.float32), 'latents': jax.random.normal(ks[1], (B, N_LAT, DIM), dtype=jnp.float32), 'ln1_g': jnp.ones((DIM,), jnp.float32), 'ln1_b': jnp.zeros((DIM,), jnp.float32), 'ln2_g': jnp.ones((DIM,), jnp.float32), 'ln2_b': jnp.zeros((DIM,), jnp.float32), 'Wq': jax.random.normal(ks[2], (DIM, INNER), dtype=jnp.float32) * std, 'Wkv': jax.random.normal(ks[3], (DIM, 2 * INNER), dtype=jnp.float32) * std, 'Wo': jax.random.normal(ks[4], (INNER, DIM), dtype=jnp.float32) * std}
    _L0_xattn_all = _L0_xattn_setup()
    _L0_xattn_in = {k: v for k, v in _L0_xattn_all.items() if k in ('ln1_g', 'ln1_b', 'ln2_g', 'ln2_b', 'Wq', 'Wkv', 'Wo')}
    del _L0_xattn_all

    def _L0_ffn_setup():
        import jax, jax.numpy as jnp
        import numpy as np
        DIM = 128
        EXPERT_DIM = 64
        N_EXPERTS = 16
        TOPK = 2
        SHARED_HIDDEN = EXPERT_DIM * TOPK
        B, T = (4, 128)

        def _moe_forward(x, router_w, router_bias, up_proj, gate_proj, down_proj, sh_gate, sh_up, sh_down):
            Bb, Tt, D = x.shape
            flat = x.reshape(Bb * Tt, D)
            N = flat.shape[0]
            logits = flat @ router_w.T
            topk_scores, topk_idx = jax.lax.top_k(logits + router_bias, TOPK)
            topk_scores = jax.nn.softmax(topk_scores, axis=-1)
            combine = jnp.zeros((N, N_EXPERTS), flat.dtype)
            combine = combine.at[jnp.arange(N)[:, None], topk_idx].add(topk_scores)
            up_all = jnp.einsum('nd,kde->nke', flat, up_proj)
            gate_all = jnp.einsum('nd,kde->nke', flat, gate_proj)
            hidden = jax.nn.silu(gate_all) * up_all
            down_all = jnp.einsum('nke,ked->nkd', hidden, down_proj)
            out = jnp.einsum('nk,nkd->nd', combine, down_all)
            sh_hidden = jax.nn.silu(flat @ sh_gate.T) * (flat @ sh_up.T)
            out = out + sh_hidden @ sh_down.T
            return out.reshape(Bb, Tt, D)
        key = jax.random.key(seed)
        ks = jax.random.split(key, 9)
        std = 0.02
        return {'x': jax.random.normal(ks[0], (B, T, DIM), jnp.float32), 'router_w': jax.random.normal(ks[1], (N_EXPERTS, DIM), jnp.float32) * std, 'router_bias': jnp.zeros((N_EXPERTS,), jnp.float32), 'up_proj': jax.random.normal(ks[2], (N_EXPERTS, DIM, EXPERT_DIM), jnp.float32) * std, 'gate_proj': jax.random.normal(ks[3], (N_EXPERTS, DIM, EXPERT_DIM), jnp.float32) * std, 'down_proj': jax.random.normal(ks[4], (N_EXPERTS, EXPERT_DIM, DIM), jnp.float32) * std, 'sh_gate': jax.random.normal(ks[5], (SHARED_HIDDEN, DIM), jnp.float32) * std, 'sh_up': jax.random.normal(ks[6], (SHARED_HIDDEN, DIM), jnp.float32) * std, 'sh_down': jax.random.normal(ks[7], (DIM, SHARED_HIDDEN), jnp.float32) * std}
    _L0_ffn_all = _L0_ffn_setup()
    _L0_ffn_in = {k: v for k, v in _L0_ffn_all.items() if k in ('router_w', 'router_bias', 'up_proj', 'gate_proj', 'down_proj', 'sh_gate', 'sh_up', 'sh_down')}
    del _L0_ffn_all

    def _L1_attn_setup():
        import jax, jax.numpy as jnp
        import numpy as np
        from jax import lax
        D_MODEL = 128
        N_HEADS = 16
        D_HEAD = 64
        INNER = N_HEADS * D_HEAD
        EPS = 1e-12

        def _delta_net(x, Wq, Wk, Wv, Wbeta, b_beta, Wout):
            B, T, _ = x.shape
            H, D = (N_HEADS, D_HEAD)
            Q = (x @ Wq).reshape(B, T, H, D)
            K = (x @ Wk).reshape(B, T, H, D)
            V = (x @ Wv).reshape(B, T, H, D)
            beta = jax.nn.sigmoid(x @ Wbeta + b_beta)
            K = K / jnp.maximum(jnp.linalg.norm(K, axis=-1, keepdims=True), EPS)
            xs = (jnp.moveaxis(Q, 1, 0), jnp.moveaxis(K, 1, 0), jnp.moveaxis(V, 1, 0), jnp.moveaxis(beta, 1, 0))

            def step(W, inp):
                q_t, k_t, v_t, b_t = inp
                pred = jnp.einsum('bhij,bhj->bhi', W, k_t)
                err = v_t - pred
                W_new = W + b_t[..., None, None] * jnp.einsum('bhi,bhj->bhij', err, k_t)
                o_t = jnp.einsum('bhij,bhj->bhi', W_new, q_t)
                return (W_new, o_t)
            W0 = jnp.zeros((B, H, D, D), dtype=x.dtype)
            _, O = lax.scan(step, W0, xs)
            out = jnp.moveaxis(O, 0, 1).reshape(B, T, H * D)
            return out @ Wout
        key = jax.random.key(seed)
        ks = jax.random.split(key, 7)
        B, T = (4, 256)
        s = 1.0 / np.sqrt(D_MODEL)
        return {'x': jax.random.normal(ks[0], (B, T, D_MODEL), dtype=jnp.float32), 'Wq': jax.random.normal(ks[1], (D_MODEL, INNER), dtype=jnp.float32) * s, 'Wk': jax.random.normal(ks[2], (D_MODEL, INNER), dtype=jnp.float32) * s, 'Wv': jax.random.normal(ks[3], (D_MODEL, INNER), dtype=jnp.float32) * s, 'Wbeta': jax.random.normal(ks[4], (D_MODEL, N_HEADS), dtype=jnp.float32) * s, 'b_beta': jax.random.normal(ks[5], (N_HEADS,), dtype=jnp.float32) * 0.01, 'Wout': jax.random.normal(ks[6], (INNER, D_MODEL), dtype=jnp.float32) * (1.0 / np.sqrt(INNER))}
    _L1_attn_all = _L1_attn_setup()
    _L1_attn_in = {k: v for k, v in _L1_attn_all.items() if k in ('Wq', 'Wk', 'Wv', 'Wbeta', 'b_beta', 'Wout')}
    del _L1_attn_all

    def _L1_xattn_setup():
        import jax, jax.numpy as jnp
        import numpy as np
        import math
        HDIM = 128
        B, L1, L2 = (8, 256, 256)
        key = jax.random.key(seed)
        ks = jax.random.split(key, 10)
        s = 1.0 / math.sqrt(HDIM)
        return {'Q': jax.random.normal(ks[0], (B, L1, HDIM), jnp.float32), 'K': jax.random.normal(ks[1], (B, L2, HDIM), jnp.float32), 'V': jax.random.normal(ks[2], (B, L2, HDIM), jnp.float32), 'K_mask': jax.random.randint(ks[3], (B, L2), 0, 2, jnp.int32), 'Wx': jax.random.normal(ks[4], (HDIM, HDIM), jnp.float32) * s, 'bx': jnp.zeros((HDIM,), jnp.float32), 'Wy': jax.random.normal(ks[5], (HDIM, HDIM), jnp.float32) * s, 'by': jnp.zeros((HDIM,), jnp.float32), 'Wv': jax.random.normal(ks[6], (HDIM, HDIM), jnp.float32) * s, 'bv': jnp.zeros((HDIM,), jnp.float32)}
    _L1_xattn_all = _L1_xattn_setup()
    _L1_xattn_in = {k: v for k, v in _L1_xattn_all.items() if k in ('Wx', 'bx', 'Wy', 'by', 'Wv', 'bv')}
    del _L1_xattn_all

    def _L1_ffn_setup():
        import jax, jax.numpy as jnp
        import numpy as np
        LN_EPS = 1e-12
        key = jax.random.key(seed)
        ks = jax.random.split(key, 8)
        B, S, H, I, E = (4, 256, 128, 512, 8)
        sH = 1.0 / np.sqrt(H)
        sI = 1.0 / np.sqrt(I)
        return {'hidden_states': jax.random.normal(ks[0], (B, S, H), dtype=jnp.float32), 'Wr': jax.random.uniform(ks[1], (E, H), jnp.float32, -sH, sH), 'W1': jax.random.uniform(ks[2], (E, H, I), jnp.float32, -sH, sH), 'b1': jax.random.uniform(ks[3], (E, I), jnp.float32, -sH, sH), 'Wo': jax.random.uniform(ks[4], (I, H), jnp.float32, -sI, sI), 'bo': jax.random.uniform(ks[5], (H,), jnp.float32, -sI, sI), 'gamma': jnp.ones((H,), jnp.float32), 'beta': jnp.zeros((H,), jnp.float32)}
    _L1_ffn_all = _L1_ffn_setup()
    _L1_ffn_in = {k: v for k, v in _L1_ffn_all.items() if k in ('Wr', 'W1', 'b1', 'Wo', 'bo', 'gamma', 'beta')}
    del _L1_ffn_all
    return {'x': x, 'ctx_1024': ctx_1024, 'mask_BxS2_ik1': mask_BxS2_ik1, 'L0_attn_qkv_weight': _L0_attn_in['qkv_weight'], 'L0_attn_qkv_weight_mask': _L0_attn_in['qkv_weight_mask'], 'L0_attn_out_weight': _L0_attn_in['out_weight'], 'L0_attn_out_weight_mask': _L0_attn_in['out_weight_mask'], 'L0_attn_out_bias': _L0_attn_in['out_bias'], 'L0_attn_out_bias_mask': _L0_attn_in['out_bias_mask'], 'L0_xattn_ln1_g': _L0_xattn_in['ln1_g'], 'L0_xattn_ln1_b': _L0_xattn_in['ln1_b'], 'L0_xattn_ln2_g': _L0_xattn_in['ln2_g'], 'L0_xattn_ln2_b': _L0_xattn_in['ln2_b'], 'L0_xattn_Wq': _L0_xattn_in['Wq'], 'L0_xattn_Wkv': _L0_xattn_in['Wkv'], 'L0_xattn_Wo': _L0_xattn_in['Wo'], 'L0_ffn_router_w': _L0_ffn_in['router_w'], 'L0_ffn_router_bias': _L0_ffn_in['router_bias'], 'L0_ffn_up_proj': _L0_ffn_in['up_proj'], 'L0_ffn_gate_proj': _L0_ffn_in['gate_proj'], 'L0_ffn_down_proj': _L0_ffn_in['down_proj'], 'L0_ffn_sh_gate': _L0_ffn_in['sh_gate'], 'L0_ffn_sh_up': _L0_ffn_in['sh_up'], 'L0_ffn_sh_down': _L0_ffn_in['sh_down'], 'L1_attn_Wq': _L1_attn_in['Wq'], 'L1_attn_Wk': _L1_attn_in['Wk'], 'L1_attn_Wv': _L1_attn_in['Wv'], 'L1_attn_Wbeta': _L1_attn_in['Wbeta'], 'L1_attn_b_beta': _L1_attn_in['b_beta'], 'L1_attn_Wout': _L1_attn_in['Wout'], 'L1_xattn_Wx': _L1_xattn_in['Wx'], 'L1_xattn_bx': _L1_xattn_in['bx'], 'L1_xattn_Wy': _L1_xattn_in['Wy'], 'L1_xattn_by': _L1_xattn_in['by'], 'L1_xattn_Wv': _L1_xattn_in['Wv'], 'L1_xattn_bv': _L1_xattn_in['bv'], 'L1_ffn_Wr': _L1_ffn_in['Wr'], 'L1_ffn_W1': _L1_ffn_in['W1'], 'L1_ffn_b1': _L1_ffn_in['b1'], 'L1_ffn_Wo': _L1_ffn_in['Wo'], 'L1_ffn_bo': _L1_ffn_in['bo'], 'L1_ffn_gamma': _L1_ffn_in['gamma'], 'L1_ffn_beta': _L1_ffn_in['beta']}

def reference(x, ctx_1024, mask_BxS2_ik1, L0_attn_qkv_weight, L0_attn_qkv_weight_mask, L0_attn_out_weight, L0_attn_out_weight_mask, L0_attn_out_bias, L0_attn_out_bias_mask, L0_xattn_ln1_g, L0_xattn_ln1_b, L0_xattn_ln2_g, L0_xattn_ln2_b, L0_xattn_Wq, L0_xattn_Wkv, L0_xattn_Wo, L0_ffn_router_w, L0_ffn_router_bias, L0_ffn_up_proj, L0_ffn_gate_proj, L0_ffn_down_proj, L0_ffn_sh_gate, L0_ffn_sh_up, L0_ffn_sh_down, L1_attn_Wq, L1_attn_Wk, L1_attn_Wv, L1_attn_Wbeta, L1_attn_b_beta, L1_attn_Wout, L1_xattn_Wx, L1_xattn_bx, L1_xattn_Wy, L1_xattn_by, L1_xattn_Wv, L1_xattn_bv, L1_ffn_Wr, L1_ffn_W1, L1_ffn_b1, L1_ffn_Wo, L1_ffn_bo, L1_ffn_gamma, L1_ffn_beta):
    import jax
    import jax.numpy as jnp

    def _L0_attn_ref(x, qkv_weight, qkv_weight_mask, out_weight, out_weight_mask, out_bias, out_bias_mask):
        import jax, jax.numpy as jnp
        import numpy as np
        DIM = 128
        HEADS = 16
        THS = 0.5
        C = float(np.e) * float(np.sqrt(1.0 / DIM))

        def _pm_c(key, shape):
            return jnp.where(jax.random.bernoulli(key, 0.5, shape), C, -C).astype(jnp.float32)
        b, n, _ = x.shape
        h, d = (HEADS, DIM // HEADS)
        dt = x.dtype
        g_qkv = (jax.nn.sigmoid(qkv_weight_mask) > THS).astype(dt)
        qkv = jnp.einsum('bnk,ok->bno', x, g_qkv * qkv_weight)
        qkv = qkv.reshape(b, n, 3, h, d)
        q, k, v = (jnp.transpose(qkv[:, :, i], (0, 2, 1, 3)) for i in range(3))
        scale = DIM ** (-0.5)
        dots = jnp.einsum('bhid,bhjd->bhij', q, k) * scale
        attn = jax.nn.softmax(dots, axis=-1)
        out = jnp.einsum('bhij,bhjd->bhid', attn, v)
        out = jnp.transpose(out, (0, 2, 1, 3)).reshape(b, n, h * d)
        g_w = (jax.nn.sigmoid(out_weight_mask) > THS).astype(dt)
        g_b = (jax.nn.sigmoid(out_bias_mask) > THS).astype(dt)
        out = jnp.einsum('bnk,ok->bno', out, g_w * out_weight) + g_b * out_bias
        return out

    def _L0_xattn_ref(image_embeds, latents, ln1_g, ln1_b, ln2_g, ln2_b, Wq, Wkv, Wo):
        import jax, jax.numpy as jnp
        import numpy as np
        DIM = 128
        DIM_HEAD = 64
        HEADS = 16
        INNER = DIM_HEAD * HEADS
        EPS = 1e-05

        def layer_norm(x, g, b):
            m = jnp.mean(x, axis=-1, keepdims=True)
            v = jnp.mean(jnp.square(x - m), axis=-1, keepdims=True)
            return (x - m) * jax.lax.rsqrt(v + EPS) * g + b
        B, S_lat, _ = latents.shape
        x = layer_norm(image_embeds, ln1_g, ln1_b)
        l = layer_norm(latents, ln2_g, ln2_b)
        q = l @ Wq
        kv_in = jnp.concatenate([x, l], axis=1)
        kv = kv_in @ Wkv
        k, v = jnp.split(kv, 2, axis=-1)

        def to_heads(t):
            return t.reshape(t.shape[0], t.shape[1], HEADS, DIM_HEAD).transpose(0, 2, 1, 3)
        q, k, v = (to_heads(q), to_heads(k), to_heads(v))
        scale = 1.0 / np.sqrt(np.sqrt(DIM_HEAD))
        w = jnp.einsum('bhqd,bhkd->bhqk', q * scale, k * scale)
        w = jax.nn.softmax(w.astype(jnp.float32), axis=-1).astype(q.dtype)
        out = jnp.einsum('bhqk,bhkd->bhqd', w, v)
        out = out.transpose(0, 2, 1, 3).reshape(B, S_lat, INNER)
        return out @ Wo

    def _L0_ffn_ref(x, router_w, router_bias, up_proj, gate_proj, down_proj, sh_gate, sh_up, sh_down):
        import jax, jax.numpy as jnp
        import numpy as np
        DIM = 128
        EXPERT_DIM = 64
        N_EXPERTS = 16
        TOPK = 2
        SHARED_HIDDEN = EXPERT_DIM * TOPK
        B, T = (4, 128)

        def _moe_forward(x, router_w, router_bias, up_proj, gate_proj, down_proj, sh_gate, sh_up, sh_down):
            Bb, Tt, D = x.shape
            flat = x.reshape(Bb * Tt, D)
            N = flat.shape[0]
            logits = flat @ router_w.T
            topk_scores, topk_idx = jax.lax.top_k(logits + router_bias, TOPK)
            topk_scores = jax.nn.softmax(topk_scores, axis=-1)
            combine = jnp.zeros((N, N_EXPERTS), flat.dtype)
            combine = combine.at[jnp.arange(N)[:, None], topk_idx].add(topk_scores)
            up_all = jnp.einsum('nd,kde->nke', flat, up_proj)
            gate_all = jnp.einsum('nd,kde->nke', flat, gate_proj)
            hidden = jax.nn.silu(gate_all) * up_all
            down_all = jnp.einsum('nke,ked->nkd', hidden, down_proj)
            out = jnp.einsum('nk,nkd->nd', combine, down_all)
            sh_hidden = jax.nn.silu(flat @ sh_gate.T) * (flat @ sh_up.T)
            out = out + sh_hidden @ sh_down.T
            return out.reshape(Bb, Tt, D)
        return _moe_forward(x, router_w, router_bias, up_proj, gate_proj, down_proj, sh_gate, sh_up, sh_down)

    def _L1_attn_ref(x, Wq, Wk, Wv, Wbeta, b_beta, Wout):
        import jax, jax.numpy as jnp
        import numpy as np
        from jax import lax
        D_MODEL = 128
        N_HEADS = 16
        D_HEAD = 64
        INNER = N_HEADS * D_HEAD
        EPS = 1e-12

        def _delta_net(x, Wq, Wk, Wv, Wbeta, b_beta, Wout):
            B, T, _ = x.shape
            H, D = (N_HEADS, D_HEAD)
            Q = (x @ Wq).reshape(B, T, H, D)
            K = (x @ Wk).reshape(B, T, H, D)
            V = (x @ Wv).reshape(B, T, H, D)
            beta = jax.nn.sigmoid(x @ Wbeta + b_beta)
            K = K / jnp.maximum(jnp.linalg.norm(K, axis=-1, keepdims=True), EPS)
            xs = (jnp.moveaxis(Q, 1, 0), jnp.moveaxis(K, 1, 0), jnp.moveaxis(V, 1, 0), jnp.moveaxis(beta, 1, 0))

            def step(W, inp):
                q_t, k_t, v_t, b_t = inp
                pred = jnp.einsum('bhij,bhj->bhi', W, k_t)
                err = v_t - pred
                W_new = W + b_t[..., None, None] * jnp.einsum('bhi,bhj->bhij', err, k_t)
                o_t = jnp.einsum('bhij,bhj->bhi', W_new, q_t)
                return (W_new, o_t)
            W0 = jnp.zeros((B, H, D, D), dtype=x.dtype)
            _, O = lax.scan(step, W0, xs)
            out = jnp.moveaxis(O, 0, 1).reshape(B, T, H * D)
            return out @ Wout
        return _delta_net(x, Wq, Wk, Wv, Wbeta, b_beta, Wout)

    def _L1_xattn_ref(Q, K, V, K_mask, Wx, bx, Wy, by, Wv, bv):
        import jax, jax.numpy as jnp
        import numpy as np
        import math
        HDIM = 128
        B, L1, L2 = (8, 256, 256)
        Qp = jnp.einsum('bld,ed->ble', Q, Wx) + bx
        Kp = jnp.einsum('bld,ed->ble', K, Wy) + by
        Vp = jnp.einsum('bld,ed->ble', V, Wv) + bv
        scale = 1.0 / math.sqrt(Q.shape[-1])
        scores = jnp.einsum('bqd,bkd->bqk', Qp, Kp) * scale
        scores = jnp.where((K_mask == 1)[:, None, :], -jnp.inf, scores)
        alpha = jax.nn.softmax(scores, axis=-1)
        return jnp.einsum('bqk,bkd->bqd', alpha, Vp)

    def _L1_ffn_ref(hidden_states, Wr, W1, b1, Wo, bo, gamma, beta):
        import jax, jax.numpy as jnp
        import numpy as np
        LN_EPS = 1e-12
        B, S, H = hidden_states.shape
        E = Wr.shape[0]
        x = hidden_states.reshape(-1, H)
        router_logits = x @ Wr.T
        expert_idx = jnp.argmax(jax.nn.softmax(router_logits, axis=-1), axis=-1)
        inter = jnp.zeros((x.shape[0], W1.shape[2]), dtype=x.dtype)
        for e in range(E):
            mask = (expert_idx == e)[:, None].astype(x.dtype)
            inter = inter + mask * jax.nn.gelu(x @ W1[e] + b1[e], approximate=False)
        y = inter @ Wo + bo + x
        mu = jnp.mean(y, axis=-1, keepdims=True)
        var = jnp.mean(jnp.square(y - mu), axis=-1, keepdims=True)
        out = (y - mu) * jax.lax.rsqrt(var + LN_EPS) * gamma + beta
        return out.reshape(B, S, H)
    x = _layernorm(x + _L0_attn_ref(x, L0_attn_qkv_weight, L0_attn_qkv_weight_mask, L0_attn_out_weight, L0_attn_out_weight_mask, L0_attn_out_bias, L0_attn_out_bias_mask), axis=-1)
    x = _layernorm(x + _L0_xattn_ref(ctx_1024, x, L0_xattn_ln1_g, L0_xattn_ln1_b, L0_xattn_ln2_g, L0_xattn_ln2_b, L0_xattn_Wq, L0_xattn_Wkv, L0_xattn_Wo), axis=-1)
    x = _layernorm(x + _L0_ffn_ref(x, L0_ffn_router_w, L0_ffn_router_bias, L0_ffn_up_proj, L0_ffn_gate_proj, L0_ffn_down_proj, L0_ffn_sh_gate, L0_ffn_sh_up, L0_ffn_sh_down), axis=-1)
    x = _layernorm(x + _L1_attn_ref(x, L1_attn_Wq, L1_attn_Wk, L1_attn_Wv, L1_attn_Wbeta, L1_attn_b_beta, L1_attn_Wout), axis=-1)
    x = _layernorm(x + _L1_xattn_ref(x, ctx_1024, ctx_1024, mask_BxS2_ik1, L1_xattn_Wx, L1_xattn_bx, L1_xattn_Wy, L1_xattn_by, L1_xattn_Wv, L1_xattn_bv), axis=-1)
    x = _layernorm(x + _L1_ffn_ref(x, L1_ffn_Wr, L1_ffn_W1, L1_ffn_b1, L1_ffn_Wo, L1_ffn_bo, L1_ffn_gamma, L1_ffn_beta), axis=-1)
    return x

_drawn_inputs = setup_inputs


def setup_inputs(seed=0):
    import zlib

    import numpy as np

    out = dict(_drawn_inputs(seed))
    spreads = {'L0_xattn_ln1_g': (1.0, 0.2),
     'L0_xattn_ln1_b': (0.0, 0.1),
     'L0_xattn_ln2_g': (1.0, 0.2),
     'L0_xattn_ln2_b': (0.0, 0.1),
     'L0_ffn_router_bias': (0.0, 0.8),
     'L1_xattn_bx': (0.0, 0.276),
     'L1_xattn_by': (0.0, 0.8),
     'L1_xattn_bv': (0.0, 0.1),
     'L1_ffn_gamma': (1.0, 0.2),
     'L1_ffn_beta': (0.0, 0.1)}
    factors = {'L0_ffn_router_w': 7.856,
     'L0_ffn_up_proj': 6.948,
     'L0_ffn_gate_proj': 8.0,
     'L0_ffn_down_proj': 8.0,
     'L0_ffn_sh_gate': 5.44,
     'L0_ffn_sh_up': 5.336,
     'L0_ffn_sh_down': 5.41,
     'L1_attn_b_beta': 8.0,
     'L1_ffn_b1': 6.393,
     'L1_ffn_bo': 4.019}
    for name, (base, spread) in spreads.items():
        noise = np.random.default_rng([zlib.crc32(name.encode()), seed]).standard_normal(out[name].shape)
        drawn = base * np.exp(spread * noise) if base else spread * noise
        out[name] = jnp.asarray(drawn.astype(out[name].dtype))
    for name, factor in factors.items():
        out[name] = (out[name] * factor).astype(out[name].dtype)
    return out
```

```python
from contextlib import ExitStack

import numpy as np
import concourse.bass as bass
from concourse import mybir

F32 = mybir.dt.float32
F16 = mybir.dt.float16
I32 = mybir.dt.int32
U32 = mybir.dt.uint32
ALU = mybir.AluOpType
ACT = mybir.ActivationFunctionType
AX = mybir.AxisListType.X

NB, T, D, TC = 4, 512, 128, 154
NT = NB * T // 128
ARENA = 47800


class Eng:

    def __init__(self, name, sem):
        self.name, self.sem, self.q, self.n, self.seen = name, sem, [], 0, {}

    def wait(self, *tokens):
        for t in tokens:
            if t is None:
                continue
            if isinstance(t, list):
                self.wait(*t)
                continue
            sem, v = t
            if self.seen.get(id(sem), 0) < v:
                self.seen[id(sem)] = v
                self.q.append(lambda e, sem=sem, v=v: e.wait_ge(sem, v))

    def op(self, f, inc=True):
        if self.name == "pool":
            self.wait(self.last)
        if inc:
            self.n += 1
            self.q.append(lambda e: f(e).then_inc(self.sem, 1))
        else:
            self.q.append(f)
        return (self.sem, self.n)

    @property
    def last(self):
        return (self.sem, self.n)


def build(nc, io, phases=6):
    with ExitStack() as ctx:
        def sb(name, shape, dt):
            return ctx.enter_context(nc.sbuf_tensor("sb_" + name, shape, dt))

        def sem(name):
            return ctx.enter_context(nc.semaphore(name))

        PE, DV, AC, PO = (Eng(n, sem("s_" + n)) for n in ("pe", "dve", "act", "pool"))
        SP = Eng("sp", sem("s_sp"))
        compute = (PE, DV, AC, PO)

        arena = sb("arena", [128, ARENA], F32)
        top = [0]

        def take(words, dt=F32):
            a = arena[:, top[0]:top[0] + words]
            top[0] += words
            assert top[0] <= ARENA, top[0]
            return a if dt == F32 else a.bitcast(dt)

        PS = ctx.enter_context(nc.psum_tensor("ps", [128, 8, 512], F32))
        RING = 6
        ptr = [0]
        freed = [None] * 8

        def banks(n=1):
            if ptr[0] + n > RING:
                ptr[0] = 0
            b = ptr[0]
            ptr[0] = (b + n) % RING
            PE.wait(*freed[b:b + n])
            return b

        def free(b, n, *tokens):
            for i in range(b, b + n):
                freed[i] = list(tokens)

        dma_sems = {}

        def dma(group, out, in_, *waits, eng=None):
            eng = eng or SP
            if group not in dma_sems:
                dma_sems[group] = [sem("d_" + group), 0]
            s = dma_sems[group]
            s[1] += 16
            eng.wait(*waits)
            eng.q.append(lambda e: e.dma_start(out, in_).then_inc(s[0], 16))
            return (s[0], s[1])

        def barrier():
            tokens = [e.last for e in compute] + [(s[0], s[1]) for s in dma_sems.values()]
            for e in compute + (SP,):
                e.wait(*tokens)
            for i in range(8):
                freed[i] = None

        def mm(out, lhsT, rhs, start=True, stop=True, inc=False):
            return PE.op(lambda e: e.matmul(out, lhsT, rhs, start=start, stop=stop,
                                            skip_group_check=True), inc)

        def tr(out, a, inc=False):
            return PE.op(lambda e: e.transpose(out, a, ident[:]), inc)

        def tt(eng, out, a, b, op):
            return eng.op(lambda e: e.tensor_tensor(out, a, b, op))

        def ts(eng, out, a, s1, op0, s2=None, op1=None):
            if op1 is None:
                return eng.op(lambda e: e.tensor_scalar(out, a, s1, None, op0))
            return eng.op(lambda e: e.tensor_scalar(out, a, s1, s2, op0, op1))

        def stt(out, a, s, b, op0, op1):
            return DV.op(lambda e: e.scalar_tensor_tensor(out=out, in0=a, scalar=s, in1=b, op0=op0, op1=op1))

        def cp(eng, out, a):
            if eng is AC:
                return AC.op(lambda e: e.activation(out, a, ACT.Copy))
            return eng.op(lambda e: e.tensor_copy(out, a))

        def act(out, a, f, scale=1.0, bias=0.0):
            return AC.op(lambda e: e.activation(out, a, f, scale=scale, bias=bias))

        def red(out, a, op):
            return DV.op(lambda e: e.tensor_reduce(out, a, AX, op))

        def recip(out, a):
            return DV.op(lambda e: e.reciprocal(out, a))

        def D1(tok):
            DV.wait(tok)
            return tok

        X = sb("X", [128, NT, 128], F32)
        XT = sb("XT", [128, NB * T], F32)
        ident = sb("ident", [128, 128], F32)
        ident16 = sb("ident16", [128, 128], F16)
        ones = sb("ones", [128, 128], F32)
        one16 = sb("one16", [1, 512], F16)
        sq = sb("sq", [128, 4, 128], F32)
        st = sb("st", [128, 12, 4], F32)
        magic = 0x5F3759DF

        ld = [dma("c", X[:], io["x_tm"]), dma("c", XT[:], io["x_T"]), dma("c", ident[:], io["ident"])][-1]
        DV.wait(ld)
        DV.op(lambda e: e.memset(ones[:], 1.0))
        DV.op(lambda e: e.memset(one16[:], 1.0))
        base = cp(DV, ident16[:], ident[:])
        for e in compute + (SP,):
            e.wait(ld, base)

        xt_ready = [None] * NB
        x_ready = [None] * NB

        def rsqrt(v, y, a, b):
            D1(DV.op(lambda e: e.tensor_scalar(a.bitcast(I32), v.bitcast(I32), 1, None,
                                               ALU.logical_shift_right)))
            D1(DV.op(lambda e: e.tensor_scalar(y.bitcast(I32), a.bitcast(I32), -1.0, float(magic),
                                               ALU.mult, ALU.add)))
            for _ in range(4):
                D1(tt(DV, a, y, y, ALU.mult))
                D1(stt(b, a, -0.5, v, ALU.mult, ALU.mult))
                t = D1(stt(y, b, 1.5, y, ALU.add, ALU.mult))
            return t

        def bc(a, n):
            return a.unsqueeze(2).broadcast_to([a.shape[0], a.shape[1], n])

        def normalize(x, eps, out=None):
            out = x if out is None else out
            D1(red(st[:, 0, :], x, ALU.add))
            D1(ts(DV, st[:, 1, :], st[:, 0, :], 1.0 / D, ALU.mult))
            D1(tt(DV, out, x, bc(st[:, 1, :], D), ALU.subtract))
            D1(tt(DV, sq[:], out, out, ALU.mult))
            D1(red(st[:, 2, :], sq[:], ALU.add))
            D1(ts(DV, st[:, 3, :], st[:, 2, :], 1.0 / D, ALU.mult, eps, ALU.add))
            rsqrt(st[:, 3, :], st[:, 4, :], st[:, 5, :], st[:, 6, :])
            return D1(tt(DV, out, out, bc(st[:, 4, :], D), ALU.mult))

        def transpose4(src, ready):
            b = banks()
            PE.wait(ready)
            for j in range(4):
                t = tr(PS[:, b, 128 * j:128 * j + 128], src[:, j, :], j == 3)
            return b, t

        def residual(b, ps, ps_ready, eps=1e-5):
            xb = X[:, 4 * b:4 * b + 4, :]
            DV.wait(ps_ready, x_ready[b], xt_ready[b])
            t = D1(tt(DV, xb, xb, PS[:, ps, :].rearrange("p (a b) -> p a b", a=4), ALU.add))
            free(ps, 1, t)
            x_ready[b] = normalize(xb, eps)

        def turn(b):
            tb, t2 = transpose4(X[:, 4 * b:4 * b + 4, :], x_ready[b])
            AC.wait(t2)
            t3 = cp(AC, XT[:, T * b:T * b + T], PS[:, tb, :])
            free(tb, 1, t3)
            xt_ready[b] = t3

        def l0_attn():
            top[0] = 0
            w = take(384)
            wm = take(384)
            wo = take(128)
            wom = take(128)
            bo = take(128)
            bom = take(128)
            for o, i in ((w, "qkv_w"), (wm, "qkv_m"), (wo, "ow"), (wom, "om"), (bo[0:1], "ob"), (bom[0:1], "obm")):
                l = dma("w0", o, io[i])
            DV.wait(l)
            gate = 1.5 * 2.0 ** -24
            D1(ts(DV, wm, wm, gate, ALU.is_gt))
            D1(ts(DV, wom, wom, gate, ALU.is_gt))
            D1(ts(DV, bom[0:1], bom[0:1], gate, ALU.is_gt))
            tt(DV, w, w, wm, ALU.mult)
            tt(DV, wo, wo, wom, ALU.mult)
            wr = D1(tt(DV, bo[0:1], bo[0:1], bom[0:1], ALU.mult))
            H = [take(256, F16) for _ in range(2)]
            L = [take(256, F16) for _ in range(2)]
            QS = [take(2048, F16).rearrange("p (h n) -> p h n", h=8) for _ in range(2)]
            KS = [take(2048, F16).rearrange("p (h n) -> p h n", h=8) for _ in range(2)]
            VP = [take(4 * 2048 + 128) for _ in range(2)]
            E = [take(2048).rearrange("p (c n) -> p c n", c=4) for _ in range(3)]
            rec = take(512)
            oT = [take(512) for _ in range(2)]
            mx = take(64).rearrange("p (q h) -> p q h", q=4)
            mneg = take(32, F16).rearrange("p (q h) -> p q h", q=4)
            mrow = take(256, F16)
            z = []
            for i in range(2):
                z.append(PO.op(lambda e, i=i: e.memset(VP[i], 0.0)))
                PO.op(lambda e, i=i: e.memset(KS[i][32:33], 1.0))
                PO.op(lambda e, i=i: e.memset(KS[i][96:97], 1.0))
            PO.wait(PO.last)

            def vp(i, off):
                v = VP[i]
                out = []
                for c in range(4):
                    for g in range(2):
                        s = c * 2048 + g * 1024 + off
                        out.append(v[:, s:s + 1088].rearrange("p (h x) -> p h x", x=136)[:, :, 0:8])
                return out
            for i in range(2):
                for a in vp(i, 64):
                    PO.op(lambda e, a=a: e.memset(a, 1.0))
            zero = PO.last
            scr_qk, scr_m = io["s_qk0"], io["s_m0"]
            pv_done = {}
            oT_free = {}
            E_free = {}
            prep = {}

            def part_a(b):
                i = b % 2
                cols = slice(T * b, T * b + T)
                PE.wait(wr, xt_ready[b])
                bq = banks(2)
                for k in range(2):
                    t = mm(PS[:, bq + k, :], w[:, 128 * k:128 * k + 128], XT[:, cols], inc=True)
                bv = banks()
                for c in range(4):
                    tv = mm(PS[:, bv, 128 * c:128 * c + 128], XT[:, T * b + 128 * c:T * b + 128 * c + 128],
                            w[:, 256:384], inc=(c == 3))
                prev = prep.get(b - 1, {})
                AC.wait(t, prev.get("scr"))
                for k in range(2):
                    h = cp(AC, H[k], PS[:, bq + k, :])
                DV.wait(h, t, prev.get("scr"))
                for k in range(2):
                    lo = tt(DV, L[k], PS[:, bq + k, :], H[k], ALU.subtract)
                free(bq, 2, lo, h)
                for k in range(2):
                    dma("a0w", scr_qk[k, 0], H[k], h, prev.get("rd"))
                    wrt = dma("a0w", scr_qk[k, 1], L[k], lo)
                done = pv_done.get(b - 2)
                for par in range(2):
                    p0 = 64 * par
                    src = scr_qk.rearrange("k s (h t d) n -> k s t d h n", t=2, d=8)
                    for r in range(4):
                        dma("a0r", QS[i][p0 + 8 * r:p0 + 8 * r + 8], src[0, r // 2, par], wrt, done)
                        rd = dma("a0r", KS[i][p0 + 8 * r:p0 + 8 * r + 8], src[1, r % 2, par])
                DV.wait(tv, done, zero)
                for g in range(2):
                    src = PS[:, bv, :].rearrange("p (c g h d) -> p c g h d", c=4, g=2, h=8)
                    for c in range(4):
                        vt = cp(DV, vp(i, 0)[2 * c + g], src[:, c, g])
                free(bv, 1, vt)
                PE.wait(rd)
                for h in range(16):
                    par, hp = h % 2, h // 2
                    for q2 in range(2):
                        bb = banks(2)
                        for q in range(2):
                            qt = 2 * q2 + q
                            t = mm(PS[:, bb + q, :], QS[i][64 * par:64 * par + 8, hp, 128 * qt:128 * qt + 128],
                                   KS[i][64 * par:64 * par + 8, hp, :], inc=(q == 1))
                        DV.wait(t)
                        r = red(mx[:, 2 * q2:2 * q2 + 2, 8 * par + hp], PS[:, bb:bb + 2, :], ALU.max)
                        free(bb, 2, r)
                D1(r)
                DV.wait(prev.get("mt"))
                mt = ts(DV, mneg, mx, -1.0, ALU.mult)
                bm = banks()
                PE.wait(mt)
                for qt in range(4):
                    t = mm(PS[0:16, bm, 128 * qt:128 * qt + 128], mneg[:, qt, :], ident16[:], inc=(qt == 3))
                AC.wait(t, prev.get("mscr"))
                c = cp(AC, mrow[0:16], PS[0:16, bm, :])
                free(bm, 1, c)
                mw = dma("a0m", scr_m, mrow[0:16], c, prev.get("mrd"))
                for par in range(2):
                    m = dma("a0mr", QS[i][64 * par + 32:64 * par + 33], scr_m[8 * par:8 * par + 8].unsqueeze(0), mw, done)
                prep[b] = {"scr": wrt, "rd": rd, "mt": t, "mscr": mw, "mrd": m, "vt": vt}

            def part_b(b):
                i = b % 2
                n = 0
                po = None
                PE.wait(prep[b]["mrd"], prep[b]["vt"], zero)
                for g in range(2):
                    acc = 6 + g
                    PE.wait(*(freed[acc] or []))
                    pend = []

                    def pv(h, ej, exps, first, last):
                        PE.wait(exps)
                        for c in range(4):
                            t = mm(PS[:, acc, :], VP[i][:, c * 2048 + h * 128:c * 2048 + h * 128 + 128], E[ej][:, c, :],
                                   start=(first and c == 0), stop=(last and c == 3), inc=(c == 3))
                        E_free[ej] = t
                        return t
                    for h8 in range(8):
                        h = 8 * g + h8
                        par, hp = h % 2, h // 2
                        ej = (16 * b + h) % 3
                        AC.wait(E_free.get(ej))
                        for c2 in range(2):
                            bb = banks(2)
                            for c in range(2):
                                kc = 2 * c2 + c
                                t = mm(PS[:, bb + c, :], KS[i][64 * par:64 * par + 33, hp, 128 * kc:128 * kc + 128],
                                       QS[i][64 * par:64 * par + 33, hp, :], inc=(c == 1))
                            AC.wait(t)
                            ex = act(E[ej][:, 2 * c2:2 * c2 + 2, :], PS[:, bb:bb + 2, :], ACT.Exp, scale=float(D) ** -0.5)
                            free(bb, 2, ex)
                        pend.append((h, ej, ex, h8 == 0, h8 == 7))
                        if len(pend) > 1:
                            pv(*pend.pop(0))
                    t = pv(*pend.pop(0))
                    DV.wait(t, oT_free.get(i))
                    D1(recip(rec[0:64], PS[64:128, acc, :]))
                    po = D1(tt(DV, oT[i][64 * g:64 * g + 64], PS[0:64, acc, :], rec[0:64], ALU.mult))
                    free(acc, 1, po)
                pv_done[b] = t
                bo_ = banks()
                PE.wait(po)
                for j in range(4):
                    o = PS[:, bo_, 128 * j:128 * j + 128]
                    mm(o, oT[i][:, 128 * j:128 * j + 128], wo, stop=False)
                    t = mm(o, ones[0:1, :], bo[0:1], start=False, inc=(j == 3))
                oT_free[i] = t
                residual(b, bo_, t)
            part_a(0)
            for b in range(NB):
                if b + 1 < NB:
                    part_a(b + 1)
                part_b(b)
            for b in range(NB):
                turn(b)

        def l0_xattn():
            top[0] = 0
            NK = TC + T
            sizes = [128] * 5 + [26]
            wq, wk, wv, wo = take(1024), take(1024), take(1024), take(1024).rearrange("p (a n) -> p a n", a=8)
            ln = take(4)
            sel = take(1024).rearrange("p (a n) -> p a n", a=8)
            KV = take(NB * NK).rearrange("p (b n) -> p b n", b=NB)
            CX = take(1024).rearrange("p (a n) -> p a n", a=8)
            for o, i in ((wq, "x_wq"), (wk, "x_wk"), (wv, "x_wv"), (wo, "x_wo"), (ln, "x_ln"), (CX, "ctx_tm"),
                         (sel[64:80], "sel16")):
                l = dma("w1", o, io[i])
            Hq, Lq = [take(512, F16).rearrange("p (a n) -> p a n", a=2) for _ in range(2)]
            Hk, Lk = [take(NK, F16).rearrange("p (a n) -> p a n", a=2) for _ in range(2)]

            def four(words):
                return [take(words, F16).rearrange("p (t a n) -> p t a n", t=2, a=2) for _ in range(2)]
            M1, M2, S1, S2 = four(1024), four(1024), four(2 * NK), four(2 * NK)
            VP = [take(1920).rearrange("p (c h n) -> p c h n", c=6, h=4) for _ in range(4)]
            E = [take(3072).rearrange("p (c n) -> p c n", c=6) for _ in range(2)]
            OT = [take(4096).rearrange("p (a n) -> p a n", a=8) for _ in range(1)]
            den = [take(512) for _ in range(2)]
            rden = take(512)
            LX = take(512).rearrange("p (a n) -> p a n", a=4)
            mx = take(16).rearrange("p (q h) -> p q h", q=4)
            mneg = take(8, F16).rearrange("p (q h) -> p q h", q=4)
            mrow = take(256, F16)
            for g in range(4):
                PO.op(lambda e, g=g: e.memset(VP[g][:, :, :, 64:80], 0.0))
                for j in range(4):
                    h = 4 * g + j
                    PO.op(lambda e, g=g, j=j, h=h: e.memset(VP[g][:, :, j, 64 + h:65 + h], 1.0))
            for i in range(2):
                PO.op(lambda e, i=i: e.memset(S2[i][64:65], 1.0))
            zero = PO.last
            DV.wait(l)
            PE.wait(l)
            for half in range(2):
                t = normalize(CX[:, 4 * half:4 * half + 4, :], 1e-5)
                tb, t = transpose4(CX[:, 4 * half:4 * half + 4, :], t)
                DV.wait(t)
                for j in range(2):
                    k = ts(DV, KV[:, 2 * half + j, 0:TC], PS[:, tb, 256 * j:256 * j + TC], ln[:, 0:1], ALU.mult,
                           ln[:, 1:2], ALU.add)
                free(tb, 1, k)
            kv_ready = {}
            s = {}
            E_free, vp_free, den_t = {}, {}, {}
            ot_free = [None]

            def latents(b):
                DV.wait(x_ready[b], lx_free[0])
                t = normalize_to(LX, X[:, 4 * b:4 * b + 4, :])
                tb, t = transpose4(LX, t)
                lx_free[0] = t
                DV.wait(t)
                k = ts(DV, KV[:, b, TC:], PS[:, tb, :], ln[:, 2:3], ALU.mult, ln[:, 3:4], ALU.add)
                free(tb, 1, k)
                kv_ready[b] = k

            lx_free = [None]

            def normalize_to(out, x):
                return normalize(x, 1e-5, out)

            def part_a(b, g):
                u = 4 * b + g
                i = u % 2
                prev, prev2 = s.get(u - 1, {}), s.get(u - 2, {})
                PE.wait(kv_ready[b])
                bq = banks(2)
                for a in range(2):
                    tq = mm(PS[:, bq + a, :], wq[:, 128 * (2 * g + a):128 * (2 * g + a) + 128], KV[:, b, TC:], inc=(a == 1))
                AC.wait(tq, prev.get("wr"))
                h = cp(AC, Hq, PS[:, bq:bq + 2, :])
                DV.wait(h, tq, prev.get("wr"))
                lo = tt(DV, Lq, PS[:, bq:bq + 2, :], Hq, ALU.subtract)
                free(bq, 2, h, lo)
                dma("xw", io["s_xq"][0], Hq, h, prev.get("rd"))
                dma("xw", io["s_xq"][1], Lq, lo, prev.get("rd"))
                for a in range(2):
                    bk = banks(2)
                    kp = PS[:, bk:bk + 2, :].rearrange("p a n -> p (a n)")
                    wka = wk[:, 128 * (2 * g + a):128 * (2 * g + a) + 128]
                    mm(kp[:, 0:512], wka, KV[:, b, 0:512])
                    tk = mm(kp[:, 512:NK], wka, KV[:, b, 512:NK], inc=True)
                    AC.wait(tk)
                    h = cp(AC, Hk[:, a, :], kp[:, 0:NK])
                    DV.wait(h, tk)
                    lo = tt(DV, Lk[:, a, :], kp[:, 0:NK], Hk[:, a, :], ALU.subtract)
                    free(bk, 2, h, lo)
                dma("xw", io["s_xk"][0], Hk, h, prev.get("rd"))
                wr = dma("xw", io["s_xk"][1], Lk, lo)
                done = prev2.get("sc")
                xq = io["s_xq"].rearrange("s (t p) a n -> s p t a n", t=2)
                xk = io["s_xk"].rearrange("s (t p) a n -> s p t a n", t=2)
                dma("xr", M1[i][0:64], xq[0], wr, done)
                dma("xr", S1[i][0:64], xk[0], wr, done)
                dma("xr", M1[i][64:128], xq[0], wr, done)
                dma("xr", M2[i][0:64], xq[1], wr, done)
                dma("xr", S1[i][64:128], xk[1], wr, done)
                rd = dma("xr", S2[i][0:64], xk[0], wr, done)
                for c2 in range(3):
                    bv = banks()
                    for c in range(2):
                        k = 2 * c2 + c
                        n = sizes[k]
                        tv = mm(PS[0:n, bv, 256 * c:256 * c + 256], KV[:, b, 128 * k:128 * k + n],
                                wv[:, 256 * g:256 * g + 256], inc=(c == 1))
                    AC.wait(tv, vp_free.get(g), zero)
                    ch = PS[:, bv, :].rearrange("p (c h n) -> p c h n", c=2, h=4)
                    if c2 < 2:
                        v = cp(AC, VP[g][:, 2 * c2:2 * c2 + 2, :, 0:64], ch)
                    else:
                        cp(AC, VP[g][:, 4, :, 0:64], ch[:, 0])
                        v = cp(AC, VP[g][0:26, 5, :, 0:64], ch[0:26, 1])
                    free(bv, 1, v)
                PE.wait(rd)
                for par in range(2):
                    for a in range(2):
                        for q in range(4):
                            bb = banks(2)
                            kp = PS[:, bb:bb + 2, :].rearrange("p a n -> p (a n)")
                            lq = M1[i][0:64, par, a, 128 * q:128 * q + 128]
                            mm(kp[:, 0:512], lq, S1[i][0:64, par, a, 0:512])
                            t = mm(kp[:, 512:NK], lq, S1[i][0:64, par, a, 512:NK], inc=True)
                            DV.wait(t)
                            r = red(mx[:, q, 2 * par + a:2 * par + a + 1], kp[:, 0:NK], ALU.max)
                            free(bb, 2, r)
                DV.wait(r, prev.get("mt"))
                mt = ts(DV, mneg, mx, -1.0, ALU.mult)
                bm = banks()
                PE.wait(mt)
                for q in range(4):
                    t = mm(PS[0:4, bm, 128 * q:128 * q + 128], mneg[:, q, :], ident16[:], inc=(q == 3))
                AC.wait(t, prev.get("mscr"))
                c = cp(AC, mrow[0:4], PS[0:4, bm, :])
                free(bm, 1, c)
                mw = dma("xmw", io["s_xm"], mrow[0:4], c, prev.get("mrd"))
                m = dma("xmr", M2[i][64:65].rearrange("p t a n -> p (t a) n"), io["s_xm"].unsqueeze(0), mw, done)
                s[u] = {"wr": wr, "rd": rd, "mt": t, "mscr": mw, "mrd": m, "v": v}

            def part_b(b, g):
                u = 4 * b + g
                i = u % 2
                PE.wait(s[u]["mrd"], s[u]["v"], zero)
                pend = []

                def pv(n, par, a, ej, ex):
                    acc = 6 + n % 2
                    PE.wait(ex, freed[acc])
                    for c in range(6):
                        k = sizes[c]
                        t = mm(PS[0:80, acc, :], VP[g][0:k, c, 2 * a + par, :], E[ej][0:k, c, :],
                               start=(c == 0), stop=(c == 5), inc=(c == 5))
                    E_free[ej] = t
                    AC.wait(t)
                    if n == 0 and g == 0:
                        AC.wait(ot_free[0])
                    o = cp(AC, OT[0][64 * par:64 * par + 64, 2 * g + a, :], PS[0:64, acc, :])
                    DV.wait(t, den_t.get("last"))
                    if n == 0 and g == 0:
                        d = cp(DV, den[0][64:80], PS[64:80, acc, :])
                    else:
                        d = tt(DV, den[0][64:80], PS[64:80, acc, :], den[0][64:80], ALU.add)
                    den_t["last"] = d
                    free(acc, 1, o, d)
                    return t, o
                n = 0
                for par in range(2):
                    for a in range(2):
                        ej = (4 * u + n) % 2
                        AC.wait(E_free.get(ej))
                        for c2 in range(3):
                            bb = banks(2)
                            for c in range(2):
                                k = 2 * c2 + c
                                z = sizes[k]
                                ks = slice(128 * k, 128 * k + z)
                                mm(PS[0:z, bb + c, :], S1[i][:, par, a, ks], M1[i][:, par, a, :], stop=False)
                                sc = mm(PS[0:z, bb + c, :], S2[i][0:65, par, a, ks], M2[i][0:65, par, a, :],
                                        start=False, inc=(c == 1))
                            AC.wait(sc)
                            if c2 < 2:
                                ex = act(E[ej][:, 2 * c2:2 * c2 + 2, :], PS[:, bb:bb + 2, :], ACT.Exp, scale=0.125)
                            else:
                                act(E[ej][:, 4, :], PS[:, bb, :], ACT.Exp, scale=0.125)
                                ex = act(E[ej][0:26, 5, :], PS[0:26, bb + 1, :], ACT.Exp, scale=0.125)
                            free(bb, 2, ex)
                        pend.append((n, par, a, ej, ex))
                        n += 1
                        if len(pend) > 1:
                            t, o = pv(*pend.pop(0))
                t, o = pv(*pend.pop(0))
                s[u]["sc"] = sc
                vp_free[g] = t
                return o

            def part_c(b, o):
                D1(den_t["last"])
                D1(recip(rden[64:80], den[0][64:80]))
                PE.wait(DV.last)
                DV.wait(o)
                for a in range(8):
                    bb = banks()
                    t = mm(PS[:, bb, :], sel[64:80, a, :], rden[64:80], inc=True)
                    DV.wait(t)
                    n = tt(DV, OT[0][:, a, :], OT[0][:, a, :], PS[:, bb, :], ALU.mult)
                    free(bb, 1, n)
                PE.wait(n)
                bo = banks()
                for j in range(4):
                    for a in range(8):
                        t = mm(PS[:, bo, 128 * j:128 * j + 128], OT[0][:, a, 128 * j:128 * j + 128], wo[:, a, :],
                               start=(a == 0), stop=(a == 7), inc=(j == 3 and a == 7))
                ot_free[0] = t
                residual(b, bo, t)

            for b in range(NB):
                latents(b)
            part_a(0, 0)
            for b in range(NB):
                for g in range(4):
                    u = 4 * b + g + 1
                    if u < 16:
                        part_a(u // 4, u % 4)
                    o = part_b(b, g)
                part_c(b, o)
            for b in range(NB):
                turn(b)

        def pick(b, lg, n, bits, idx, idxf):
            for j in range(4):
                t = DV.op(lambda e, j=j: e.max(bits[:, j, :], lg[:, j, :]))
            D1(t)
            for j in range(4):
                t = DV.op(lambda e, j=j: e.max_index(idx[:, j, :], bits[:, j, :], lg[:, j, :]))
            D1(t)
            return D1(cp(DV, idxf, idx[:, :, 0:2]))

        def l0_ffn():
            top[0] = 0
            up, gt = take(1024), take(1024)
            dn = take(1024 + 128).rearrange("p (a n) -> p a n", a=9)
            sg, su = take(128), take(128)
            rw, rb, iota = take(16), take(16), take(16)
            sel = take(1024).rearrange("p (a n) -> p a n", a=8)
            for o, i in ((up, "m_up"), (gt, "m_gate"), (dn, "m_down"), (sg, "m_sg"), (su, "m_su"), (rw, "m_rw"),
                         (rb[0:1], "m_rb"), (iota, "iota16"), (sel[0:16], "sel16")):
                l = dma("w2", o, io[i])
            v4 = lambda n, m: take(4 * n * m).rearrange("p (k a n) -> p k a n", k=n, a=4)
            lg = v4(1, 16)[:, 0]
            m8, i8 = v4(1, 8)[:, 0], v4(1, 8)[:, 0].bitcast(U32)
            ixf = v4(1, 2)[:, 0]
            oh = v4(3, 16)
            wt = take(16).rearrange("p (k a) -> p k a", k=4)
            CT = [take(512) for _ in range(2)]
            SG = [take(512) for _ in range(3)]
            Hh = [take(4608).rearrange("p (a n) -> p a n", a=9) for _ in range(2)]
            PE.wait(l)
            DV.wait(l)
            ct_ready, h_free, sg_free = {}, {}, {}
            iob = iota.unsqueeze(1).broadcast_to([128, 4, 16])

            def route(b):
                bb = banks()
                PE.wait(xt_ready[b])
                for j in range(4):
                    o = PS[:, bb, 16 * j:16 * j + 16]
                    mm(o, XT[:, T * b + 128 * j:T * b + 128 * j + 128], rw, stop=False)
                    t = mm(o, ones[0:1, :], rb[0:1], start=False, inc=(j == 3))
                DV.wait(t)
                t = D1(cp(DV, lg, PS[:, bb, 0:64].rearrange("p (a n) -> p a n", a=4)))
                free(bb, 1, t)
                pick(b, lg, 16, m8, i8, ixf)
                t = D1(tt(DV, wt[:, 0, :], m8[:, :, 1], m8[:, :, 0], ALU.subtract))
                AC.wait(t)
                t = act(wt[:, 1, :], wt[:, 0, :], ACT.Exp)
                DV.wait(t)
                D1(ts(DV, wt[:, 0, :], wt[:, 1, :], 1.0, ALU.add))
                D1(recip(wt[:, 2, :], wt[:, 0, :]))
                D1(tt(DV, wt[:, 3, :], wt[:, 1, :], wt[:, 2, :], ALU.mult))
                tt(DV, oh[:, 0], iob, bc(ixf[:, :, 0], 16), ALU.is_equal)
                D1(tt(DV, oh[:, 1], iob, bc(ixf[:, :, 1], 16), ALU.is_equal))
                tt(DV, oh[:, 0], oh[:, 0], bc(wt[:, 2, :], 16), ALU.mult)
                D1(tt(DV, oh[:, 1], oh[:, 1], bc(wt[:, 3, :], 16), ALU.mult))
                t = D1(tt(DV, oh[:, 2], oh[:, 0], oh[:, 1], ALU.add))
                bb = banks()
                PE.wait(t)
                for j in range(4):
                    t = tr(PS[0:16, bb, 128 * j:128 * j + 128], oh[:, 2, j, :], j == 3)
                D1(t)
                t = cp(DV, CT[b % 2][0:16], PS[0:16, bb, :])
                free(bb, 1, t)
                ct_ready[b] = t

            def experts(b):
                cols = slice(T * b, T * b + T)
                H = Hh[b % 2]
                PE.wait(xt_ready[b])
                for p in range(9):
                    i = (9 * b + p) % 3
                    bu = banks(2)
                    c = slice(128 * p, 128 * p + 128)
                    tg = mm(PS[:, bu, :], gt[:, c] if p < 8 else sg, XT[:, cols], inc=True)
                    t = mm(PS[:, bu + 1, :], up[:, c] if p < 8 else su, XT[:, cols], inc=True)
                    AC.wait(tg, sg_free.get(i))
                    a = act(SG[i], PS[:, bu, :], ACT.Silu)
                    DV.wait(a, t, h_free.get(b % 2))
                    if p == 8:
                        t = tt(DV, H[:, p, :], SG[i], PS[:, bu + 1, :], ALU.mult)
                        free(bu, 2, t)
                    else:
                        bw = 6 + p % 2
                        PE.wait(ct_ready[b], freed[bw])
                        w = mm(PS[:, bw, :], sel[0:16, p, :], CT[b % 2][0:16], inc=True)
                        t = D1(tt(DV, SG[i], SG[i], PS[:, bu + 1, :], ALU.mult))
                        free(bu, 2, t)
                        DV.wait(w)
                        t = tt(DV, H[:, p, :], SG[i], PS[:, bw, :], ALU.mult)
                        free(bw, 1, t)
                    sg_free[i] = t
                return t

            def down(b, ready):
                H = Hh[b % 2]
                bo = banks()
                PE.wait(ready)
                for j in range(4):
                    for p in range(9):
                        t = mm(PS[:, bo, 128 * j:128 * j + 128], H[:, p, 128 * j:128 * j + 128], dn[:, p, :],
                               start=(p == 0), stop=(p == 8), inc=(j == 3 and p == 8))
                h_free[b % 2] = t
                residual(b, bo, t)
            route(0)
            for b in range(NB):
                if b + 1 < NB:
                    route(b + 1)
                h = experts(b)
                down(b, h)
                if b:
                    turn(b - 1)
            turn(NB - 1)

        def l1_attn():
            top[0] = 0
            wq, wk, wv, wo = take(1024), take(1024), take(1024), take(1024).rearrange("p (a n) -> p a n", a=8)
            wb, bb_ = take(16), take(16)
            maskL, maskU = take(128), take(128)
            eye = take(1024)
            for o, i in ((wq, "d_wq"), (wk, "d_wk"), (wv, "d_wv"), (wo, "d_wo"), (wb, "d_wb"), (bb_[0:1], "d_bb"),
                         (maskL, "mask_l"), (maskU, "mask_u"), (eye, "eye32")):
                l = dma("w3", o, io[i])
            Kn = [take(4096).rearrange("p (c n) -> p c n", c=4) for _ in range(2)]
            KT = [take(4096).rearrange("p (a n) -> p a n", a=8) for _ in range(2)]
            beta = [take(64).rearrange("p (h c) -> p h c", h=16) for _ in range(2)]
            GA = take(2048)
            XI = take(2048)
            tmp = take(512)
            sqk = take(512)
            ss = take(64 * 4).rearrange("p (k c h) -> p k c h", k=4, c=4)
            QT = take(2048).rearrange("p (a n) -> p a n", a=4)
            V = take(2048).rearrange("p (c n) -> p c n", c=4)
            LN_ = take(4096).rearrange("p (h c n) -> p h c n", h=8, c=4)
            P = take(4096).rearrange("p (h c n) -> p h c n", h=8, c=4)
            XE = take(4096).rearrange("p (h c n) -> p h c n", h=8, c=4)
            OT = take(2048).rearrange("p (a n) -> p a n", a=4)
            S = take(512).rearrange("p (a n) -> p a n", a=4)
            RR = [[take(256) for _ in range(3)] for _ in range(2)]
            for e in compute:
                e.wait(l)
            PO.op(lambda e: e.memset(XE, 0.0))
            zero = PO.op(lambda e: e.memset(S, 0.0))
            s1, s2 = {}, {}

            def stage1(b):
                i = b % 2
                prev = s1.get(b - 1, {})
                done = s2.get(b - 2)
                PE.wait(xt_ready[b])
                bbk = banks()
                for c in range(4):
                    o = PS[:, bbk, 16 * c:16 * c + 16]
                    mm(o, XT[:, T * b + 128 * c:T * b + 128 * c + 128], wb, stop=False)
                    t = mm(o, ones[0:1, :], bb_[0:1], start=False, inc=(c == 3))
                AC.wait(t, done)
                t = act(beta[i].rearrange("p h c -> p c h"), PS[:, bbk, 0:64].rearrange("p (c h) -> p c h", c=4), ACT.Sigmoid)
                free(bbk, 1, t)
                bt = t
                AC.wait(done)
                for c in range(4):
                    bk = banks(2)
                    for j in range(2):
                        t = mm(PS[:, bk + j, :], XT[:, T * b + 128 * c:T * b + 128 * c + 128],
                               wk[:, 512 * j:512 * j + 512], inc=True)
                        AC.wait(t)
                        k = cp(AC, Kn[i][:, c, 512 * j:512 * j + 512], PS[:, bk + j, :])
                        AC.wait(DV.last)
                        t = act(sqk, PS[:, bk + j, :], ACT.Square)
                        free(bk + j, 1, t, k)
                        DV.wait(t)
                        r = red(ss[:, 0, c, 8 * j:8 * j + 8], sqk.rearrange("p (h n) -> p h n", h=8), ALU.add)
                D1(r)
                fl = [ss[:, k].rearrange("p c h -> p (c h)") for k in range(4)]
                D1(ts(DV, fl[0], fl[0], 1e-24, ALU.max))
                rsqrt(fl[0], fl[1], fl[2], fl[3])
                for c in range(4):
                    kc = Kn[i][:, c, :].rearrange("p (h n) -> p h n", h=16)
                    t = tt(DV, kc, kc, bc(ss[:, 1, c], 64), ALU.mult)
                PE.wait(t)
                for p in range(8):
                    bk = banks()
                    for c in range(4):
                        t = tr(PS[:, bk, 128 * c:128 * c + 128], Kn[i][:, c, 128 * p:128 * p + 128], c == 3)
                    AC.wait(t)
                    k = cp(AC, KT[i][:, p, :], PS[:, bk, :])
                    free(bk, 1, k)
                PE.wait(k)
                DV.wait(bt, prev.get("ga_free"))
                G = GA.rearrange("p (u n) -> p u n", u=64)
                for p in range(8):
                    bk = banks(2)
                    for par in range(2):
                        for c in range(4):
                            kk = KT[i][64 * par:64 * par + 64, p, 128 * c:128 * c + 128]
                            t = mm(PS[:, bk + par, 128 * c:128 * c + 128], kk, kk, inc=(par == 1 and c == 3))
                    DV.wait(t)
                    for q in range(4):
                        r = slice(32 * q, 32 * q + 32)
                        src = PS[r, bk:bk + 2, :].rearrange("p h (c n) -> p (h c) n", c=4)[:, :, 32 * q:32 * q + 32]
                        g = tt(DV, G[r, 8 * p:8 * p + 8, :], src,
                               bc(beta[i][r, 2 * p:2 * p + 2, :].rearrange("p h c -> p (h c)"), 32), ALU.mult)
                    free(bk, 2, g)
                w = dma("gw", io["s_g"], GA, g, prev.get("grd"))
                sg = io["s_g"].rearrange("(q t) (l u s) -> q l u t s", q=4, l=2, u=32)
                L4 = GA.rearrange("p (l t s) -> p l t s", l=2, t=32)
                for q in range(4):
                    for sl in range(2):
                        rd = dma("gr", L4[32 * q:32 * q + 32, sl], sg[q, sl], w)
                XL = XI.rearrange("p (l s t) -> p l s t", l=2, s=32)
                PO.wait(rd, prev.get("xw"))
                for sl in range(2):
                    PO.op(lambda e, sl=sl: e.tensor_scalar(XI[:, 1024 * sl:1024 * sl + 1024], eye, 1.0, None, ALU.mult))
                for t in range(31, 0, -1):
                    n = 32 - t
                    tm = tmp[:, 0:2 * t * n].rearrange("p (l s t) -> p l s t", l=2, s=t)
                    a = L4[:, :, t, 0:t].unsqueeze(3).broadcast_to([128, 2, t, n])
                    x = XL[:, :, t, t:32].unsqueeze(2).broadcast_to([128, 2, t, n])
                    tt(PO, tm, a, x, ALU.mult)
                    z = tt(PO, XL[:, :, 0:t, t:32], XL[:, :, 0:t, t:32], tm, ALU.subtract)
                xw = dma("xw1", io["s_x"][i], XI, z, s1.get(b - 2, {}).get("xrd"))
                s1[b] = {"ga_free": z, "grd": rd, "xw": xw, "bt": bt, "k": k}

            def stage2(b, half):
                i = b % 2
                cols = slice(T * b, T * b + T)
                free2 = s2.get("last")
                sx = io["s_x"][i].rearrange("(q u) (l s t) -> q l s u t", q=4, l=2, s=32)
                XEu = XE.rearrange("p h c n -> p (h c) n")
                for q in range(4):
                    r = slice(32 * q, 32 * q + 32)
                    xr = dma("xer", XEu[r, :, 32 * q:32 * q + 32], sx[q, half], s1[b]["xw"], free2, zero)
                s1[b]["xrd"] = xr
                for a in range(4):
                    bk = banks()
                    t = mm(PS[:, bk, :], wq[:, 512 * half + 128 * a:512 * half + 128 * a + 128], XT[:, cols], inc=True)
                    AC.wait(t, free2)
                    t = cp(AC, QT[:, a, :], PS[:, bk, :])
                    free(bk, 1, t)
                for c in range(4):
                    bk = banks()
                    t = mm(PS[:, bk, :], XT[:, T * b + 128 * c:T * b + 128 * c + 128], wv[:, 512 * half:512 * half + 512], inc=True)
                    AC.wait(t)
                    t = cp(AC, V[:, c, :], PS[:, bk, :])
                    free(bk, 1, t)
                PE.wait(t)
                DV.wait(t, free2)
                mu = maskU.unsqueeze(1).broadcast_to([128, 4, 128])
                for h in range(8):
                    par, a = h % 2, h // 2
                    r = slice(64 * par, 64 * par + 64)
                    bk = banks(2)
                    for c in range(4):
                        kk = KT[i][r, 4 * half + a, 128 * c:128 * c + 128]
                        mm(PS[:, bk, 128 * c:128 * c + 128], kk, kk)
                        t = mm(PS[:, bk + 1, 128 * c:128 * c + 128], kk, QT[r, a, 128 * c:128 * c + 128], inc=(c == 3))
                    DV.wait(t)
                    for c in range(4):
                        ll = stt(LN_[:, h, c, :], PS[:, bk, 128 * c:128 * c + 128], beta[i][:, 8 * half + h, c:c + 1],
                                 maskL, ALU.mult, ALU.mult)
                    pp = tt(DV, P[:, h], PS[:, bk + 1, :].rearrange("p (c n) -> p c n", c=4), mu, ALU.mult)
                    free(bk, 2, pp)
                    PE.wait(ll, xr)
                    bk = banks()
                    for c in range(4):
                        t = mm(PS[:, bk, 128 * c:128 * c + 128], LN_[:, h, c, :], XE[:, h, c, :], inc=(c == 3))
                    AC.wait(t)
                    n = cp(AC, LN_[:, h], PS[:, bk, :].rearrange("p (c n) -> p c n", c=4))
                    free(bk, 1, n)
                PE.wait(n, pp)

                def chain(g):
                    R, A, B = RR[g]
                    h0 = 4 * g
                    v3 = lambda x: x.rearrange("p (h n) -> p h n", h=4)
                    st_ready = None
                    ot = None
                    for c in range(4):
                        bcol = bc(beta[i][:, 8 * half + h0:8 * half + h0 + 4, c], 64)
                        if c:
                            bk = banks()
                            PE.wait(st_ready)
                            for a in range(2):
                                t = mm(PS[:, bk, 128 * a:128 * a + 128], KT[i][:, 4 * half + 2 * g + a, 128 * c:128 * c + 128],
                                       S[:, 2 * g + a, :], inc=(a == 1))
                            DV.wait(t)
                            t = D1(tt(DV, R, V[:, c, 256 * g:256 * g + 256], PS[:, bk, 0:256], ALU.subtract))
                            free(bk, 1, t)
                            t = tt(DV, v3(R), v3(R), bcol, ALU.mult)
                        else:
                            t = tt(DV, v3(R), v3(V[:, c, 256 * g:256 * g + 256]), bcol, ALU.mult)
                        yield
                        bk = banks()
                        PE.wait(t)
                        for h in range(4):
                            t = mm(PS[:, bk, 64 * h:64 * h + 64], XE[:, h0 + h, c, :], R[:, 64 * h:64 * h + 64], inc=(h == 3))
                        DV.wait(t)
                        t = cp(DV, A, PS[:, bk, 0:256])
                        free(bk, 1, t)
                        src = A
                        for k in range(3):
                            yield
                            bk = banks()
                            PE.wait(t)
                            for h in range(4):
                                t = mm(PS[:, bk, 64 * h:64 * h + 64], LN_[:, h0 + h, c, :], src[:, 64 * h:64 * h + 64],
                                       inc=(h == 3))
                            D1(t)
                            t = tt(DV, B, A, PS[:, bk, 0:256], ALU.subtract)
                            free(bk, 1, t)
                            src = B
                        yield
                        PE.wait(t)
                        if c < 3:
                            bk = banks()
                            for h in range(4):
                                par, a = h % 2, h // 2
                                r = slice(64 * par, 64 * par + 64)
                                t = mm(PS[r, bk, 64 * a:64 * a + 64],
                                       Kn[i][:, c, 512 * half + 64 * (h0 + h):512 * half + 64 * (h0 + h) + 64],
                                       B[:, 64 * h:64 * h + 64], inc=(h == 3))
                        bo = banks()
                        for a in range(2):
                            oo = PS[:, bo, 128 * a:128 * a + 128]
                            if c:
                                mm(oo, S[:, 2 * g + a, :], QT[:, 2 * g + a, 128 * c:128 * c + 128], stop=False)
                            for par in range(2):
                                h = 2 * a + par
                                to = mm(PS[64 * par:64 * par + 64, bo, 128 * a:128 * a + 128], B[:, 64 * h:64 * h + 64],
                                        P[:, h0 + h, c, :], start=(c == 0), inc=(h == 3))
                        if c < 3:
                            DV.wait(to)
                            for par in range(2):
                                r = slice(64 * par, 64 * par + 64)
                                so = S[r, 2 * g:2 * g + 2, 64 * par:64 * par + 64]
                                ps = PS[r, bk, 0:128].rearrange("p (a n) -> p a n", a=2)
                                t = cp(DV, so, ps) if c == 0 else tt(DV, so, so, ps, ALU.add)
                            free(bk, 1, t)
                            st_ready = t
                        AC.wait(to, free2)
                        ot = cp(AC, OT[:, 2 * g:2 * g + 2, 128 * c:128 * c + 128],
                                PS[:, bo, 0:256].rearrange("p (a n) -> p a n", a=2))
                        free(bo, 1, ot)
                        yield
                        D1(t)
                PE.wait(zero)
                runs = [chain(0), chain(1)]
                while runs:
                    for r in list(runs):
                        if next(r, StopIteration) is StopIteration:
                            runs.remove(r)
                PE.wait(AC.last)
                bo = banks()
                for j in range(4):
                    for a in range(4):
                        t = mm(PS[:, bo, 128 * j:128 * j + 128], OT[:, a, 128 * j:128 * j + 128], wo[:, 4 * half + a, :],
                               start=(a == 0), stop=(a == 3), inc=(j == 3 and a == 3))
                s2["last"] = [t, DV.last]
                if half == 0:
                    xb = X[:, 4 * b:4 * b + 4, :]
                    DV.wait(t, x_ready[b], xt_ready[b])
                    t = tt(DV, xb, xb, PS[:, bo, :].rearrange("p (a b) -> p a b", a=4), ALU.add)
                    free(bo, 1, t)
                    x_ready[b] = t
                else:
                    s2[b] = [t, DV.last]
                    residual(b, bo, t)
            stage1(0)
            for b in range(NB):
                if b + 1 < NB:
                    stage1(b + 1)
                stage2(b, 0)
                stage2(b, 1)
                if b:
                    turn(b - 1)
            turn(NB - 1)

        def l1_xattn():
            top[0] = 0
            wx, wy, wv, cT = take(128), take(128), take(128), take(NB * TC)
            bxy, bv = take(2), take(128)
            mc, mr = take(8), take(NB * TC)
            for o, i in ((wx, "y_wx"), (wy, "y_wy"), (wv, "y_wv"), (cT, "ctx_T"), (bxy, "y_bxy"), (bv[0:1], "y_bv"),
                         (mc.bitcast(I32), "mask_c"), (mr[0:1].bitcast(I32), "mask_r")):
                l = dma("w4", o, io[i])
            mcf, mrf = take(8).rearrange("p (b c) -> p b c", b=4), take(NB * TC)
            Kp = take(NB * TC)
            Vp = take(NB * 2 * 129).rearrange("p (b c n) -> p b c n", b=4, c=2)
            Qp = [take(512) for _ in range(2)]
            E = [take(1024).rearrange("p (c n) -> p c n", c=2) for _ in range(2)]
            mx = [take(8).rearrange("p (k q) -> p k q", k=2) for _ in range(2)]
            mrow = [take(512) for _ in range(2)]
            rd = take(4)
            sizes = [128, 26]
            scale = float(D) ** -0.5
            DV.wait(l)
            PE.wait(l)
            ts(DV, mcf.rearrange("p b c -> p (b c)"), mc.bitcast(I32), 1.0, ALU.is_equal, -1e30, ALU.mult)
            t = ts(DV, mrf[0:1], mr[0:1].bitcast(I32), 1.0, ALU.is_equal, -1e30, ALU.mult)
            vm = DV.op(lambda e: e.memset(Vp[:, :, :, 128:129], 1.0))
            for k in range(2):
                bk = banks()
                c = slice(308 * k, 308 * k + 308)
                t = mm(PS[:, bk, 0:308], wy, cT[:, c], inc=True)
                DV.wait(t)
                t = ts(DV, Kp[:, c], PS[:, bk, 0:308], bxy[:, 1:2], ALU.add)
                free(bk, 1, t)
            for b in range(NB):
                bk = banks()
                for c in range(2):
                    n = sizes[c]
                    o = PS[0:n, bk, 128 * c:128 * c + 128]
                    mm(o, cT[:, TC * b + 128 * c:TC * b + 128 * c + n], wv, stop=False)
                    t = mm(o, ones[0:1, 0:n], bv[0:1], start=False, inc=True)
                DV.wait(t)
                for c in range(2):
                    n = sizes[c]
                    t = cp(DV, Vp[0:n, b, c, 0:128], PS[0:n, bk, 128 * c:128 * c + 128])
                free(bk, 1, t)
            PE.wait(t, DV.last)
            AC.wait(t)
            r = {}

            def part_a(b):
                i = b % 2
                bk = banks()
                PE.wait(xt_ready[b])
                t = mm(PS[:, bk, :], wx, XT[:, T * b:T * b + T], inc=True)
                DV.wait(t, r.get(b - 2))
                q = ts(DV, Qp[i], PS[:, bk, :], bxy[:, 0:1], ALU.add)
                free(bk, 1, q)
                bk = banks(2)
                PE.wait(q)
                kb = slice(TC * b, TC * b + TC)
                for j in range(4):
                    o = PS[:, bk + j // 2, TC * (j % 2):TC * (j % 2) + TC]
                    mm(o, Qp[i][:, 128 * j:128 * j + 128], Kp[:, kb], stop=False)
                    t = mm(o, ones[0:1, :], mrf[0:1, kb], start=False, inc=(j == 3))
                DV.wait(t)
                t = D1(red(mx[i][:, 0, :].rearrange("p (a q) -> p a q", a=2),
                           PS[:, bk:bk + 2, 0:2 * TC].rearrange("p a (q n) -> p a q n", q=2), ALU.max))
                free(bk, 2, t)
                t = ts(DV, mx[i][:, 1, :], mx[i][:, 0, :], -1.0, ALU.mult)
                bk = banks()
                PE.wait(t)
                for j in range(4):
                    t = mm(PS[0:1, bk, 128 * j:128 * j + 128], mx[i][:, 1, j:j + 1], ident[:], inc=(j == 3))
                D1(t)
                t = cp(DV, mrow[i][0:1], PS[0:1, bk, :])
                free(bk, 1, t)
                return t

            def part_b(b, ready):
                i = b % 2
                bk = banks(2)
                PE.wait(ready)
                for c in range(2):
                    n = sizes[c]
                    mm(PS[0:n, bk + c, :], Kp[:, TC * b + 128 * c:TC * b + 128 * c + n], Qp[i], stop=False)
                    t = mm(PS[0:n, bk + c, :], ones[0:1, 0:n], mrow[i][0:1], start=False, inc=True)
                AC.wait(t, r.get(b - 2))
                for c in range(2):
                    n = sizes[c]
                    t = act(E[i][0:n, c, :], PS[0:n, bk + c, :], ACT.Exp, scale=scale, bias=mcf[0:n, b, c:c + 1])
                free(bk, 2, t)
                bk = banks(2)
                PE.wait(t)
                for j in range(4):
                    for c in range(2):
                        n = sizes[c]
                        t = mm(PS[:, bk + j // 2, 129 * (j % 2):129 * (j % 2) + 129], E[i][0:n, c, 128 * j:128 * j + 128],
                               Vp[0:n, b, c, :], start=(c == 0), stop=(c == 1), inc=(j == 3 and c == 1))
                r[b] = t
                DV.wait(t, x_ready[b], xt_ready[b])
                den = PS[:, bk:bk + 2, 0:258].rearrange("p a (q n) -> p a q n", q=2)[:, :, :, 128]
                D1(recip(rd.rearrange("p (a q) -> p a q", a=2), den))
                for j in range(4):
                    t = stt(X[:, 4 * b + j, :], PS[:, bk + j // 2, 129 * (j % 2):129 * (j % 2) + 128], rd[:, j:j + 1],
                            X[:, 4 * b + j, :], ALU.mult, ALU.add)
                free(bk, 2, t)
                D1(t)
                x_ready[b] = normalize(X[:, 4 * b:4 * b + 4, :], 1e-5)
            t = part_a(0)
            for b in range(NB):
                nt = part_a(b + 1) if b + 1 < NB else None
                part_b(b, t)
                t = nt
                if b:
                    turn(b - 1)
            turn(NB - 1)

        def l1_ffn():
            top[0] = 0
            w1 = take(4096).rearrange("p (e n) -> p e n", e=8)
            b1, wo, rw = take(512), take(512).rearrange("p (a n) -> p a n", a=4), take(8)
            bo, gb, iota = take(128), take(256), take(16)
            sel = take(1024)
            for o, i in ((w1, "f_w1"), (b1[0:8], "f_b1"), (wo, "f_wo"), (rw, "f_rw"), (bo[0:1], "f_bo"),
                         (gb[0:1], "f_gb"), (iota, "iota16"), (sel[0:8], "sel8")):
                l = dma("w5", o, io[i])
            sel16 = take(512, F16).rearrange("p (e n) -> p e n", e=8)
            gam = take(256)
            lg = take(32).rearrange("p (a n) -> p a n", a=4)
            m8, i8 = take(32).rearrange("p (a n) -> p a n", a=4), take(32).rearrange("p (a n) -> p a n", a=4).bitcast(U32)
            ixf = take(8).rearrange("p (a n) -> p a n", a=4)
            oh = take(32).rearrange("p (a n) -> p a n", a=4)
            MT = [take(512) for _ in range(2)]
            M16 = [take(256, F16) for _ in range(2)]
            XM = [take(4096).rearrange("p (e n) -> p e n", e=8) for _ in range(2)]
            HT = [take(2048).rearrange("p (a n) -> p a n", a=4) for _ in range(2)]
            DV.wait(l)
            PE.wait(l)
            cp(DV, sel16[0:8], sel[0:8].rearrange("p (e n) -> p e n", e=8))
            bk = banks()
            t = mm(PS[:, bk, 0:256], ones[0:1, :], gb[0:1], inc=True)
            DV.wait(t)
            t = cp(DV, gam, PS[:, bk, 0:256])
            free(bk, 1, t)
            D1(t)
            g3 = gam[:, 0:128].unsqueeze(1).broadcast_to([128, 4, 128])
            b3 = gam[:, 128:256].unsqueeze(1).broadcast_to([128, 4, 128])
            iob = iota[:, 0:8].unsqueeze(1).broadcast_to([128, 4, 8])
            xm_free, ht_free = {}, {}

            def route(b):
                i = b % 2
                bk = banks()
                PE.wait(xt_ready[b])
                for j in range(4):
                    t = mm(PS[:, bk, 8 * j:8 * j + 8], XT[:, T * b + 128 * j:T * b + 128 * j + 128], rw, inc=(j == 3))
                D1(t)
                t = D1(cp(DV, lg, PS[:, bk, 0:32].rearrange("p (a n) -> p a n", a=4)))
                free(bk, 1, t)
                pick(b, lg, 8, m8, i8, ixf)
                t = D1(tt(DV, oh, iob, bc(ixf[:, :, 0], 8), ALU.is_equal))
                bk = banks()
                PE.wait(t)
                for j in range(4):
                    t = tr(PS[0:8, bk, 128 * j:128 * j + 128], oh[:, j, :], j == 3)
                DV.wait(t, xm_free.get(i))
                cp(DV, MT[i][0:8], PS[0:8, bk, :])
                m = cp(DV, M16[i][0:8], PS[0:8, bk, :])
                free(bk, 1, m)
                PE.wait(m)
                for e in range(8):
                    bk = banks()
                    t = mm(PS[:, bk, :], sel16[0:8, e, :], M16[i][0:8], inc=True)
                    DV.wait(t)
                    t = tt(DV, XM[i][:, e, :], XT[:, T * b:T * b + T], PS[:, bk, :], ALU.mult)
                    free(bk, 1, t)
                return t

            def hidden(b, ready):
                i = b % 2
                PE.wait(ready)
                for a in range(4):
                    bk = banks()
                    c = slice(128 * a, 128 * a + 128)
                    for e in range(8):
                        mm(PS[:, bk, :], w1[:, e, c], XM[i][:, e, :], start=(e == 0), stop=False)
                    t = mm(PS[:, bk, :], b1[0:8, c], MT[i][0:8], start=False, inc=True)
                    AC.wait(t, ht_free.get(i))
                    h = act(HT[i][:, a, :], PS[:, bk, :], ACT.Gelu)
                    free(bk, 1, h)
                xm_free[i] = t
                return h

            def out(b, ready):
                i = b % 2
                bk = banks()
                PE.wait(ready)
                for j in range(4):
                    o = PS[:, bk, 128 * j:128 * j + 128]
                    for a in range(4):
                        mm(o, HT[i][:, a, 128 * j:128 * j + 128], wo[:, a, :], start=(a == 0), stop=False)
                    t = mm(o, ones[0:1, :], bo[0:1], start=False, inc=(j == 3))
                ht_free[i] = t
                xb = X[:, 4 * b:4 * b + 4, :]
                Y = XM[i].rearrange("p e n -> p (e n)")[:, 0:512].rearrange("p (a n) -> p a n", a=4)
                DV.wait(t, x_ready[b])
                t = D1(tt(DV, Y, xb, PS[:, bk, :].rearrange("p (a b) -> p a b", a=4), ALU.add))
                free(bk, 1, t)
                normalize(Y, 1e-12)
                D1(tt(DV, Y, Y, g3, ALU.mult))
                D1(tt(DV, Y, Y, b3, ALU.add))
                D1(tt(DV, xb, xb, Y, ALU.add))
                t = normalize(xb, 1e-5)
                xm_free[i] = t
                x_ready[b] = t
            t = route(0)
            for b in range(NB):
                nt = route(b + 1) if b + 1 < NB else None
                h = hidden(b, t)
                out(b, h)
                t = nt

        for f in (l0_attn, l0_xattn, l0_ffn, l1_attn, l1_xattn, l1_ffn)[:phases]:
            f()
            barrier()

        o = dma("out", io["out"], X[:])
        SP.wait(o)

        block = ctx.enter_context(nc.Block())

        @block.tensor
        def _(e):
            for f in PE.q:
                f(e)

        @block.vector
        def _(e):
            for f in DV.q:
                f(e)

        @block.scalar
        def _(e):
            for f in AC.q:
                f(e)

        @block.gpsimd
        def _(e):
            for f in PO.q:
                f(e)

        @block.sync
        def _(e):
            for f in SP.q:
                f(e)


OUTS = ["out"]
SCRATCH = {"s_g": ([128, 2048], F32), "s_x": ([2, 128, 2048], F32), "s_xq": ([2, 128, 2, 512], F16), "s_xk": ([2, 128, 2, 666], F16), "s_xm": ([4, 512], F16),
           "s_qk0": ([2, 2, 128, 512], F16), "s_m0": ([16, 512], F16)}

PHASES = 6


def kernel(**inputs):
    import concourse.bacc as bacc
    from concourse.bass_utils import run_bass_kernel_spmd

    a = {k: np.asarray(v) for k, v in inputs.items()}
    x = a["x"].reshape(NB * T, D)
    arrays = {
        "x_tm": x.reshape(NT, 128, D).transpose(1, 0, 2),
        "x_T": x.T,
        "ident": np.eye(128, dtype=np.float32),
        "qkv_w": a["L0_attn_qkv_weight"].T,
        "qkv_m": a["L0_attn_qkv_weight_mask"].T,
        "ow": a["L0_attn_out_weight"].T,
        "om": a["L0_attn_out_weight_mask"].T,
        "ob": a["L0_attn_out_bias"][None],
        "obm": a["L0_attn_out_bias_mask"][None],
    }
    ctx_pad = np.zeros((NB, 256, D), np.float32)
    ctx_pad[:, :TC] = a["ctx_1024"]
    sel = np.zeros((16, 8, 2, 64), np.float32)
    for h in range(16):
        sel[h, h // 2, h % 2] = 1.0
    arrays |= {
        "ctx_tm": ctx_pad.reshape(8, 128, D).transpose(1, 0, 2),
        "x_wq": a["L0_xattn_Wq"],
        "x_wk": a["L0_xattn_Wkv"][:, :1024],
        "x_wv": a["L0_xattn_Wkv"][:, 1024:],
        "x_wo": a["L0_xattn_Wo"].reshape(8, 128, D).transpose(1, 0, 2),
        "x_ln": np.stack([a["L0_xattn_ln1_g"], a["L0_xattn_ln1_b"], a["L0_xattn_ln2_g"], a["L0_xattn_ln2_b"]], 1),
        "sel16": sel.reshape(16, 8, 128),
    }
    def experts(w):
        return w.transpose(1, 0, 2).reshape(D, -1)
    down = np.concatenate([a["L0_ffn_down_proj"].reshape(8, 128, D), a["L0_ffn_sh_down"].T[None]])
    mask = np.zeros((NB, 256), np.int32)
    mask[:, :TC] = a["mask_BxS2_ik1"]
    ii = np.arange(128)
    arrays |= {
        "m_up": experts(a["L0_ffn_up_proj"]),
        "m_gate": experts(a["L0_ffn_gate_proj"]),
        "m_down": down.transpose(1, 0, 2),
        "m_sg": a["L0_ffn_sh_gate"].T,
        "m_su": a["L0_ffn_sh_up"].T,
        "m_rw": a["L0_ffn_router_w"].T,
        "m_rb": a["L0_ffn_router_bias"][None],
        "iota16": np.tile(np.arange(16, dtype=np.float32), (128, 1)),
        "d_wq": a["L1_attn_Wq"],
        "d_wk": a["L1_attn_Wk"],
        "d_wv": a["L1_attn_Wv"],
        "d_wo": a["L1_attn_Wout"].reshape(8, 128, D).transpose(1, 0, 2),
        "d_wb": a["L1_attn_Wbeta"],
        "d_bb": a["L1_attn_b_beta"][None],
        "mask_l": (ii[None, :] // 32 < ii[:, None] // 32).astype(np.float32),
        "mask_u": (ii[:, None] <= ii[None, :]).astype(np.float32),
        "eye32": np.tile(np.eye(32, dtype=np.float32).reshape(1, 1024), (128, 1)),
        "y_wx": a["L1_xattn_Wx"].T,
        "y_wy": a["L1_xattn_Wy"].T,
        "y_wv": a["L1_xattn_Wv"].T,
        "ctx_T": a["ctx_1024"].reshape(NB * TC, D).T,
        "y_bxy": np.stack([a["L1_xattn_bx"], a["L1_xattn_by"]], 1),
        "y_bv": a["L1_xattn_bv"][None],
        "mask_c": mask.reshape(8, 128).T,
        "mask_r": a["mask_BxS2_ik1"].reshape(1, NB * TC),
        "f_w1": a["L1_ffn_W1"].transpose(1, 0, 2),
        "f_b1": a["L1_ffn_b1"],
        "f_wo": a["L1_ffn_Wo"].reshape(4, 128, D).transpose(1, 0, 2),
        "f_rw": a["L1_ffn_Wr"].T,
        "f_bo": a["L1_ffn_bo"][None],
        "f_gb": np.concatenate([a["L1_ffn_gamma"], a["L1_ffn_beta"]])[None],
        "sel8": np.repeat(np.eye(8, dtype=np.float32), 128, axis=1),
    }
    arrays = {k: np.ascontiguousarray(v) for k, v in arrays.items()}
    nc = bacc.Bacc("TRN2", target_bir_lowering=False, num_devices=1)
    io = {k: nc.dram_tensor(k, v.shape, mybir.dt.from_np(v.dtype), kind="ExternalInput").ap()
          for k, v in arrays.items()}
    io["out"] = nc.dram_tensor("out", [128, NT, 128], F32, kind="ExternalOutput").ap()
    for k, (shape, dt) in SCRATCH.items():
        io[k] = nc.dram_tensor(k, shape, dt).ap()
    build(nc, io, PHASES)
    r = run_bass_kernel_spmd(nc, [arrays], core_ids=[0])
    out = r.results[0]["out"]
    return np.ascontiguousarray(out.transpose(1, 0, 2)).reshape(NB, T, D)
```

```python
from contextlib import ExitStack

import numpy as np
import concourse.bass as bass
from concourse import mybir

F32 = mybir.dt.float32
F16 = mybir.dt.float16
I32 = mybir.dt.int32
U32 = mybir.dt.uint32
ALU = mybir.AluOpType
ACT = mybir.ActivationFunctionType
AX = mybir.AxisListType.X

NB, T, D, TC = 4, 512, 128, 154
NT = NB * T // 128
ARENA = 48128


class Eng:

    def __init__(self, name, sem):
        self.name, self.sem, self.q, self.n, self.seen = name, sem, [], 0, {}

    def wait(self, *tokens):
        for t in tokens:
            if t is None:
                continue
            if isinstance(t, list):
                self.wait(*t)
                continue
            sem, v = t
            if self.seen.get(id(sem), 0) < v:
                self.seen[id(sem)] = v
                self.q.append(lambda e, sem=sem, v=v: e.wait_ge(sem, v))

    def op(self, f, inc=True):
        if self.name == "pool":
            self.wait(self.last)
        if inc:
            self.n += 1
            self.q.append(lambda e: f(e).then_inc(self.sem, 1))
        else:
            self.q.append(f)
        return (self.sem, self.n)

    @property
    def last(self):
        return (self.sem, self.n)


def build(nc, io, phases=6):
    with ExitStack() as ctx:
        def sb(name, shape, dt):
            return ctx.enter_context(nc.sbuf_tensor("sb_" + name, shape, dt))

        def sem(name):
            return ctx.enter_context(nc.semaphore(name))

        PE, DV, AC, PO = (Eng(n, sem("s_" + n)) for n in ("pe", "dve", "act", "pool"))
        SP = Eng("sp", sem("s_sp"))
        compute = (PE, DV, AC, PO)

        arena = sb("arena", [128, ARENA], F32)
        top = [0]

        def take(words, dt=F32):
            a = arena[:, top[0]:top[0] + words]
            top[0] += words
            assert top[0] <= ARENA, top[0]
            return a if dt == F32 else a.bitcast(dt)

        PS = ctx.enter_context(nc.psum_tensor("ps", [128, 8, 512], F32))
        RING = 6
        ptr = [0]
        freed = [None] * 8

        def banks(n=1):
            if ptr[0] + n > RING:
                ptr[0] = 0
            b = ptr[0]
            ptr[0] = (b + n) % RING
            assert "taken" not in freed[b:b + n]
            PE.wait(*freed[b:b + n])
            freed[b:b + n] = ["taken"] * n
            return b

        def free(b, n, *tokens):
            for i in range(b, b + n):
                freed[i] = list(tokens)

        dma_sems = {}

        def dma(group, out, in_, *waits, eng=None):
            eng = eng or SP
            if group not in dma_sems:
                dma_sems[group] = [sem("d_" + group), 0]
            s = dma_sems[group]
            s[1] += 16
            eng.wait(*waits)
            eng.q.append(lambda e: e.dma_start(out, in_).then_inc(s[0], 16))
            return (s[0], s[1])

        def barrier():
            tokens = [e.last for e in compute] + [(s[0], s[1]) for s in dma_sems.values()]
            for e in compute + (SP,):
                e.wait(*tokens)
            for i in range(8):
                freed[i] = None

        def mm(out, lhsT, rhs, start=True, stop=True, inc=False):
            return PE.op(lambda e: e.matmul(out, lhsT, rhs, start=start, stop=stop,
                                            skip_group_check=True), inc)

        def tr(out, a, inc=False):
            return PE.op(lambda e: e.transpose(out, a, ident[:]), inc)

        def tt(eng, out, a, b, op):
            return eng.op(lambda e: e.tensor_tensor(out, a, b, op))

        def ts(eng, out, a, s1, op0, s2=None, op1=None):
            if op1 is None:
                return eng.op(lambda e: e.tensor_scalar(out, a, s1, None, op0))
            return eng.op(lambda e: e.tensor_scalar(out, a, s1, s2, op0, op1))

        def stt(out, a, s, b, op0, op1):
            return DV.op(lambda e: e.scalar_tensor_tensor(out=out, in0=a, scalar=s, in1=b, op0=op0, op1=op1))

        def cp(eng, out, a):
            if eng is AC:
                return AC.op(lambda e: e.activation(out, a, ACT.Copy))
            return eng.op(lambda e: e.tensor_copy(out, a))

        def act(out, a, f, scale=1.0, bias=0.0):
            return AC.op(lambda e: e.activation(out, a, f, scale=scale, bias=bias))

        def red(out, a, op):
            return DV.op(lambda e: e.tensor_reduce(out, a, AX, op))

        def memset(eng, out, v):
            return eng.op(lambda e: e.memset(out, v))

        def recip(out, a):
            return DV.op(lambda e: e.reciprocal(out, a))

        def D1(tok):
            DV.wait(tok)
            return tok

        def weave(*streams):
            live = [[g, n, 0] for g, n in streams]
            while live:
                s = min(live, key=lambda s: (s[2] + 1) / s[1])
                s[2] += 1
                if next(s[0], StopIteration) is StopIteration:
                    live.remove(s)

        X = sb("X", [128, NT, 128], F32)
        XT = sb("XT", [128, NB * T], F32)
        ident = sb("ident", [128, 128], F32)
        ident16 = sb("ident16", [128, 128], F16)
        ones = sb("ones", [128, 128], F32)
        sq = sb("sq", [128, 4, 128], F32)
        st = sb("st", [128, 12, 4], F32)
        magic = 0x5F3759DF

        ld = [dma("c", X[:], io["x_tm"]), dma("c", XT[:], io["x_T"]), dma("c", ident[:], io["ident"])][-1]
        DV.wait(ld)
        DV.op(lambda e: e.memset(ones[:], 1.0))
        base = cp(DV, ident16[:], ident[:])
        for e in compute + (SP,):
            e.wait(ld, base)

        xt_ready = [None] * NB
        x_ready = [None] * NB

        def rsqrt(v, y, a, b):
            D1(DV.op(lambda e: e.tensor_scalar(a.bitcast(I32), v.bitcast(I32), 1, None,
                                               ALU.logical_shift_right)))
            D1(DV.op(lambda e: e.tensor_scalar(y.bitcast(I32), a.bitcast(I32), -1.0, float(magic),
                                               ALU.mult, ALU.add)))
            for _ in range(4):
                D1(tt(DV, a, y, y, ALU.mult))
                D1(stt(b, a, -0.5, v, ALU.mult, ALU.mult))
                t = D1(stt(y, b, 1.5, y, ALU.add, ALU.mult))
            return t

        def bc(a, n):
            return a.unsqueeze(2).broadcast_to([a.shape[0], a.shape[1], n])

        def normalize(x, eps, out=None):
            out = x if out is None else out
            D1(red(st[:, 0, :], x, ALU.add))
            D1(ts(DV, st[:, 1, :], st[:, 0, :], 1.0 / D, ALU.mult))
            D1(tt(DV, out, x, bc(st[:, 1, :], D), ALU.subtract))
            D1(tt(DV, sq[:], out, out, ALU.mult))
            D1(red(st[:, 2, :], sq[:], ALU.add))
            D1(ts(DV, st[:, 3, :], st[:, 2, :], 1.0 / D, ALU.mult, eps, ALU.add))
            rsqrt(st[:, 3, :], st[:, 4, :], st[:, 5, :], st[:, 6, :])
            return D1(tt(DV, out, out, bc(st[:, 4, :], D), ALU.mult))

        def transpose4(src, ready):
            b = banks()
            PE.wait(ready)
            for j in range(4):
                t = tr(PS[:, b, 128 * j:128 * j + 128], src[:, j, :], j == 3)
            return b, t

        def residual(b, ps, ps_ready, eps=1e-5):
            xb = X[:, 4 * b:4 * b + 4, :]
            DV.wait(ps_ready, x_ready[b], xt_ready[b])
            t = D1(tt(DV, xb, xb, PS[:, ps, :].rearrange("p (a b) -> p a b", a=4), ALU.add))
            free(ps, 1, t)
            x_ready[b] = normalize(xb, eps)

        def turn(b):
            tb, t2 = transpose4(X[:, 4 * b:4 * b + 4, :], x_ready[b])
            AC.wait(t2)
            t3 = cp(AC, XT[:, T * b:T * b + T], PS[:, tb, :])
            free(tb, 1, t3)
            xt_ready[b] = t3

        def l0_attn():
            top[0] = 0
            w = take(384)
            wm = take(384)
            wo = take(128)
            wom = take(128)
            bo = take(128)
            bom = take(128)
            for o, i in ((w, "qkv_w"), (wm, "qkv_m"), (wo, "ow"), (wom, "om"), (bo[0:1], "ob"), (bom[0:1], "obm")):
                l = dma("w0", o, io[i])
            DV.wait(l)
            gate = 1.5 * 2.0 ** -24
            D1(ts(DV, wm, wm, gate, ALU.is_gt))
            D1(ts(DV, wom, wom, gate, ALU.is_gt))
            D1(ts(DV, bom[0:1], bom[0:1], gate, ALU.is_gt))
            tt(DV, w, w, wm, ALU.mult)
            tt(DV, wo, wo, wom, ALU.mult)
            wr = D1(tt(DV, bo[0:1], bo[0:1], bom[0:1], ALU.mult))
            H = [take(256, F16) for _ in range(2)]
            L = [take(256, F16) for _ in range(2)]
            QS32, KS32, VP32 = [[take(n) for _ in range(2)] for n in (4096, 2048, 3072)]
            QS = [t.bitcast(F16).rearrange("p (t h n) -> p t h n", t=2, h=8) for t in QS32]
            KS = [t.bitcast(F16).rearrange("p (h n) -> p h n", h=8) for t in KS32]
            VP = [t.bitcast(F16).rearrange("p (c g h x) -> p (c g) h x", c=4, g=4, h=4) for t in VP32]
            E = [take(1024).rearrange("p (c n) -> p c n", c=2) for _ in range(4)]
            EH, EL = [[take(1024, F16).rearrange("p (c n) -> p c n", c=4) for _ in range(3)] for _ in range(2)]
            rec, dn = take(512), take(512)
            oT = [take(512) for _ in range(2)]
            mx = take(64).rearrange("p (q h) -> p q h", q=4)
            mneg = take(32, F16).rearrange("p (q h) -> p q h", q=4)
            mrow = take(256, F16)
            zeros = []

            def clear(i):
                memset(PO, KS32[i], 0.0)
                k = PO.last
                memset(DV, QS32[i][:, 0:2048], 0.0)
                DV.wait(memset(DV, VP32[i], 0.0))
                for r in (32, 96):
                    o = dma("a0o", KS[i][r:r + 1], io["ones16"].unsqueeze(0), k)
                memset(PO, QS32[i][:, 2048:], 0.0)
                for h in range(4):
                    memset(DV, VP[i][:, :, h, 64 + 8 * h:72 + 8 * h], 1.0)
                zeros.append([DV.last, PO.last, o])
            clear(0)
            scr_qk, scr_m = io["s_qk0"], io["s_m0"]
            pv_done = {}
            oT_free = {}
            E_free = {}
            er_free, e_n, dn_free = {}, [0], [None]
            prep = {}

            def part_a(b):
                i = b % 2
                cols = slice(T * b, T * b + T)
                PE.wait(wr, xt_ready[b])
                bq = banks(2)
                for k in range(2):
                    t = mm(PS[:, bq + k, :], w[:, 128 * k:128 * k + 128], XT[:, cols], inc=True)
                bv = banks()
                for c in range(4):
                    tv = mm(PS[:, bv, 128 * c:128 * c + 128], XT[:, T * b + 128 * c:T * b + 128 * c + 128],
                            w[:, 256:384], inc=(c == 3))
                prev = prep.get(b - 1, {})
                zero = zeros[i]
                AC.wait(t, prev.get("scr"))
                for k in range(2):
                    h = cp(AC, H[k], PS[:, bq + k, :])
                DV.wait(h, t, prev.get("scr"))
                for k in range(2):
                    lo = tt(DV, L[k], PS[:, bq + k, :], H[k], ALU.subtract)
                free(bq, 2, lo, h)
                for k in range(2):
                    dma("a0w", scr_qk[k, 0], H[k], h, prev.get("rd"))
                    wrt = dma("a0w", scr_qk[k, 1], L[k], lo)
                done = pv_done.get(b - 2)
                for par in range(2):
                    p0 = 64 * par
                    if b > 1:
                        dma("a0r", QS[i][p0 + 32:p0 + 33, par], io["zeros"].unsqueeze(0), done)
                    src = scr_qk.rearrange("k s (h t d) n -> k s t d h n", t=2, d=8)
                    for r in range(4):
                        dma("a0r", QS[i][p0 + 8 * r:p0 + 8 * r + 8, par], src[0, r // 2, par], wrt, done, zero)
                        rd = dma("a0r", KS[i][p0 + 8 * r:p0 + 8 * r + 8], src[1, r % 2, par])
                DV.wait(tv, done, zero)
                src = PS[:, bv, :].rearrange("p (k h d) -> p k h d", h=4, d=8)
                for h in range(4):
                    vt = cp(DV, VP[i][:, :, h, 8 * h:8 * h + 8], src[:, :, h])
                D1(vt)
                for h in range(4):
                    vt = tt(DV, VP[i][:, :, h, 32 + 8 * h:40 + 8 * h], src[:, :, h], VP[i][:, :, h, 8 * h:8 * h + 8],
                            ALU.subtract)
                free(bv, 1, vt)
                if b == 0:
                    clear(1)
                for k in range(4):
                    yield
                    if k == 1 and b > 1:
                        part_c(b - 2)
                PE.wait(rd)
                for h in range(16):
                    par, hp = h % 2, h // 2
                    if h == 3 and b > 1:
                        turn(b - 2)
                    for q2 in range(2):
                        yield
                        bb = banks(2)
                        for q in range(2):
                            qt = 2 * q2 + q
                            t = mm(PS[:, bb + q, :], QS[i][:, par, hp, 128 * qt:128 * qt + 128], KS[i][:, hp, :],
                                   inc=(q == 1))
                        DV.wait(t)
                        r = red(mx[:, 2 * q2:2 * q2 + 2, 8 * par + hp], PS[:, bb:bb + 2, :], ALU.max)
                        free(bb, 2, r)
                D1(r)
                DV.wait(prev.get("mt"))
                mt = ts(DV, mneg, mx, -1.0, ALU.mult)
                yield
                bm = banks()
                PE.wait(mt)
                for qt in range(4):
                    t = mm(PS[0:16, bm, 128 * qt:128 * qt + 128], mneg[:, qt, :], ident16[:], inc=(qt == 3))
                AC.wait(t, prev.get("mscr"))
                c = cp(AC, mrow[0:16], PS[0:16, bm, :])
                free(bm, 1, c)
                mw = dma("a0m", scr_m, mrow[0:16], c, prev.get("mrd"))
                for par in range(2):
                    m = dma("a0mr", QS[i][64 * par + 32:64 * par + 33, par], scr_m[8 * par:8 * par + 8].unsqueeze(0), mw, r)
                prep[b] = {"scr": wrt, "rd": rd, "mt": t, "mscr": mw, "mrd": m, "vt": vt}

            def part_b(b):
                i = b % 2
                PE.wait(prep[b]["mrd"], prep[b]["vt"], zeros[i])
                pend = []

                def pv(h, ej, split, half):
                    g, acc = h // 4, 6 + h // 4 % 2
                    PE.wait(split[half])
                    if h % 4 == 0 and half == 0:
                        PE.wait(freed[acc])
                    for c in range(2 * half, 2 * half + 2):
                        lv = VP[i][:, 4 * c + g, h % 4]
                        mm(PS[0:96, acc, :], lv, EH[ej][:, c, :], start=(h % 4 == 0 and c == 0), stop=False)
                        t = mm(PS[0:96, acc, :], lv, EL[ej][:, c, :], start=False, stop=(h % 4 == 3 and c == 3),
                               inc=(c == 3))
                    if half == 0:
                        return
                    E_free[ej] = t
                    if h % 4 == 3:
                        r = slice(32 * g, 32 * g + 32)
                        AC.wait(t, dn_free[0])
                        d = cp(AC, dn[r], PS[64:96, acc, :])
                        DV.wait(t, d, oT_free.get(i))
                        o = D1(cp(DV, oT[i][r], PS[32:64, acc, :]))
                        o = tt(DV, oT[i][r], PS[0:32, acc, :], oT[i][r], ALU.add)
                        free(acc, 1, d, o)
                        pv_done[b] = [t, d, o]
                lows, splits = [], [None, None]

                def low(x):
                    h, ej, er, c2, hi, token = x
                    c = slice(2 * c2, 2 * c2 + 2)
                    eng = PO if c2 == 0 else DV
                    eng.wait(hi, E_free.get((ej, h)))
                    if b == NB - 1 and c2:
                        D1(cp(DV, EH[ej][:, c, :], E[er]))
                    token[0] = tt(eng, EL[ej][:, c, :], E[er], EH[ej][:, c, :], ALU.subtract)
                for h in range(16):
                    par, hp = h % 2, h // 2
                    ej = (16 * b + h) % 3
                    E_free[ej, h] = E_free.get(ej)
                    for c2 in range(2):
                        er = e_n[0] % 4
                        e_n[0] += 1
                        bb = banks(2)
                        for c in range(2):
                            kc = 2 * c2 + c
                            t = mm(PS[:, bb + c, :], KS[i][:, hp, 128 * kc:128 * kc + 128], QS[i][:, par, hp, :],
                                   inc=(c == 1))
                        AC.wait(t, er_free.get(er))
                        ex = act(E[er], PS[:, bb:bb + 2, :], ACT.Exp, scale=float(D) ** -0.5)
                        free(bb, 2, ex)
                        AC.wait(ex, E_free.get(ej))
                        c = slice(2 * c2, 2 * c2 + 2)
                        hi = ex if b == NB - 1 and c2 else cp(AC, EH[ej][:, c, :], E[er])
                        low(lows.pop(0)) if lows else None
                        split = er_free[er] = [None]
                        lows.append((h, ej, er, c2, hi, split))
                        if pend:
                            pv(*pend[0], c2)
                        yield
                        splits[c2] = split
                    pend = [(h, ej, list(splits))]
                low(lows.pop(0))
                pv(*pend[0], 0)
                pv(*pend[0], 1)
                yield
                t, d, o = pv_done[b]
                pv_done[b] = t
                DV.wait(d, o)
                D1(recip(rec, dn))
                po = dn_free[0] = D1(tt(DV, oT[i], oT[i], rec, ALU.mult))
                outs[b] = (po, i)

            def part_c(b):
                po, i = outs[b]
                bo_ = banks()
                PE.wait(po)
                for j in range(4):
                    o = PS[:, bo_, 128 * j:128 * j + 128]
                    mm(o, oT[i][:, 128 * j:128 * j + 128], wo, stop=False)
                    t = mm(o, ones[0:1, :], bo[0:1], start=False, inc=(j == 3))
                oT_free[i] = t
                residual(b, bo_, t)

            outs = {}

            def stream_a(b):
                if b < NB:
                    yield from part_a(b)
                else:
                    yield
                    yield
                    part_c(b - 2)
                    for _ in range(8):
                        yield
                    turn(b - 2)
            weave((stream_a(0), 1))
            for b in range(NB):
                weave((stream_a(b + 1), 38 if b + 1 < NB else 33), (part_b(b), 33))
            part_c(NB - 1)
            turn(NB - 1)

        def l0_xattn():
            top[0] = 0
            NK = TC + T
            sizes = [128] * 5 + [26]
            wq, wk, wv, wo = take(1024), take(1024), take(1024), take(1024).rearrange("p (a n) -> p a n", a=8)
            ln = take(4)
            sel = take(1024).rearrange("p (a n) -> p a n", a=8)
            KV = take(NB * NK).rearrange("p (b n) -> p b n", b=NB)
            CX = take(1024).rearrange("p (a n) -> p a n", a=8)
            for o, i in ((wq, "x_wq"), (wk, "x_wk"), (wv, "x_wv"), (wo, "x_wo"), (ln, "x_ln"), (CX, "ctx_tm"),
                         (sel[64:80], "sel16")):
                l = dma("w1", o, io[i])
            Hq, Lq = [take(512, F16).rearrange("p (a n) -> p a n", a=2) for _ in range(2)]
            Hk, Lk = [take(NK, F16).rearrange("p (a n) -> p a n", a=2) for _ in range(2)]

            def four(words):
                return [take(words, F16).rearrange("p (t a n) -> p t a n", t=2, a=2) for _ in range(2)]
            M1, M2, S1, S2 = four(1024), four(1024), four(2 * NK), four(2 * NK)
            VH = [take(960, F16).rearrange("p (c h n) -> p c h n", c=6, h=4) for _ in range(4)]
            VL = [take(768, F16).rearrange("p (c h n) -> p c h n", c=6, h=4) for _ in range(4)]
            E = [take(1024).rearrange("p (c n) -> p c n", c=2) for _ in range(3)]
            EH, EL = [[take(1536, F16).rearrange("p (c n) -> p c n", c=6) for _ in range(2)] for _ in range(2)]
            er_free, e_n = {}, [0]
            OT = [take(4096).rearrange("p (a n) -> p a n", a=8) for _ in range(2)]
            den = [take(512) for _ in range(2)]
            rden = take(512)
            LX = take(512).rearrange("p (a n) -> p a n", a=4)
            mx = take(16).rearrange("p (q h) -> p q h", q=4)
            mneg = take(8, F16).rearrange("p (q h) -> p q h", q=4)
            mrow = take(256, F16)
            for g in range(4):
                PO.op(lambda e, g=g: e.memset(VH[g][:, :, :, 64:80], 0.0))
                for j in range(4):
                    h = 4 * g + j
                    PO.op(lambda e, g=g, j=j, h=h: e.memset(VH[g][:, :, j, 64 + h:65 + h], 1.0))
            for i in range(2):
                memset(PO, S2[i][64:128], 0.0)
                memset(PO, M2[i][64:128], 0.0)
                memset(PO, S2[i][64:65], 1.0)
            zero = PO.last
            DV.wait(l)
            PE.wait(l)
            for half in range(2):
                t = normalize(CX[:, 4 * half:4 * half + 4, :], 1e-5)
                tb, t = transpose4(CX[:, 4 * half:4 * half + 4, :], t)
                DV.wait(t)
                for j in range(2):
                    k = ts(DV, KV[:, 2 * half + j, 0:TC], PS[:, tb, 256 * j:256 * j + TC], ln[:, 0:1], ALU.mult,
                           ln[:, 1:2], ALU.add)
                free(tb, 1, k)
            kv_ready = {}
            s = {}
            E_free, vp_free, den_t = {}, {}, {}
            ot_free, done_pv = {}, {}

            def latents(b):
                DV.wait(x_ready[b], lx_free[0])
                t = normalize_to(LX, X[:, 4 * b:4 * b + 4, :])
                tb, t = transpose4(LX, t)
                lx_free[0] = t
                DV.wait(t)
                k = ts(DV, KV[:, b, TC:], PS[:, tb, :], ln[:, 2:3], ALU.mult, ln[:, 3:4], ALU.add)
                free(tb, 1, k)
                kv_ready[b] = k

            lx_free = [None]

            def normalize_to(out, x):
                return normalize(x, 1e-5, out)

            def project(b, g):
                u = 4 * b + g
                i = u % 2
                prev, prev2 = s.get(u - 1, {}), s.get(u - 2, {})
                PE.wait(kv_ready[b])
                bq = banks(2)
                for a in range(2):
                    tq = mm(PS[:, bq + a, :], wq[:, 128 * (2 * g + a):128 * (2 * g + a) + 128], KV[:, b, TC:], inc=(a == 1))
                AC.wait(tq, prev.get("wr"))
                h = cp(AC, Hq, PS[:, bq:bq + 2, :])
                DV.wait(h, tq, prev.get("wr"))
                lo = tt(DV, Lq, PS[:, bq:bq + 2, :], Hq, ALU.subtract)
                free(bq, 2, h, lo)
                xw = f"xp{i}"
                dma(xw, io["s_xq"][i, 0], Hq, h, prev2.get("rd"))
                dma(xw, io["s_xq"][i, 1], Lq, lo, prev2.get("rd"))
                yield
                for a in range(2):
                    bk = banks(2)
                    kp = PS[:, bk:bk + 2, :].rearrange("p a n -> p (a n)")
                    wka = wk[:, 128 * (2 * g + a):128 * (2 * g + a) + 128]
                    mm(kp[:, 0:512], wka, KV[:, b, 0:512])
                    tk = mm(kp[:, 512:NK], wka, KV[:, b, 512:NK], inc=True)
                    AC.wait(tk)
                    h = cp(AC, Hk[:, a, :], kp[:, 0:NK])
                    DV.wait(h, tk)
                    lo = tt(DV, Lk[:, a, :], kp[:, 0:NK], Hk[:, a, :], ALU.subtract)
                    free(bk, 2, h, lo)
                dma(xw, io["s_xk"][i, 0], Hk, h, prev2.get("rd"))
                yield
                wr = dma(xw, io["s_xk"][i, 1], Lk, lo)
                s[u] = {"wr": wr}
                for c2 in range(3):
                    yield
                    bv = banks()
                    for c in range(2):
                        k = 2 * c2 + c
                        n = sizes[k]
                        tv = mm(PS[0:n, bv, 256 * c:256 * c + 256], KV[:, b, 128 * k:128 * k + n],
                                wv[:, 256 * g:256 * g + 256], inc=(c == 1))
                    AC.wait(tv, vp_free.get(g), zero)
                    ch = PS[:, bv, :].rearrange("p (c h n) -> p c h n", c=2, h=4)
                    parts = ((128, slice(0, 2)),) if c2 < 2 else ((128, slice(0, 1)), (26, slice(1, 2)))
                    for r, k in parts:
                        kc = slice(2 * c2 + k.start, 2 * c2 + k.stop)
                        v = cp(AC, VH[g][0:r, kc, :, 0:64], ch[0:r, k])
                    DV.wait(v, vp_free.get(g))
                    for r, k in parts:
                        kc = slice(2 * c2 + k.start, 2 * c2 + k.stop)
                        v = tt(DV, VL[g][0:r, kc], ch[0:r, k], VH[g][0:r, kc, :, 0:64], ALU.subtract)
                    free(bv, 1, v)
                s[u]["v"] = v

            def maxima(b, g):
                u = 4 * b + g
                i = u % 2
                prev, prev2 = s.get(u - 1, {}), s.get(u - 2, {})
                wr = s[u]["wr"]
                done = prev2.get("sc")
                xq = io["s_xq"][i].rearrange("s (t p) a n -> s p t a n", t=2)
                xk = io["s_xk"][i].rearrange("s (t p) a n -> s p t a n", t=2)
                dma("xr", M1[i][0:64], xq[0], wr, done)
                dma("xr", S1[i][0:64], xk[0], wr, done)
                dma("xr", M1[i][64:128], xq[0], wr, done)
                dma("xr", M2[i][0:64], xq[1], wr, done)
                dma("xr", S1[i][64:128], xk[1], wr, done)
                rd = dma("xr", S2[i][0:64], xk[0], wr, done)
                for _ in range(3):
                    yield
                PE.wait(rd)
                for par in range(2):
                    for a in range(2):
                        for q in range(4):
                            yield
                            bb = banks(2)
                            kp = PS[:, bb:bb + 2, :].rearrange("p a n -> p (a n)")
                            lq = M1[i][:, par, a, 128 * q:128 * q + 128]
                            mm(kp[:, 0:512], lq, S1[i][:, par, a, 0:512])
                            t = mm(kp[:, 512:NK], lq, S1[i][:, par, a, 512:NK], inc=True)
                            DV.wait(t)
                            r = red(mx[:, q, 2 * par + a:2 * par + a + 1], kp[:, 0:NK], ALU.max)
                            free(bb, 2, r)
                DV.wait(r, prev.get("mt"))
                mt = ts(DV, mneg, mx, -1.0, ALU.mult)
                yield
                yield
                bm = banks()
                PE.wait(mt)
                for q in range(4):
                    t = mm(PS[0:4, bm, 128 * q:128 * q + 128], mneg[:, q, :], ident16[:], inc=(q == 3))
                AC.wait(t, prev.get("mscr"))
                c = cp(AC, mrow[0:4], PS[0:4, bm, :])
                free(bm, 1, c)
                mw = dma("xmw", io["s_xm"], mrow[0:4], c, prev.get("mrd"))
                m = dma("xmr", M2[i][64:65].rearrange("p t a n -> p (t a) n"), io["s_xm"].unsqueeze(0), mw, done, zero)
                yield
                s[u] |= {"rd": rd, "mt": t, "mscr": mw, "mrd": m}

            def part_b(b, g):
                u = 4 * b + g
                i = u % 2
                PE.wait(s[u]["mrd"], s[u]["v"], zero)
                pend = []

                def pv(n, par, a, ej, exs, part):
                    acc = 6 + n % 2
                    PE.wait(exs[part], freed[acc])
                    for c in range(2 * part, 2 * part + 2):
                        k = sizes[c]
                        j = 2 * a + par
                        mm(PS[0:80, acc, :], VH[g][0:k, c, j, :], EH[ej][0:k, c, :], start=(c == 0), stop=False)
                        mm(PS[0:64, acc, :], VL[g][0:k, c, j, :], EH[ej][0:k, c, :], start=False, stop=False)
                        t = mm(PS[0:80, acc, :], VH[g][0:k, c, j, :], EL[ej][0:k, c, :],
                               start=False, stop=(c == 5), inc=(c == 5))
                    if part < 2:
                        return
                    E_free[ej] = t
                    AC.wait(t)
                    if n == 0 and g == 0:
                        AC.wait(ot_free.get(b % 2))
                    o = cp(AC, OT[b % 2][64 * par:64 * par + 64, 2 * g + a, :], PS[0:64, acc, :])
                    DV.wait(t, den_t.get("last"))
                    if n == 0 and g == 0:
                        d = cp(DV, den[b % 2][64:80], PS[64:80, acc, :])
                    else:
                        d = tt(DV, den[b % 2][64:80], PS[64:80, acc, :], den[b % 2][64:80], ALU.add)
                    den_t["last"] = d
                    free(acc, 1, o, d)
                    done_pv["t"], done_pv["o"] = t, o
                n = 0
                lows = []

                def low(ej, er, c2, hi, ready, token, parts):
                    eng = DV if c2 else PO
                    eng.wait(hi, ready)
                    for r, k in parts:
                        kc = slice(2 * c2 + k.start, 2 * c2 + k.stop)
                        token[0] = tt(eng, EL[ej][0:r, kc], E[er][0:r, k], EH[ej][0:r, kc], ALU.subtract)
                for par in range(2):
                    for a in range(2):
                        ej = (4 * u + n) % 2
                        exs = []
                        for c2 in range(3):
                            er = e_n[0] % 3
                            e_n[0] += 1
                            bb = banks(2)
                            for c in range(2):
                                k = 2 * c2 + c
                                z = sizes[k]
                                ks = slice(128 * k, 128 * k + z)
                                mm(PS[0:z, bb + c, :], S1[i][:, par, a, ks], M1[i][:, par, a, :], stop=False)
                                sc = mm(PS[0:z, bb + c, :], S2[i][:, par, a, ks], M2[i][:, par, a, :],
                                        start=False, inc=(c == 1))
                            AC.wait(sc, er_free.get(er))
                            parts = ((128, slice(0, 2)),) if c2 < 2 else ((128, slice(0, 1)), (26, slice(1, 2)))
                            for r, k in parts:
                                ex = act(E[er][0:r, k], PS[0:r, bb + k.start:bb + k.stop, :], ACT.Exp, scale=0.125)
                            free(bb, 2, ex)
                            AC.wait(ex, E_free.get(ej))
                            for r, k in parts:
                                kc = slice(2 * c2 + k.start, 2 * c2 + k.stop)
                                hi = cp(AC, EH[ej][0:r, kc], E[er][0:r, k])
                            if lows:
                                low(*lows.pop(0))
                            ex = er_free[er] = [None]
                            lows.append((ej, er, c2, hi, E_free.get(ej), ex, parts))
                            exs.append(ex)
                            if pend:
                                pv(*pend[0], c2)
                            yield
                        if pend:
                            pend.pop(0)
                        pend.append((n, par, a, ej, exs))
                        n += 1
                low(*lows.pop(0))
                for part in range(3):
                    pv(*pend[0], part)
                s[u]["sc"] = sc
                vp_free[g] = done_pv["t"]
                if g == 3:
                    done_pv[b] = done_pv["o"]

            def part_c(b):
                O, dn = OT[b % 2], den[b % 2]
                D1(den_t["last"])
                rt = recip(rden[64:80], dn[64:80])
                yield
                yield
                yield
                PE.wait(rt)
                DV.wait(done_pv[b])
                for a in range(8):
                    bb = banks()
                    t = mm(PS[:, bb, :], sel[64:80, a, :], rden[64:80], inc=True)
                    DV.wait(t)
                    n = tt(DV, O[:, a, :], O[:, a, :], PS[:, bb, :], ALU.mult)
                    free(bb, 1, n)
                    yield
                yield
                PE.wait(n)
                bo = banks()
                for j in range(4):
                    for a in range(8):
                        t = mm(PS[:, bo, 128 * j:128 * j + 128], O[:, a, 128 * j:128 * j + 128], wo[:, a, :],
                               start=(a == 0), stop=(a == 7), inc=(j == 3 and a == 7))
                ot_free[b % 2] = t
                residual(b, bo, t)

            def stream_p(u):
                if u < 16:
                    yield from project(u // 4, u % 4)
                if u % 4 == 2 and u > 4:
                    yield from part_c(u // 4 - 1)
                if u % 4 == 0 and u > 4:
                    turn(u // 4 - 2)

            for b in range(NB):
                latents(b)
            weave((project(0, 0), 1))
            weave((maxima(0, 0), 20), (project(0, 1), 7))
            for u in range(16):
                b, g = u // 4, u % 4
                streams = [(part_b(b, g), 13), (stream_p(u + 2), 7 + (12 if g == 0 and u else 0))]
                if u < 15:
                    streams.append((maxima((u + 1) // 4, (u + 1) % 4), 26))
                weave(*streams)
            weave((part_c(NB - 1), 1))
            turn(NB - 1)

        def pick(b, lg, n, bits, idx, idxf):
            for j in range(4):
                t = DV.op(lambda e, j=j: e.max(bits[:, j, :], lg[:, j, :]))
            D1(t)
            for j in range(4):
                t = DV.op(lambda e, j=j: e.max_index(idx[:, j, :], bits[:, j, :], lg[:, j, :]))
            D1(t)
            return D1(cp(DV, idxf, idx[:, :, 0:2]))

        def l0_ffn():
            top[0] = 0
            up, gt = take(1024), take(1024)
            dn = take(1024 + 128).rearrange("p (a n) -> p a n", a=9)
            sg, su = take(128), take(128)
            rw, rb, iota = take(16), take(16), take(16)
            sel = take(1024).rearrange("p (a n) -> p a n", a=8)
            for o, i in ((up, "m_up"), (gt, "m_gate"), (dn, "m_down"), (sg, "m_sg"), (su, "m_su"), (rw, "m_rw"),
                         (rb[0:1], "m_rb"), (iota, "iota16"), (sel[0:16], "sel16")):
                l = dma("w2", o, io[i])
            v4 = lambda n, m: take(4 * n * m).rearrange("p (k a n) -> p k a n", k=n, a=4)
            lg = v4(1, 16)[:, 0]
            m8, i8 = v4(1, 8)[:, 0], v4(1, 8)[:, 0].bitcast(U32)
            ixf = v4(1, 2)[:, 0]
            oh = v4(3, 16)
            wt = take(16).rearrange("p (k a) -> p k a", k=4)
            CT = [take(512) for _ in range(2)]
            SG = [take(512) for _ in range(3)]
            Hh = [take(4608).rearrange("p (a n) -> p a n", a=9) for _ in range(2)]
            PE.wait(l)
            DV.wait(l)
            ct_ready, h_free, sg_free = {}, {}, {}
            iob = iota.unsqueeze(1).broadcast_to([128, 4, 16])

            def route(b):
                bb = banks()
                PE.wait(xt_ready[b])
                for j in range(4):
                    o = PS[:, bb, 16 * j:16 * j + 16]
                    mm(o, XT[:, T * b + 128 * j:T * b + 128 * j + 128], rw, stop=False)
                    t = mm(o, ones[0:1, :], rb[0:1], start=False, inc=(j == 3))
                DV.wait(t)
                t = D1(cp(DV, lg, PS[:, bb, 0:64].rearrange("p (a n) -> p a n", a=4)))
                free(bb, 1, t)
                pick(b, lg, 16, m8, i8, ixf)
                t = D1(tt(DV, wt[:, 0, :], m8[:, :, 1], m8[:, :, 0], ALU.subtract))
                AC.wait(t)
                t = act(wt[:, 1, :], wt[:, 0, :], ACT.Exp)
                DV.wait(t)
                D1(ts(DV, wt[:, 0, :], wt[:, 1, :], 1.0, ALU.add))
                D1(recip(wt[:, 2, :], wt[:, 0, :]))
                D1(tt(DV, wt[:, 3, :], wt[:, 1, :], wt[:, 2, :], ALU.mult))
                tt(DV, oh[:, 0], iob, bc(ixf[:, :, 0], 16), ALU.is_equal)
                D1(tt(DV, oh[:, 1], iob, bc(ixf[:, :, 1], 16), ALU.is_equal))
                tt(DV, oh[:, 0], oh[:, 0], bc(wt[:, 2, :], 16), ALU.mult)
                D1(tt(DV, oh[:, 1], oh[:, 1], bc(wt[:, 3, :], 16), ALU.mult))
                t = D1(tt(DV, oh[:, 2], oh[:, 0], oh[:, 1], ALU.add))
                bb = banks()
                PE.wait(t)
                for j in range(4):
                    t = tr(PS[0:16, bb, 128 * j:128 * j + 128], oh[:, 2, j, :], j == 3)
                D1(t)
                t = cp(DV, CT[b % 2][0:16], PS[0:16, bb, :])
                free(bb, 1, t)
                ct_ready[b] = t

            def experts(b):
                cols = slice(T * b, T * b + T)
                H = Hh[b % 2]
                PE.wait(xt_ready[b])
                for p in range(9):
                    i = (9 * b + p) % 3
                    bu = banks(2)
                    c = slice(128 * p, 128 * p + 128)
                    tg = mm(PS[:, bu, :], gt[:, c] if p < 8 else sg, XT[:, cols], inc=True)
                    t = mm(PS[:, bu + 1, :], up[:, c] if p < 8 else su, XT[:, cols], inc=True)
                    AC.wait(tg, sg_free.get(i))
                    a = act(SG[i], PS[:, bu, :], ACT.Silu)
                    DV.wait(a, t, h_free.get(b % 2))
                    if p == 8:
                        t = tt(DV, H[:, p, :], SG[i], PS[:, bu + 1, :], ALU.mult)
                        free(bu, 2, t)
                    else:
                        bw = 6 + p % 2
                        PE.wait(ct_ready[b], freed[bw])
                        w = mm(PS[:, bw, :], sel[0:16, p, :], CT[b % 2][0:16], inc=True)
                        t = D1(tt(DV, SG[i], SG[i], PS[:, bu + 1, :], ALU.mult))
                        free(bu, 2, t)
                        DV.wait(w)
                        t = tt(DV, H[:, p, :], SG[i], PS[:, bw, :], ALU.mult)
                        free(bw, 1, t)
                    sg_free[i] = t
                return t

            def down(b, ready):
                H = Hh[b % 2]
                bo = banks()
                PE.wait(ready)
                for j in range(4):
                    for p in range(9):
                        t = mm(PS[:, bo, 128 * j:128 * j + 128], H[:, p, 128 * j:128 * j + 128], dn[:, p, :],
                               start=(p == 0), stop=(p == 8), inc=(j == 3 and p == 8))
                h_free[b % 2] = t
                residual(b, bo, t)
            route(0)
            for b in range(NB):
                if b + 1 < NB:
                    route(b + 1)
                h = experts(b)
                down(b, h)
                if b:
                    turn(b - 1)
            turn(NB - 1)

        def l1_attn():
            top[0] = 0
            wq, wk, wv, wo = take(1024), take(1024), take(1024), take(1024).rearrange("p (a n) -> p a n", a=8)
            wb, bb_ = take(16), take(16)
            maskL, maskU = take(128), take(128)
            for o, i in ((wq, "d_wq"), (wk, "d_wk"), (wv, "d_wv"), (wo, "d_wo"), (wb, "d_wb"), (bb_[0:1], "d_bb"),
                         (maskL, "mask_l"), (maskU, "mask_u")):
                l = dma("w3", o, io[i])
            Kn = [take(4096).rearrange("p (c n) -> p c n", c=4) for _ in range(2)]
            KT = [take(4096).rearrange("p (a n) -> p a n", a=8) for _ in range(2)]
            beta = [take(64).rearrange("p (h c) -> p h c", h=16) for _ in range(2)]
            GA = take(2048)
            XI = take(2048)
            tmp = take(512)
            sqk = take(512)
            ss = take(64 * 4).rearrange("p (k c h) -> p k c h", k=4, c=4)
            two = range(2)
            QT = [take(1024).rearrange("p (a n) -> p a n", a=2) for _ in two]
            V = [take(1024).rearrange("p (c n) -> p c n", c=4) for _ in two]
            LN_ = [take(2048).rearrange("p (h c n) -> p h c n", h=4, c=4) for _ in two]
            P = [take(2048).rearrange("p (h c n) -> p h c n", h=4, c=4) for _ in two]
            XE = [take(2048).rearrange("p (h c n) -> p h c n", h=4, c=4) for _ in two]
            OT = take(1024).rearrange("p (a n) -> p a n", a=2)
            BD = take(2048).rearrange("p (k t n) -> p k t n", k=2, t=2)
            KB = take(1024).rearrange("p (t n) -> p t n", t=2)
            S = [take(256).rearrange("p (a n) -> p a n", a=2) for _ in two]
            R, A, B = [take(256) for _ in range(3)]
            for e in compute:
                e.wait(l)
            for i in two:
                memset(PO, XE[i], 0.0)
                zero = memset(PO, S[i], 0.0)
            memset(PO, BD, 0.0)
            zero = memset(PO, KB, 0.0)
            s1, s2 = {}, {}
            sq_read, kb_read = [None], [None]

            def stage1(b):
                i = b % 2
                prev = s1.get(b - 1, {})
                done = s2.get(b - 2)
                PE.wait(xt_ready[b])
                bbk = banks()
                for c in range(4):
                    o = PS[:, bbk, 16 * c:16 * c + 16]
                    mm(o, XT[:, T * b + 128 * c:T * b + 128 * c + 128], wb, stop=False)
                    t = mm(o, ones[0:1, :], bb_[0:1], start=False, inc=(c == 3))
                AC.wait(t, done)
                t = act(beta[i].rearrange("p h c -> p c h"), PS[:, bbk, 0:64].rearrange("p (c h) -> p c h", c=4), ACT.Sigmoid)
                free(bbk, 1, t)
                bt = t
                AC.wait(done)
                for c in range(4):
                    for j in range(2):
                        bk = banks()
                        t = mm(PS[:, bk, :], XT[:, T * b + 128 * c:T * b + 128 * c + 128],
                               wk[:, 512 * j:512 * j + 512], inc=True)
                        AC.wait(t)
                        k = cp(AC, Kn[i][:, c, 512 * j:512 * j + 512], PS[:, bk, :])
                        AC.wait(sq_read[0])
                        t = act(sqk, PS[:, bk, :], ACT.Square)
                        free(bk, 1, t, k)
                        DV.wait(t)
                        r = sq_read[0] = red(ss[:, 0, c, 8 * j:8 * j + 8], sqk.rearrange("p (h n) -> p h n", h=8), ALU.add)
                        yield
                D1(r)
                fl = [ss[:, k].rearrange("p c h -> p (c h)") for k in range(4)]
                D1(ts(DV, fl[0], fl[0], 1e-24, ALU.max))
                rsqrt(fl[0], fl[1], fl[2], fl[3])
                for c in range(4):
                    kc = Kn[i][:, c, :].rearrange("p (h n) -> p h n", h=16)
                    t = tt(DV, kc, kc, bc(ss[:, 1, c], 64), ALU.mult)
                yield
                yield
                yield
                PE.wait(t)
                G = GA.rearrange("p (h c n) -> p h c n", h=16, c=4)
                for p in range(8):
                    bk = banks()
                    for c in range(4):
                        t = tr(PS[:, bk, 128 * c:128 * c + 128], Kn[i][:, c, 128 * p:128 * p + 128], c == 3)
                    AC.wait(t)
                    k = cp(AC, KT[i][:, p, :], PS[:, bk, :])
                    AC.wait(kb_read[0], zero)
                    for par in range(2):
                        k = cp(AC, KB[64 * par:64 * par + 64, par, :], PS[64 * par:64 * par + 64, bk, :])
                    free(bk, 1, k)
                    yield
                    PE.wait(k)
                    if p == 0:
                        DV.wait(bt, prev.get("ga_free"))
                    bk = banks(2)
                    for c in range(4):
                        cc = slice(128 * c, 128 * c + 128)
                        t = mm(PS[:, bk + c // 2, 256 * (c % 2):256 * (c % 2) + 256], KT[i][:, p, cc], KB[:, :, cc],
                               inc=(c == 3))
                    kb_read[0] = t
                    DV.wait(t)
                    for q in range(4):
                        r = slice(32 * q, 32 * q + 32)
                        for par in range(2):
                            src = PS[r, bk:bk + 2, :].rearrange("p k (c h n) -> p (k c) h n", c=2, h=2)[
                                :, :, par, 32 * q:32 * q + 32]
                            g = tt(DV, G[r, 2 * p + par], src, bc(beta[i][r, 2 * p + par, :], 32), ALU.mult)
                    free(bk, 2, g)
                    yield
                w = dma("gw", io["s_g"], GA, g, prev.get("grd"))
                sg = io["s_g"].rearrange("(q t) (l u s) -> q l u t s", q=4, l=2, u=32)
                L4 = GA.rearrange("p (l t s) -> p l t s", l=2, t=32)
                for q in range(4):
                    for sl in range(2):
                        rd = dma("gr", L4[32 * q:32 * q + 32, sl], sg[q, sl], w)
                XL = XI.rearrange("p (l s t) -> p l s t", l=2, s=32)
                for sl in range(2):
                    rd = dma("gr", XI[:, 1024 * sl:1024 * sl + 1024], io["eye32"], prev.get("xw"))
                PO.wait(rd)
                for t in range(31, 0, -1):
                    n = 32 - t
                    tm = tmp[:, 0:2 * t * n].rearrange("p (l s t) -> p l s t", l=2, s=t)
                    a = L4[:, :, t, 0:t].unsqueeze(3).broadcast_to([128, 2, t, n])
                    x = XL[:, :, t, t:32].unsqueeze(2).broadcast_to([128, 2, t, n])
                    tt(PO, tm, a, x, ALU.mult)
                    z = tt(PO, XL[:, :, 0:t, t:32], XL[:, :, 0:t, t:32], tm, ALU.subtract)
                xw = dma("xw1", io["s_x"][i], XI, z, s1.get(b - 2, {}).get("xrd"), eng=PO)
                s1[b] = {"ga_free": z, "grd": rd, "xw": xw, "bt": bt, "k": k}

            last = {}

            def prep(u):
                b, g, j, i = u // 4, u % 4, u % 2, (u // 4) % 2
                cols = slice(T * b, T * b + T)
                sx = io["s_x"][i].rearrange("(q v u) (l s t) -> q v l s u t", q=4, v=2, l=2, s=32)
                XEu = XE[j].rearrange("p h c n -> p (h c) n")
                for q in range(4):
                    r = slice(32 * q, 32 * q + 32)
                    xr = dma(f"xer{j}", XEu[r, :, 32 * q:32 * q + 32], sx[q, g % 2, g // 2], s1[b]["xw"], last.get(u - 2), zero)
                s1[b]["xrd"] = xr
                for c2 in range(2):
                    bk = banks()
                    for c in range(2):
                        k = T * b + 128 * (2 * c2 + c)
                        t = mm(PS[:, bk, 256 * c:256 * c + 256], XT[:, k:k + 128], wv[:, 256 * g:256 * g + 256],
                               inc=(c == 1))
                    AC.wait(t, last.get(u - 2))
                    t = cp(AC, V[j][:, 2 * c2:2 * c2 + 2, :], PS[:, bk, :].rearrange("p (c n) -> p c n", c=2))
                    free(bk, 1, t)
                    yield
                DV.wait(last.get(u - 2))
                mu = maskU.unsqueeze(1).broadcast_to([128, 2, 128])

                def turned(h, ll):
                    PE.wait(ll, xr)
                    bk = banks()
                    for c in range(4):
                        t = mm(PS[:, bk, 128 * c:128 * c + 128], LN_[j][:, h, c, :], XE[j][:, h, c, :], inc=(c == 3))
                    AC.wait(t)
                    n = cp(AC, LN_[j][:, h], PS[:, bk, :].rearrange("p (c n) -> p c n", c=4))
                    free(bk, 1, n)
                    return n
                ll = None
                for a in range(2):
                    bk = banks()
                    t = mm(PS[:, bk, :], wq[:, 256 * g + 128 * a:256 * g + 128 * a + 128], XT[:, cols], inc=True)
                    AC.wait(t, bd_read[0], zero)
                    cp(AC, QT[j][:, a, :], PS[:, bk, :])
                    for par in range(2):
                        r = slice(64 * par, 64 * par + 64)
                        t = cp(AC, BD[r, 1, par, :], PS[r, bk, :])
                        k = cp(AC, BD[r, 0, par, :], KT[i][r, 2 * g + a, :])
                    free(bk, 1, t)
                    yield
                    if a:
                        turned(0, ll)
                        yield
                        turned(1, ll)
                        yield
                    PE.wait(k)
                    for c in range(4):
                        cc = slice(128 * c, 128 * c + 128)
                        bk = banks()
                        t = bd_read[0] = mm(PS[:, bk, :], KT[i][:, 2 * g + a, cc], BD[:, :, :, cc], inc=True)
                        ps = PS[:, bk, :].rearrange("p (k t n) -> p k t n", k=2, t=2)
                        DV.wait(t)
                        for par in range(2):
                            h = 2 * a + par
                            ll = stt(LN_[j][:, h, c, :], ps[:, 0, par], beta[i][:, 4 * g + h, c:c + 1],
                                     maskL, ALU.mult, ALU.mult)
                        pp = tt(DV, P[j][:, 2 * a:2 * a + 2, c, :], ps[:, 1], mu, ALU.mult)
                        free(bk, 1, pp)
                        yield
                turned(2, ll)
                yield
                n = turned(3, ll)
                ready[u] = [n, pp]

            bd_read = [None]
            ready = {}

            def chain(u):
                b, g, j, i = u // 4, u % 4, u % 2, (u // 4) % 2
                v3 = lambda x: x.rearrange("p (h n) -> p h n", h=4)
                st_ready = None
                PE.wait(ready[u])
                for c in range(4):
                    bcol = bc(beta[i][:, 4 * g:4 * g + 4, c], 64)
                    if c:
                        bk = banks()
                        PE.wait(st_ready)
                        for a in range(2):
                            t = mm(PS[:, bk, 128 * a:128 * a + 128], KT[i][:, 2 * g + a, 128 * c:128 * c + 128],
                                   S[j][:, a, :], inc=(a == 1))
                        DV.wait(t)
                        t = D1(tt(DV, R, V[j][:, c, :], PS[:, bk, 0:256], ALU.subtract))
                        free(bk, 1, t)
                        t = tt(DV, v3(R), v3(R), bcol, ALU.mult)
                    else:
                        t = tt(DV, v3(R), v3(V[j][:, c, :]), bcol, ALU.mult)
                    yield
                    bk = banks()
                    PE.wait(t)
                    for h in range(4):
                        t = mm(PS[:, bk, 64 * h:64 * h + 64], XE[j][:, h, c, :], R[:, 64 * h:64 * h + 64], inc=(h == 3))
                    DV.wait(t)
                    t = cp(DV, A, PS[:, bk, 0:256])
                    free(bk, 1, t)
                    src = A
                    for k in range(3):
                        yield
                        bk = banks()
                        PE.wait(t)
                        for h in range(4):
                            t = mm(PS[:, bk, 64 * h:64 * h + 64], LN_[j][:, h, c, :], src[:, 64 * h:64 * h + 64],
                                   inc=(h == 3))
                        D1(t)
                        t = tt(DV, B, A, PS[:, bk, 0:256], ALU.subtract)
                        free(bk, 1, t)
                        src = B
                    yield
                    PE.wait(t)
                    if c < 3:
                        bk = banks()
                        for h in range(4):
                            par, a = h % 2, h // 2
                            t = mm(PS[64 * par:64 * par + 64, bk, 64 * a:64 * a + 64],
                                   Kn[i][:, c, 64 * (4 * g + h):64 * (4 * g + h) + 64],
                                   B[:, 64 * h:64 * h + 64], inc=(h == 3))
                    bo = banks()
                    for a in range(2):
                        if c:
                            mm(PS[:, bo, 128 * a:128 * a + 128], S[j][:, a, :], QT[j][:, a, 128 * c:128 * c + 128], stop=False)
                        for par in range(2):
                            h = 2 * a + par
                            to = mm(PS[64 * par:64 * par + 64, bo, 128 * a:128 * a + 128], B[:, 64 * h:64 * h + 64],
                                    P[j][:, h, c, :], start=(c == 0), inc=(h == 3))
                    if c < 3:
                        DV.wait(to)
                        for par in range(2):
                            r = slice(64 * par, 64 * par + 64)
                            so = S[j][r, :, 64 * par:64 * par + 64]
                            ps = PS[r, bk, 0:128].rearrange("p (a n) -> p a n", a=2)
                            t = cp(DV, so, ps) if c == 0 else tt(DV, so, so, ps, ALU.add)
                        free(bk, 1, t)
                        st_ready = t
                    AC.wait(to, last.get(u - 1))
                    ot = cp(AC, OT[:, :, 128 * c:128 * c + 128], PS[:, bo, 0:256].rearrange("p (a n) -> p a n", a=2))
                    free(bo, 1, ot)
                    yield
                    D1(t)
                PE.wait(ot)
                bo = banks()
                for k in range(4):
                    for a in range(2):
                        t = mm(PS[:, bo, 128 * k:128 * k + 128], OT[:, a, 128 * k:128 * k + 128], wo[:, 2 * g + a, :],
                               start=(a == 0), stop=(a == 1), inc=(k == 3 and a == 1))
                last[u] = [t, DV.last]
                if g < 3:
                    xb = X[:, 4 * b:4 * b + 4, :]
                    DV.wait(t, x_ready[b], xt_ready[b])
                    t = tt(DV, xb, xb, PS[:, bo, :].rearrange("p (a b) -> p a b", a=4), ALU.add)
                    free(bo, 1, t)
                    x_ready[b] = t
                else:
                    s2[b] = [t, DV.last]
                    residual(b, bo, t)

            def part(gen, n):
                for _ in range(n):
                    if next(gen, StopIteration) is StopIteration:
                        return
                    yield

            def late_turn(b):
                yield
                turn(b)
            first = stage1(0)
            weave((first, 1))
            nxt = stage1(1)
            weave((part(nxt, 20), 1))
            weave((prep(0), 1))
            for u in range(16):
                b, g = u // 4, u % 4
                if g == 0 and b:
                    nxt = stage1(b + 1) if b + 1 < NB else iter(())
                streams = [(chain(u), 26)]
                if u + 1 < 16:
                    streams.append((prep(u + 1), 16))
                if g < 2:
                    streams.append((part(nxt, 18 if g == 0 else 100), 16))
                if g == 1 and b:
                    streams.append((late_turn(b - 1), 4))
                weave(*streams)
            turn(NB - 1)

        def l1_xattn():
            top[0] = 0
            wx, wy, wv, cT = take(128), take(128), take(128), take(NB * TC)
            bxy, bv = take(2), take(128)
            mc, mr = take(8), take(NB * TC)
            for o, i in ((wx, "y_wx"), (wy, "y_wy"), (wv, "y_wv"), (cT, "ctx_T"), (bxy, "y_bxy"), (bv[0:1], "y_bv"),
                         (mc.bitcast(I32), "mask_c"), (mr[0:1].bitcast(I32), "mask_r")):
                l = dma("w4", o, io[i])
            mcf, mrf = take(8).rearrange("p (b c) -> p b c", b=4), take(NB * TC)
            Kp = take(NB * TC)
            Vp = take(NB * 2 * 129).rearrange("p (b c n) -> p b c n", b=4, c=2)
            Qp = [take(512) for _ in range(2)]
            E = [take(1024).rearrange("p (c n) -> p c n", c=2) for _ in range(2)]
            mx = [take(8).rearrange("p (k q) -> p k q", k=2) for _ in range(2)]
            mrow = [take(512) for _ in range(2)]
            rd = take(4)
            sizes = [128, 26]
            scale = float(D) ** -0.5
            DV.wait(l)
            PE.wait(l)
            ts(DV, mcf.rearrange("p b c -> p (b c)"), mc.bitcast(I32), 1.0, ALU.is_equal, -1e30, ALU.mult)
            t = ts(DV, mrf[0:1], mr[0:1].bitcast(I32), 1.0, ALU.is_equal, -1e30, ALU.mult)
            vm = DV.op(lambda e: e.memset(Vp[:, :, :, 128:129], 1.0))
            for k in range(2):
                bk = banks()
                c = slice(308 * k, 308 * k + 308)
                t = mm(PS[:, bk, 0:308], wy, cT[:, c], inc=True)
                DV.wait(t)
                t = ts(DV, Kp[:, c], PS[:, bk, 0:308], bxy[:, 1:2], ALU.add)
                free(bk, 1, t)
            for b in range(NB):
                bk = banks()
                for c in range(2):
                    n = sizes[c]
                    o = PS[0:n, bk, 128 * c:128 * c + 128]
                    mm(o, cT[:, TC * b + 128 * c:TC * b + 128 * c + n], wv, stop=False)
                    t = mm(o, ones[0:1, 0:n], bv[0:1], start=False, inc=True)
                DV.wait(t)
                for c in range(2):
                    n = sizes[c]
                    t = cp(DV, Vp[0:n, b, c, 0:128], PS[0:n, bk, 128 * c:128 * c + 128])
                free(bk, 1, t)
            PE.wait(t, DV.last)
            AC.wait(t)
            r = {}

            def part_a(b):
                i = b % 2
                bk = banks()
                PE.wait(xt_ready[b])
                t = mm(PS[:, bk, :], wx, XT[:, T * b:T * b + T], inc=True)
                DV.wait(t, r.get(b - 2))
                q = ts(DV, Qp[i], PS[:, bk, :], bxy[:, 0:1], ALU.add)
                free(bk, 1, q)
                bk = banks(2)
                PE.wait(q)
                kb = slice(TC * b, TC * b + TC)
                for j in range(4):
                    o = PS[:, bk + j // 2, TC * (j % 2):TC * (j % 2) + TC]
                    mm(o, Qp[i][:, 128 * j:128 * j + 128], Kp[:, kb], stop=False)
                    t = mm(o, ones[0:1, :], mrf[0:1, kb], start=False, inc=(j == 3))
                DV.wait(t)
                t = D1(red(mx[i][:, 0, :].rearrange("p (a q) -> p a q", a=2),
                           PS[:, bk:bk + 2, 0:2 * TC].rearrange("p a (q n) -> p a q n", q=2), ALU.max))
                free(bk, 2, t)
                t = ts(DV, mx[i][:, 1, :], mx[i][:, 0, :], -1.0, ALU.mult)
                bk = banks()
                PE.wait(t)
                for j in range(4):
                    t = mm(PS[0:1, bk, 128 * j:128 * j + 128], mx[i][:, 1, j:j + 1], ident[:], inc=(j == 3))
                D1(t)
                t = cp(DV, mrow[i][0:1], PS[0:1, bk, :])
                free(bk, 1, t)
                return t

            def part_b(b, ready):
                i = b % 2
                bk = banks(2)
                PE.wait(ready)
                for c in range(2):
                    n = sizes[c]
                    mm(PS[0:n, bk + c, :], Kp[:, TC * b + 128 * c:TC * b + 128 * c + n], Qp[i], stop=False)
                    t = mm(PS[0:n, bk + c, :], ones[0:1, 0:n], mrow[i][0:1], start=False, inc=True)
                AC.wait(t, r.get(b - 2))
                for c in range(2):
                    n = sizes[c]
                    t = act(E[i][0:n, c, :], PS[0:n, bk + c, :], ACT.Exp, scale=scale, bias=mcf[0:n, b, c:c + 1])
                free(bk, 2, t)
                bk = banks(2)
                PE.wait(t)
                for j in range(4):
                    for c in range(2):
                        n = sizes[c]
                        t = mm(PS[:, bk + j // 2, 129 * (j % 2):129 * (j % 2) + 129], E[i][0:n, c, 128 * j:128 * j + 128],
                               Vp[0:n, b, c, :], start=(c == 0), stop=(c == 1), inc=(j == 3 and c == 1))
                r[b] = t
                DV.wait(t, x_ready[b], xt_ready[b])
                den = PS[:, bk:bk + 2, 0:258].rearrange("p a (q n) -> p a q n", q=2)[:, :, :, 128]
                D1(recip(rd.rearrange("p (a q) -> p a q", a=2), den))
                for j in range(4):
                    t = stt(X[:, 4 * b + j, :], PS[:, bk + j // 2, 129 * (j % 2):129 * (j % 2) + 128], rd[:, j:j + 1],
                            X[:, 4 * b + j, :], ALU.mult, ALU.add)
                free(bk, 2, t)
                D1(t)
                x_ready[b] = normalize(X[:, 4 * b:4 * b + 4, :], 1e-5)
            t = part_a(0)
            for b in range(NB):
                nt = part_a(b + 1) if b + 1 < NB else None
                part_b(b, t)
                t = nt
                if b:
                    turn(b - 1)
            turn(NB - 1)

        def l1_ffn():
            top[0] = 0
            w1 = take(4096).rearrange("p (e n) -> p e n", e=8)
            b1, wo, rw = take(512), take(512).rearrange("p (a n) -> p a n", a=4), take(8)
            bo, gb, iota = take(128), take(256), take(16)
            sel = take(1024)
            for o, i in ((w1, "f_w1"), (b1[0:8], "f_b1"), (wo, "f_wo"), (rw, "f_rw"), (bo[0:1], "f_bo"),
                         (gb[0:1], "f_gb"), (iota, "iota16"), (sel[0:8], "sel8")):
                l = dma("w5", o, io[i])
            sel16 = take(512, F16).rearrange("p (e n) -> p e n", e=8)
            gam = take(256)
            lg = take(32).rearrange("p (a n) -> p a n", a=4)
            m8, i8 = take(32).rearrange("p (a n) -> p a n", a=4), take(32).rearrange("p (a n) -> p a n", a=4).bitcast(U32)
            ixf = take(8).rearrange("p (a n) -> p a n", a=4)
            oh = take(32).rearrange("p (a n) -> p a n", a=4)
            MT = [take(512) for _ in range(2)]
            M16 = [take(256, F16) for _ in range(2)]
            XM = [take(4096).rearrange("p (e n) -> p e n", e=8) for _ in range(2)]
            HT = [take(2048).rearrange("p (a n) -> p a n", a=4) for _ in range(2)]
            DV.wait(l)
            PE.wait(l)
            cp(DV, sel16[0:8], sel[0:8].rearrange("p (e n) -> p e n", e=8))
            bk = banks()
            t = mm(PS[:, bk, 0:256], ones[0:1, :], gb[0:1], inc=True)
            DV.wait(t)
            t = cp(DV, gam, PS[:, bk, 0:256])
            free(bk, 1, t)
            D1(t)
            g3 = gam[:, 0:128].unsqueeze(1).broadcast_to([128, 4, 128])
            b3 = gam[:, 128:256].unsqueeze(1).broadcast_to([128, 4, 128])
            iob = iota[:, 0:8].unsqueeze(1).broadcast_to([128, 4, 8])
            xm_free, ht_free = {}, {}

            def route(b):
                i = b % 2
                bk = banks()
                PE.wait(xt_ready[b])
                for j in range(4):
                    t = mm(PS[:, bk, 8 * j:8 * j + 8], XT[:, T * b + 128 * j:T * b + 128 * j + 128], rw, inc=(j == 3))
                D1(t)
                t = D1(cp(DV, lg, PS[:, bk, 0:32].rearrange("p (a n) -> p a n", a=4)))
                free(bk, 1, t)
                pick(b, lg, 8, m8, i8, ixf)
                t = D1(tt(DV, oh, iob, bc(ixf[:, :, 0], 8), ALU.is_equal))
                bk = banks()
                PE.wait(t)
                for j in range(4):
                    t = tr(PS[0:8, bk, 128 * j:128 * j + 128], oh[:, j, :], j == 3)
                DV.wait(t, xm_free.get(i))
                cp(DV, MT[i][0:8], PS[0:8, bk, :])
                m = cp(DV, M16[i][0:8], PS[0:8, bk, :])
                free(bk, 1, m)
                PE.wait(m)
                for e in range(8):
                    bk = banks()
                    t = mm(PS[:, bk, :], sel16[0:8, e, :], M16[i][0:8], inc=True)
                    DV.wait(t)
                    t = tt(DV, XM[i][:, e, :], XT[:, T * b:T * b + T], PS[:, bk, :], ALU.mult)
                    free(bk, 1, t)
                return t

            def hidden(b, ready):
                i = b % 2
                PE.wait(ready)
                for a in range(4):
                    bk = banks()
                    c = slice(128 * a, 128 * a + 128)
                    for e in range(8):
                        mm(PS[:, bk, :], w1[:, e, c], XM[i][:, e, :], start=(e == 0), stop=False)
                    t = mm(PS[:, bk, :], b1[0:8, c], MT[i][0:8], start=False, inc=True)
                    AC.wait(t, ht_free.get(i))
                    h = act(HT[i][:, a, :], PS[:, bk, :], ACT.Gelu)
                    free(bk, 1, h)
                xm_free[i] = t
                return h

            def out(b, ready):
                i = b % 2
                bk = banks()
                PE.wait(ready)
                for j in range(4):
                    o = PS[:, bk, 128 * j:128 * j + 128]
                    for a in range(4):
                        mm(o, HT[i][:, a, 128 * j:128 * j + 128], wo[:, a, :], start=(a == 0), stop=False)
                    t = mm(o, ones[0:1, :], bo[0:1], start=False, inc=(j == 3))
                ht_free[i] = t
                xb = X[:, 4 * b:4 * b + 4, :]
                Y = XM[i].rearrange("p e n -> p (e n)")[:, 0:512].rearrange("p (a n) -> p a n", a=4)
                DV.wait(t, x_ready[b])
                t = D1(tt(DV, Y, xb, PS[:, bk, :].rearrange("p (a b) -> p a b", a=4), ALU.add))
                free(bk, 1, t)
                normalize(Y, 1e-12)
                D1(tt(DV, Y, Y, g3, ALU.mult))
                D1(tt(DV, Y, Y, b3, ALU.add))
                D1(tt(DV, xb, xb, Y, ALU.add))
                t = normalize(xb, 1e-5)
                xm_free[i] = t
                x_ready[b] = t
            t = route(0)
            for b in range(NB):
                nt = route(b + 1) if b + 1 < NB else None
                h = hidden(b, t)
                out(b, h)
                t = nt

        for f in (l0_attn, l0_xattn, l0_ffn, l1_attn, l1_xattn, l1_ffn)[:phases]:
            f()
            barrier()

        o = dma("out", io["out"], X[:])
        SP.wait(o)

        block = ctx.enter_context(nc.Block())

        @block.tensor
        def _(e):
            for f in PE.q:
                f(e)

        @block.vector
        def _(e):
            for f in DV.q:
                f(e)

        @block.scalar
        def _(e):
            for f in AC.q:
                f(e)

        @block.gpsimd
        def _(e):
            for f in PO.q:
                f(e)

        @block.sync
        def _(e):
            for f in SP.q:
                f(e)


OUTS = ["out"]
SCRATCH = {"s_g": ([128, 2048], F32), "s_x": ([2, 128, 2048], F32), "s_xq": ([2, 2, 128, 2, 512], F16), "s_xk": ([2, 2, 128, 2, 666], F16), "s_xm": ([4, 512], F16),
           "s_qk0": ([2, 2, 128, 512], F16), "s_m0": ([16, 512], F16)}
PHASES = 6


def kernel(**inputs):
    import concourse.bacc as bacc
    from concourse.bass_utils import run_bass_kernel_spmd

    a = {k: np.asarray(v) for k, v in inputs.items()}
    x = a["x"].reshape(NB * T, D)
    arrays = {
        "x_tm": x.reshape(NT, 128, D).transpose(1, 0, 2),
        "x_T": x.T,
        "ident": np.eye(128, dtype=np.float32),
        "qkv_w": a["L0_attn_qkv_weight"].T,
        "qkv_m": a["L0_attn_qkv_weight_mask"].T,
        "ow": a["L0_attn_out_weight"].T,
        "om": a["L0_attn_out_weight_mask"].T,
        "ob": a["L0_attn_out_bias"][None],
        "obm": a["L0_attn_out_bias_mask"][None],
    }
    ctx_pad = np.zeros((NB, 256, D), np.float32)
    ctx_pad[:, :TC] = a["ctx_1024"]
    sel = np.zeros((16, 8, 2, 64), np.float32)
    for h in range(16):
        sel[h, h // 2, h % 2] = 1.0
    arrays |= {
        "ctx_tm": ctx_pad.reshape(8, 128, D).transpose(1, 0, 2),
        "x_wq": a["L0_xattn_Wq"],
        "x_wk": a["L0_xattn_Wkv"][:, :1024],
        "x_wv": a["L0_xattn_Wkv"][:, 1024:],
        "x_wo": a["L0_xattn_Wo"].reshape(8, 128, D).transpose(1, 0, 2),
        "x_ln": np.stack([a["L0_xattn_ln1_g"], a["L0_xattn_ln1_b"], a["L0_xattn_ln2_g"], a["L0_xattn_ln2_b"]], 1),
        "sel16": sel.reshape(16, 8, 128),
        "zeros": np.zeros((8, 512), np.float16),
        "ones16": np.ones((8, 512), np.float16),
    }
    def experts(w):
        return w.transpose(1, 0, 2).reshape(D, -1)
    down = np.concatenate([a["L0_ffn_down_proj"].reshape(8, 128, D), a["L0_ffn_sh_down"].T[None]])
    mask = np.zeros((NB, 256), np.int32)
    mask[:, :TC] = a["mask_BxS2_ik1"]
    ii = np.arange(128)
    arrays |= {
        "m_up": experts(a["L0_ffn_up_proj"]),
        "m_gate": experts(a["L0_ffn_gate_proj"]),
        "m_down": down.transpose(1, 0, 2),
        "m_sg": a["L0_ffn_sh_gate"].T,
        "m_su": a["L0_ffn_sh_up"].T,
        "m_rw": a["L0_ffn_router_w"].T,
        "m_rb": a["L0_ffn_router_bias"][None],
        "iota16": np.tile(np.arange(16, dtype=np.float32), (128, 1)),
        "d_wq": a["L1_attn_Wq"],
        "d_wk": a["L1_attn_Wk"],
        "d_wv": a["L1_attn_Wv"],
        "d_wo": a["L1_attn_Wout"].reshape(8, 128, D).transpose(1, 0, 2),
        "d_wb": a["L1_attn_Wbeta"],
        "d_bb": a["L1_attn_b_beta"][None],
        "mask_l": (ii[None, :] // 32 < ii[:, None] // 32).astype(np.float32),
        "mask_u": (ii[:, None] <= ii[None, :]).astype(np.float32),
        "eye32": np.tile(np.eye(32, dtype=np.float32).reshape(1, 1024), (128, 1)),
        "y_wx": a["L1_xattn_Wx"].T,
        "y_wy": a["L1_xattn_Wy"].T,
        "y_wv": a["L1_xattn_Wv"].T,
        "ctx_T": a["ctx_1024"].reshape(NB * TC, D).T,
        "y_bxy": np.stack([a["L1_xattn_bx"], a["L1_xattn_by"]], 1),
        "y_bv": a["L1_xattn_bv"][None],
        "mask_c": mask.reshape(8, 128).T,
        "mask_r": a["mask_BxS2_ik1"].reshape(1, NB * TC),
        "f_w1": a["L1_ffn_W1"].transpose(1, 0, 2),
        "f_b1": a["L1_ffn_b1"],
        "f_wo": a["L1_ffn_Wo"].reshape(4, 128, D).transpose(1, 0, 2),
        "f_rw": a["L1_ffn_Wr"].T,
        "f_bo": a["L1_ffn_bo"][None],
        "f_gb": np.concatenate([a["L1_ffn_gamma"], a["L1_ffn_beta"]])[None],
        "sel8": np.repeat(np.eye(8, dtype=np.float32), 128, axis=1),
    }
    arrays = {k: np.ascontiguousarray(v) for k, v in arrays.items()}
    nc = bacc.Bacc("TRN2", target_bir_lowering=False, num_devices=1)
    io = {k: nc.dram_tensor(k, v.shape, mybir.dt.from_np(v.dtype), kind="ExternalInput").ap()
          for k, v in arrays.items()}
    io["out"] = nc.dram_tensor("out", [128, NT, 128], F32, kind="ExternalOutput").ap()
    for k, (shape, dt) in SCRATCH.items():
        io[k] = nc.dram_tensor(k, shape, dt).ap()
    build(nc, io, PHASES)
    r = run_bass_kernel_spmd(nc, [arrays], core_ids=[0])
    out = r.results[0]["out"]
    return np.ascontiguousarray(out.transpose(1, 0, 2)).reshape(NB, T, D)
```

```python
from contextlib import ExitStack

import numpy as np
import concourse.bass as bass
from concourse import mybir

F32 = mybir.dt.float32
F16 = mybir.dt.float16
I32 = mybir.dt.int32
U32 = mybir.dt.uint32
ALU = mybir.AluOpType
ACT = mybir.ActivationFunctionType
AX = mybir.AxisListType.X

NB, T, D, TC = 4, 512, 128, 154
SEL = 1024.0
NT = NB * T // 128
ARENA = 48128


class Eng:

    def __init__(self, name, sem):
        self.name, self.sem, self.q, self.n, self.seen = name, sem, [], 0, {}

    def wait(self, *tokens):
        for t in tokens:
            if t is None:
                continue
            if isinstance(t, list):
                self.wait(*t)
                continue
            sem, v = t
            if self.seen.get(id(sem), 0) < v:
                self.seen[id(sem)] = v
                self.q.append(lambda e, sem=sem, v=v: e.wait_ge(sem, v))

    def op(self, f, inc=True):
        if self.name == "pool":
            self.wait(self.last)
        if inc:
            self.n += 1
            self.q.append(lambda e: f(e).then_inc(self.sem, 1))
        else:
            self.q.append(f)
        return (self.sem, self.n)

    @property
    def last(self):
        return (self.sem, self.n)


def build(nc, io, phases=6):
    with ExitStack() as ctx:
        def sb(name, shape, dt):
            return ctx.enter_context(nc.sbuf_tensor("sb_" + name, shape, dt))

        def sem(name):
            return ctx.enter_context(nc.semaphore(name))

        PE, DV, AC, PO = (Eng(n, sem("s_" + n)) for n in ("pe", "dve", "act", "pool"))
        SP = Eng("sp", sem("s_sp"))
        compute = (PE, DV, AC, PO)

        arena = sb("arena", [128, ARENA], F32)
        top = [0]

        def take(words, dt=F32):
            a = arena[:, top[0]:top[0] + words]
            top[0] += words
            assert top[0] <= ARENA, top[0]
            return a if dt == F32 else a.bitcast(dt)

        PS = ctx.enter_context(nc.psum_tensor("ps", [128, 8, 512], F32))
        RING = 6
        ptr = [0]
        freed = [None] * 8

        def banks(n=1):
            if ptr[0] + n > RING:
                ptr[0] = 0
            b = ptr[0]
            ptr[0] = (b + n) % RING
            assert "taken" not in freed[b:b + n]
            PE.wait(*freed[b:b + n])
            freed[b:b + n] = ["taken"] * n
            return b

        def free(b, n, *tokens):
            for i in range(b, b + n):
                freed[i] = list(tokens)

        dma_sems = {}

        def dma(group, out, in_, *waits, eng=None):
            eng = eng or SP
            if group not in dma_sems:
                dma_sems[group] = [sem("d_" + group), 0]
            s = dma_sems[group]
            s[1] += 16
            eng.wait(*waits)
            eng.q.append(lambda e: e.dma_start(out, in_).then_inc(s[0], 16))
            return (s[0], s[1])

        def barrier():
            tokens = [e.last for e in compute] + [(s[0], s[1]) for s in dma_sems.values()]
            for e in compute + (SP,):
                e.wait(*tokens)
            for i in range(8):
                if freed[i] != "taken":
                    freed[i] = None

        def mm(out, lhsT, rhs, start=True, stop=True, inc=False):
            return PE.op(lambda e: e.matmul(out, lhsT, rhs, start=start, stop=stop,
                                            skip_group_check=True), inc)

        def tr(out, a, inc=False):
            return PE.op(lambda e: e.transpose(out, a, ident[:]), inc)

        def tt(eng, out, a, b, op):
            return eng.op(lambda e: e.tensor_tensor(out, a, b, op))

        def ts(eng, out, a, s1, op0, s2=None, op1=None):
            if op1 is None:
                return eng.op(lambda e: e.tensor_scalar(out, a, s1, None, op0))
            return eng.op(lambda e: e.tensor_scalar(out, a, s1, s2, op0, op1))

        def stt(out, a, s, b, op0, op1):
            return DV.op(lambda e: e.scalar_tensor_tensor(out=out, in0=a, scalar=s, in1=b, op0=op0, op1=op1))

        def cp(eng, out, a):
            if eng is AC:
                return AC.op(lambda e: e.activation(out, a, ACT.Copy))
            return eng.op(lambda e: e.tensor_copy(out, a))

        def act(out, a, f, scale=1.0, bias=0.0):
            return AC.op(lambda e: e.activation(out, a, f, scale=scale, bias=bias))

        def red(out, a, op):
            return DV.op(lambda e: e.tensor_reduce(out, a, AX, op))

        def memset(eng, out, v):
            return eng.op(lambda e: e.memset(out, v))

        def recip(out, a):
            return DV.op(lambda e: e.reciprocal(out, a))

        def D1(tok):
            DV.wait(tok)
            return tok

        def weave(*streams):
            live = [[g, n, 0] for g, n in streams]
            while live:
                s = min(live, key=lambda s: (s[2] + 1) / s[1])
                s[2] += 1
                if next(s[0], StopIteration) is StopIteration:
                    live.remove(s)

        X = sb("X", [128, NT, 128], F32)
        XT = sb("XT", [128, NB * T], F32)
        ident = sb("ident", [128, 128], F32)
        ident16 = sb("ident16", [128, 128], F16)
        ones = sb("ones", [128, 128], F32)
        sq = sb("sq", [128, 4, 128], F32)
        st = sb("st", [128, 14, 4], F32)
        magic = 0x5F3759DF

        x_ready, xt_ready = [], []

        def load_x():
            for b in range(NB):
                xt_ready.append(dma(f"cx{b}", XT[:, T * b:T * b + T], io["x_T"][:, T * b:T * b + T]))
            i = dma("ci", ident[:], io["ident"])
            x_ready.extend([dma("c", X[:], io["x_tm"])] * NB)
            DV.op(lambda e: e.memset(ones[:], 1.0))
            DV.wait(i)
            base = cp(DV, ident16[:], ident[:])
            PE.wait(i, base)

        def rsqrt(v, y, a, b):
            D1(DV.op(lambda e: e.tensor_scalar(a.bitcast(I32), v.bitcast(I32), 1, None,
                                               ALU.logical_shift_right)))
            D1(DV.op(lambda e: e.tensor_scalar(y.bitcast(I32), a.bitcast(I32), -1.0, float(magic),
                                               ALU.mult, ALU.add)))
            for _ in range(3):
                D1(tt(DV, a, y, y, ALU.mult))
                D1(stt(b, a, -0.5, v, ALU.mult, ALU.mult))
                t = D1(stt(y, b, 1.5, y, ALU.add, ALU.mult))
            return t

        def bc(a, n):
            return a.unsqueeze(2).broadcast_to([a.shape[0], a.shape[1], n])

        def normalize_steps(x, eps, out=None, k=0):
            out = x if out is None else out
            D1(red(st[:, k, :], x, ALU.add))
            D1(ts(DV, st[:, k + 1, :], st[:, k, :], 1.0 / D, ALU.mult))
            D1(tt(DV, out, x, bc(st[:, k + 1, :], D), ALU.subtract))
            yield
            D1(tt(DV, sq[:], out, out, ALU.mult))
            D1(red(st[:, k + 2, :], sq[:], ALU.add))
            yield
            D1(ts(DV, st[:, k + 3, :], st[:, k + 2, :], 1.0 / D, ALU.mult, eps, ALU.add))
            rsqrt(st[:, k + 3, :], st[:, k + 4, :], st[:, k + 5, :], st[:, k + 6, :])
            yield
            return D1(tt(DV, out, out, bc(st[:, k + 4, :], D), ALU.mult))

        def normalize(x, eps, out=None):
            steps = normalize_steps(x, eps, out)
            while True:
                try:
                    next(steps)
                except StopIteration as end:
                    return end.value

        def transpose4(src, ready):
            b = banks()
            PE.wait(ready)
            for j in range(4):
                t = tr(PS[:, b, 128 * j:128 * j + 128], src[:, j, :], j == 3)
            return b, t

        def residual(b, ps, ps_ready, eps=1e-5):
            add(b, ps, ps_ready)
            x_ready[b] = normalize(X[:, 4 * b:4 * b + 4, :], eps)

        def residual_steps(b, ps, ps_ready):
            add(b, ps, ps_ready)
            x_ready[b] = yield from normalize_steps(X[:, 4 * b:4 * b + 4, :], 1e-5)

        def add(b, ps, ps_ready):
            xb = X[:, 4 * b:4 * b + 4, :]
            DV.wait(ps_ready, x_ready[b], xt_ready[b])
            t = D1(tt(DV, xb, xb, PS[:, ps, :].rearrange("p (a b) -> p a b", a=4), ALU.add))
            free(ps, 1, t)

        def turn(b):
            tb, t2 = transpose4(X[:, 4 * b:4 * b + 4, :], x_ready[b])
            AC.wait(t2)
            t3 = cp(AC, XT[:, T * b:T * b + T], PS[:, tb, :])
            free(tb, 1, t3)
            xt_ready[b] = t3

        def l0_attn(cross):
            top[0] = 9324
            w = take(384)
            wm = take(384)
            wo = take(128)
            wom = take(128)
            bo = take(128)
            bom = take(128)
            for o, i in ((w, "qkv_w"), (wm, "qkv_m"), (wo, "ow"), (wom, "om"), (bo[0:1], "ob"), (bom[0:1], "obm")):
                l = dma("w0", o, io[i])
            load_x()
            DV.wait(l)
            gate = 1.5 * 2.0 ** -24
            D1(ts(DV, wm, wm, gate, ALU.is_gt))
            D1(ts(DV, wom, wom, gate, ALU.is_gt))
            D1(ts(DV, bom[0:1], bom[0:1], gate, ALU.is_gt))
            tt(DV, w, w, wm, ALU.mult)
            tt(DV, wo, wo, wom, ALU.mult)
            wr = D1(tt(DV, bo[0:1], bo[0:1], bom[0:1], ALU.mult))
            H = [take(256, F16) for _ in range(2)]
            L = [take(256, F16) for _ in range(2)]
            QS32, KS32, VP32 = [[take(n) for _ in range(2)] for n in (4096, 2048, 3072)]
            QS = [t.bitcast(F16).rearrange("p (t h n) -> p t h n", t=2, h=8) for t in QS32]
            KS = [t.bitcast(F16).rearrange("p (h n) -> p h n", h=8) for t in KS32]
            VP = [t.bitcast(F16).rearrange("p (c g h x) -> p (c g) h x", c=4, g=4, h=4) for t in VP32]
            E = [take(1024).rearrange("p (c n) -> p c n", c=2) for _ in range(4)]
            EH, EL = [[take(1024, F16).rearrange("p (c n) -> p c n", c=4) for _ in range(3)] for _ in range(2)]
            rec, dn = take(512), take(512)
            oT = [take(512) for _ in range(2)]
            mx = take(64).rearrange("p (q h) -> p q h", q=4)
            mneg = take(32, F16).rearrange("p (q h) -> p q h", q=4)
            mrow = take(256, F16)
            zeros = []

            def clear(i):
                memset(PO, KS32[i], 0.0)
                k = PO.last
                memset(DV, QS32[i][:, 0:2048], 0.0)
                DV.wait(memset(DV, VP32[i], 0.0))
                for r in (32, 96):
                    o = dma("a0o", KS[i][r:r + 1], io["ones16"].unsqueeze(0), k)
                memset(PO, QS32[i][:, 2048:], 0.0)
                for h in range(4):
                    memset(DV, VP[i][:, :, h, 64 + 8 * h:72 + 8 * h], 1.0)
                zeros.append([DV.last, PO.last, o])
            clear(0)
            scr_qk, scr_m = io["s_qk0"], io["s_m0"]
            pv_done = {}
            oT_free = {}
            E_free = {}
            er_free, e_n, dn_free = {}, [0], [None]
            prep = {}

            def part_a(b):
                i = b % 2
                cols = slice(T * b, T * b + T)
                PE.wait(wr, xt_ready[b])
                bq = banks(2)
                for k in range(2):
                    t = mm(PS[:, bq + k, :], w[:, 128 * k:128 * k + 128], XT[:, cols], inc=True)
                bv = banks()
                for c in range(4):
                    tv = mm(PS[:, bv, 128 * c:128 * c + 128], XT[:, T * b + 128 * c:T * b + 128 * c + 128],
                            w[:, 256:384], inc=(c == 3))
                prev = prep.get(b - 1, {})
                zero = zeros[i]
                AC.wait(t, prev.get("scr"))
                for k in range(2):
                    h = cp(AC, H[k], PS[:, bq + k, :])
                DV.wait(h, t, prev.get("scr"))
                for k in range(2):
                    lo = tt(DV, L[k], PS[:, bq + k, :], H[k], ALU.subtract)
                free(bq, 2, lo, h)
                for k in range(2):
                    dma("a0w", scr_qk[k, 0], H[k], h, prev.get("rd"))
                    wrt = dma("a0w", scr_qk[k, 1], L[k], lo)
                done = pv_done.get(b - 2)
                rds = {}
                for par in range(2):
                    p0 = 64 * par
                    if b > 1:
                        dma("a0r", QS[i][p0 + 32:p0 + 33, par], io["zeros"].unsqueeze(0), done)
                    src = scr_qk.rearrange("k s (h t d) n -> k s t d h n", t=2, d=8)
                    q, n = (AC, "a0s") if b == 0 and par else (SP, "a0r")
                    for r in range(4):
                        rds[n] = dma(n, QS[i][p0 + 8 * r:p0 + 8 * r + 8, par], src[0, r // 2, par], wrt, done, zero, eng=q)
                        rds[n] = dma(n, KS[i][p0 + 8 * r:p0 + 8 * r + 8], src[1, r % 2, par], eng=q)
                rd = list(rds.values())
                DV.wait(tv, done, zero)
                src = PS[:, bv, :].rearrange("p (k h d) -> p k h d", h=4, d=8)
                for h in range(4):
                    vt = cp(DV, VP[i][:, :, h, 8 * h:8 * h + 8], src[:, :, h])
                D1(vt)
                for h in range(4):
                    vt = tt(DV, VP[i][:, :, h, 32 + 8 * h:40 + 8 * h], src[:, :, h], VP[i][:, :, h, 8 * h:8 * h + 8],
                            ALU.subtract)
                free(bv, 1, vt)
                if b == 0:
                    clear(1)
                    next(cross)
                for k in range(4):
                    yield
                    if k == 1 and b > 1:
                        yield from part_c(b - 2)
                PE.wait(rd)
                for h in range(16):
                    par, hp = h % 2, h // 2
                    if h == 3 and b > 1:
                        turn(b - 2)
                    for q2 in range(2):
                        yield
                        bb = banks(2)
                        for q in range(2):
                            qt = 2 * q2 + q
                            t = mm(PS[:, bb + q, :], QS[i][:, par, hp, 128 * qt:128 * qt + 128], KS[i][:, hp, :],
                                   inc=(q == 1))
                        DV.wait(t)
                        r = red(mx[:, 2 * q2:2 * q2 + 2, 8 * par + hp], PS[:, bb:bb + 2, :], ALU.max)
                        free(bb, 2, r)
                D1(r)
                DV.wait(prev.get("mt"))
                mt = ts(DV, mneg, mx, -1.0, ALU.mult)
                yield
                bm = banks()
                PE.wait(mt)
                for qt in range(4):
                    t = mm(PS[0:16, bm, 128 * qt:128 * qt + 128], mneg[:, qt, :], ident16[:], inc=(qt == 3))
                AC.wait(t, prev.get("mscr"))
                c = cp(AC, mrow[0:16], PS[0:16, bm, :])
                free(bm, 1, c)
                mw = dma("a0m", scr_m, mrow[0:16], c, prev.get("mrd"))
                for par in range(2):
                    m = dma("a0mr", QS[i][64 * par + 32:64 * par + 33, par], scr_m[8 * par:8 * par + 8].unsqueeze(0), mw, r)
                prep[b] = {"scr": wrt, "rd": rd, "mt": t, "mscr": mw, "mrd": m, "vt": vt}

            def part_b(b):
                i = b % 2
                PE.wait(prep[b]["mrd"], prep[b]["vt"], zeros[i])
                pend = []

                def pv(h, ej, split, half):
                    g, acc = h // 4, 6 + h // 4 % 2
                    PE.wait(split[half])
                    if h % 4 == 0 and half == 0:
                        PE.wait(freed[acc])
                    for c in range(2 * half, 2 * half + 2):
                        lv = VP[i][:, 4 * c + g, h % 4]
                        mm(PS[0:96, acc, :], lv, EH[ej][:, c, :], start=(h % 4 == 0 and c == 0), stop=False)
                        t = mm(PS[0:96, acc, :], lv, EL[ej][:, c, :], start=False, stop=(h % 4 == 3 and c == 3),
                               inc=(c == 3))
                    if half == 0:
                        return
                    E_free[ej] = t
                    if h % 4 == 3:
                        r = slice(32 * g, 32 * g + 32)
                        AC.wait(t, dn_free[0])
                        d = cp(AC, dn[r], PS[64:96, acc, :])
                        DV.wait(t, d, oT_free.get(i))
                        o = D1(cp(DV, oT[i][r], PS[32:64, acc, :]))
                        o = tt(DV, oT[i][r], PS[0:32, acc, :], oT[i][r], ALU.add)
                        free(acc, 1, d, o)
                        pv_done[b] = [t, d, o]
                lows, splits = [], [None, None]

                def low(x):
                    h, ej, er, c2, hi, token = x
                    c = slice(2 * c2, 2 * c2 + 2)
                    eng = PO if c2 == 0 else DV
                    eng.wait(hi, E_free.get((ej, h)))
                    if b == NB - 1 and c2:
                        D1(cp(DV, EH[ej][:, c, :], E[er]))
                    token[0] = tt(eng, EL[ej][:, c, :], E[er], EH[ej][:, c, :], ALU.subtract)
                for h in range(16):
                    par, hp = h % 2, h // 2
                    ej = (16 * b + h) % 3
                    E_free[ej, h] = E_free.get(ej)
                    for c2 in range(2):
                        er = e_n[0] % 4
                        e_n[0] += 1
                        bb = banks(2)
                        for c in range(2):
                            kc = 2 * c2 + c
                            t = mm(PS[:, bb + c, :], KS[i][:, hp, 128 * kc:128 * kc + 128], QS[i][:, par, hp, :],
                                   inc=(c == 1))
                        AC.wait(t, er_free.get(er))
                        ex = act(E[er], PS[:, bb:bb + 2, :], ACT.Exp, scale=float(D) ** -0.5)
                        free(bb, 2, ex)
                        AC.wait(ex, E_free.get(ej))
                        c = slice(2 * c2, 2 * c2 + 2)
                        hi = ex if b == NB - 1 and c2 else cp(AC, EH[ej][:, c, :], E[er])
                        low(lows.pop(0)) if lows else None
                        split = er_free[er] = [None]
                        lows.append((h, ej, er, c2, hi, split))
                        if pend:
                            pv(*pend[0], c2)
                        yield
                        splits[c2] = split
                    pend = [(h, ej, list(splits))]
                low(lows.pop(0))
                pv(*pend[0], 0)
                pv(*pend[0], 1)
                yield
                t, d, o = pv_done[b]
                pv_done[b] = t
                DV.wait(d, o)
                D1(recip(rec, dn))
                po = dn_free[0] = D1(tt(DV, oT[i], oT[i], rec, ALU.mult))
                outs[b] = (po, i)

            def part_c(b):
                po, i = outs[b]
                bo_ = banks()
                PE.wait(po)
                for j in range(4):
                    o = PS[:, bo_, 128 * j:128 * j + 128]
                    mm(o, oT[i][:, 128 * j:128 * j + 128], wo, stop=False)
                    t = mm(o, ones[0:1, :], bo[0:1], start=False, inc=(j == 3))
                oT_free[i] = t
                yield from residual_steps(b, bo_, t)

            outs = {}

            def stream_a(b):
                if b < NB:
                    yield from part_a(b)
                else:
                    yield
                    yield
                    yield from part_c(b - 2)
                    yield from latents[0]
                    turn(b - 2)
                    yield from latents[1]
            weave((stream_a(0), 1))
            for b in range(NB):
                if b + 1 == NB:
                    latents = next(cross)
                weave((stream_a(b + 1), 40 if b + 1 < NB else 33), (part_b(b), 33))

            def tail():
                yield from part_c(NB - 1)
                for _ in range(3):
                    yield
                turn(NB - 1)
            return tail()

        def l0_xattn():
            keep, top[0] = top[0], 0
            NK = TC + T
            sizes = [128] * 5 + [26]
            wq, wk, wv, wo = take(1024), take(1024), take(1024), take(1024).rearrange("p (a n) -> p a n", a=8)
            ln = take(4)
            sel = take(1024)[:, 0:512].bitcast(F16).rearrange("p (a n) -> p a n", a=8)
            KV = take(NB * NK).rearrange("p (b n) -> p b n", b=NB)
            CX = take(1024).rearrange("p (a n) -> p a n", a=8)
            LX = take(512).rearrange("p (a n) -> p a n", a=4)
            assert top[0] == 9324
            top[0] = keep
            for o, i in ((wq, "x_wq"), (wk, "x_wk"), (wv, "x_wv"), (wo, "x_wo"), (ln, "x_ln"), (CX, "ctx_tm"),
                         (sel[0:112], "sel16")):
                l = dma("w1", o, io[i])
            kv_ready = {}

            def context():
                DV.wait(l)
                PE.wait(l)
                for half in range(2):
                    t = yield from normalize_steps(CX[:, 4 * half:4 * half + 4, :], 1e-5)
                    for _ in range(2):
                        yield
                    tb, t = transpose4(CX[:, 4 * half:4 * half + 4, :], t)
                    DV.wait(t)
                    for j in range(2):
                        k = ts(DV, KV[:, 2 * half + j, 0:TC], PS[:, tb, 256 * j:256 * j + TC], ln[:, 0:1], ALU.mult,
                               ln[:, 1:2], ALU.add)
                    free(tb, 1, k)

            def latents(b):
                DV.wait(x_ready[b], lx_free[0])
                t = yield from normalize_steps(X[:, 4 * b:4 * b + 4, :], 1e-5, LX)
                for _ in range(2):
                    yield
                tb, t = transpose4(LX, t)
                lx_free[0] = t
                DV.wait(t)
                k = ts(DV, KV[:, b, TC:], PS[:, tb, :], ln[:, 2:3], ALU.mult, ln[:, 3:4], ALU.add)
                free(tb, 1, k)
                kv_ready[b] = k

            lx_free = [None]

            yield

            def first():
                yield from context()
                yield from latents(0)

            def second():
                yield from latents(1)
                yield from latents(2)
            yield first(), second()
            top[0] = 9324
            OT = [take(4096).rearrange("p (a n) -> p a n", a=8) for _ in range(2)]
            den = [take(512) for _ in range(2)]
            rden, rpart = take(512), take(256, F16)
            Hq, Lq = [take(512, F16).rearrange("p (a n) -> p a n", a=2) for _ in range(2)]
            Hk, Lk = [take(NK, F16).rearrange("p (a n) -> p a n", a=2) for _ in range(2)]

            def four(words):
                return [take(words, F16).rearrange("p (t a n) -> p t a n", t=2, a=2) for _ in range(2)]
            M1, M2, S1, S2 = four(1024), four(1024), four(2 * NK), four(2 * NK)
            VH = [take(960, F16).rearrange("p (c h n) -> p c h n", c=6, h=4) for _ in range(4)]
            VL = [take(768, F16).rearrange("p (c h n) -> p c h n", c=6, h=4) for _ in range(4)]
            E = [take(1024).rearrange("p (c n) -> p c n", c=2) for _ in range(3)]
            EH, EL = [[take(1536, F16).rearrange("p (c n) -> p c n", c=6) for _ in range(2)] for _ in range(2)]
            er_free, e_n = {}, [0]
            mx = take(16).rearrange("p (q h) -> p q h", q=4)
            mneg = take(8, F16).rearrange("p (q h) -> p q h", q=4)
            mrow = take(256, F16)
            memset(PO, rpart, 0.0)
            for g in range(4):
                PO.op(lambda e, g=g: e.memset(VH[g][:, :, :, 64:80], 0.0))
                for j in range(4):
                    h = 4 * g + j
                    PO.op(lambda e, g=g, j=j, h=h: e.memset(VH[g][:, :, j, 64 + h:65 + h], 1.0))
            for i in range(2):
                memset(DV, S2[i][64:128], 0.0)
                PO.wait(DV.last)
                memset(PO, M2[i][64:128], 0.0)
                memset(PO, S2[i][64:65], 1.0)
            zero = PO.last
            s = {}
            E_free, vp_free, den_t = {}, {}, {}
            ot_free, done_pv = {}, {}

            def project(b, g):
                u = 4 * b + g
                i = u % 2
                prev, prev2 = s.get(u - 1, {}), s.get(u - 2, {})
                PE.wait(kv_ready[b])
                bq = banks(2)
                for a in range(2):
                    tq = mm(PS[:, bq + a, :], wq[:, 128 * (2 * g + a):128 * (2 * g + a) + 128], KV[:, b, TC:], inc=(a == 1))
                AC.wait(tq, prev.get("wr"))
                h = cp(AC, Hq, PS[:, bq:bq + 2, :])
                DV.wait(h, tq, prev.get("wr"))
                lo = tt(DV, Lq, PS[:, bq:bq + 2, :], Hq, ALU.subtract)
                free(bq, 2, h, lo)
                xw = f"xp{i}"
                dma(xw, io["s_xq"][i, 0], Hq, h, prev2.get("rd"))
                dma(xw, io["s_xq"][i, 1], Lq, lo, prev2.get("rd"))
                yield
                for a in range(2):
                    bk = banks(2)
                    kp = PS[:, bk:bk + 2, :].rearrange("p a n -> p (a n)")
                    wka = wk[:, 128 * (2 * g + a):128 * (2 * g + a) + 128]
                    mm(kp[:, 0:512], wka, KV[:, b, 0:512])
                    tk = mm(kp[:, 512:NK], wka, KV[:, b, 512:NK], inc=True)
                    AC.wait(tk)
                    h = cp(AC, Hk[:, a, :], kp[:, 0:NK])
                    DV.wait(h, tk)
                    lo = tt(DV, Lk[:, a, :], kp[:, 0:NK], Hk[:, a, :], ALU.subtract)
                    free(bk, 2, h, lo)
                dma(xw, io["s_xk"][i, 0], Hk, h, prev2.get("rd"))
                yield
                wr = dma(xw, io["s_xk"][i, 1], Lk, lo)
                s[u] = {"wr": wr}
                for c2 in range(3):
                    yield
                    bv = banks()
                    for c in range(2):
                        k = 2 * c2 + c
                        n = sizes[k]
                        tv = mm(PS[0:n, bv, 256 * c:256 * c + 256], KV[:, b, 128 * k:128 * k + n],
                                wv[:, 256 * g:256 * g + 256], inc=(c == 1))
                    AC.wait(tv, vp_free.get(g), zero)
                    ch = PS[:, bv, :].rearrange("p (c h n) -> p c h n", c=2, h=4)
                    parts = ((128, slice(0, 2)),) if c2 < 2 else ((128, slice(0, 1)), (26, slice(1, 2)))
                    for r, k in parts:
                        kc = slice(2 * c2 + k.start, 2 * c2 + k.stop)
                        v = cp(AC, VH[g][0:r, kc, :, 0:64], ch[0:r, k])
                    DV.wait(v, vp_free.get(g))
                    for r, k in parts:
                        kc = slice(2 * c2 + k.start, 2 * c2 + k.stop)
                        v = tt(DV, VL[g][0:r, kc], ch[0:r, k], VH[g][0:r, kc, :, 0:64], ALU.subtract)
                    free(bv, 1, v)
                s[u]["v"] = v

            def maxima(b, g):
                u = 4 * b + g
                i = u % 2
                prev, prev2 = s.get(u - 1, {}), s.get(u - 2, {})
                wr = s[u]["wr"]
                done = prev2.get("sc")
                xq = io["s_xq"][i].rearrange("s (t p) a n -> s p t a n", t=2)
                xk = io["s_xk"][i].rearrange("s (t p) a n -> s p t a n", t=2)
                dma("xr", M1[i][0:64], xq[0], wr, done)
                dma("xr", S1[i][0:64], xk[0], wr, done)
                dma("xr", M1[i][64:128], xq[0], wr, done)
                dma("xr", M2[i][0:64], xq[1], wr, done)
                dma("xr", S1[i][64:128], xk[1], wr, done)
                rd = dma("xr", S2[i][0:64], xk[0], wr, done)
                for _ in range(3):
                    yield
                PE.wait(rd)
                for par in range(2):
                    for a in range(2):
                        for q in range(4):
                            yield
                            bb = banks(2)
                            kp = PS[:, bb:bb + 2, :].rearrange("p a n -> p (a n)")
                            lq = M1[i][:, par, a, 128 * q:128 * q + 128]
                            mm(kp[:, 0:512], lq, S1[i][:, par, a, 0:512])
                            t = mm(kp[:, 512:NK], lq, S1[i][:, par, a, 512:NK], inc=True)
                            DV.wait(t)
                            r = red(mx[:, q, 2 * par + a:2 * par + a + 1], kp[:, 0:NK], ALU.max)
                            free(bb, 2, r)
                DV.wait(r, prev.get("mt"))
                mt = ts(DV, mneg, mx, -1.0, ALU.mult)
                yield
                yield
                bm = banks()
                PE.wait(mt)
                for q in range(4):
                    t = mm(PS[0:4, bm, 128 * q:128 * q + 128], mneg[:, q, :], ident16[:], inc=(q == 3))
                AC.wait(t, prev.get("mscr"))
                c = cp(AC, mrow[0:4], PS[0:4, bm, :])
                free(bm, 1, c)
                mw = dma("xmw", io["s_xm"], mrow[0:4], c, prev.get("mrd"))
                m = dma("xmr", M2[i][64:65].rearrange("p t a n -> p (t a) n"), io["s_xm"].unsqueeze(0), mw, done, zero)
                yield
                s[u] |= {"rd": rd, "mt": t, "mscr": mw, "mrd": m}

            def part_b(b, g):
                u = 4 * b + g
                i = u % 2
                PE.wait(s[u]["mrd"], s[u]["v"], zero)
                pend = []

                def pv(n, par, a, ej, exs, part):
                    acc = 6 + n % 2
                    PE.wait(exs[part], freed[acc])
                    for c in range(2 * part, 2 * part + 2):
                        k = sizes[c]
                        j = 2 * a + par
                        mm(PS[0:80, acc, :], VH[g][0:k, c, j, :], EH[ej][0:k, c, :], start=(c == 0), stop=False)
                        mm(PS[0:64, acc, :], VL[g][0:k, c, j, :], EH[ej][0:k, c, :], start=False, stop=False)
                        t = mm(PS[0:80, acc, :], VH[g][0:k, c, j, :], EL[ej][0:k, c, :],
                               start=False, stop=(c == 5), inc=(c == 5))
                    if part < 2:
                        return
                    E_free[ej] = t
                    AC.wait(t)
                    if n == 0 and g == 0:
                        AC.wait(ot_free.get(b % 2))
                    o = cp(AC, OT[b % 2][64 * par:64 * par + 64, 2 * g + a, :], PS[0:64, acc, :])
                    DV.wait(t, den_t.get("last"))
                    if n == 0 and g == 0:
                        d = cp(DV, den[b % 2][64:80], PS[64:80, acc, :])
                    else:
                        d = tt(DV, den[b % 2][64:80], PS[64:80, acc, :], den[b % 2][64:80], ALU.add)
                    den_t["last"] = d
                    free(acc, 1, o, d)
                    done_pv["t"], done_pv["o"] = t, o
                n = 0
                lows = []

                def low(ej, er, c2, hi, ready, token, parts):
                    eng = DV if c2 else PO
                    eng.wait(hi, ready)
                    for r, k in parts:
                        kc = slice(2 * c2 + k.start, 2 * c2 + k.stop)
                        token[0] = tt(eng, EL[ej][0:r, kc], E[er][0:r, k], EH[ej][0:r, kc], ALU.subtract)
                for par in range(2):
                    for a in range(2):
                        ej = (4 * u + n) % 2
                        exs = []
                        for c2 in range(3):
                            er = e_n[0] % 3
                            e_n[0] += 1
                            bb = banks(2)
                            for c in range(2):
                                k = 2 * c2 + c
                                z = sizes[k]
                                ks = slice(128 * k, 128 * k + z)
                                mm(PS[0:z, bb + c, :], S1[i][:, par, a, ks], M1[i][:, par, a, :], stop=False)
                                sc = mm(PS[0:z, bb + c, :], S2[i][:, par, a, ks], M2[i][:, par, a, :],
                                        start=False, inc=(c == 1))
                            AC.wait(sc, er_free.get(er))
                            parts = ((128, slice(0, 2)),) if c2 < 2 else ((128, slice(0, 1)), (26, slice(1, 2)))
                            for r, k in parts:
                                ex = act(E[er][0:r, k], PS[0:r, bb + k.start:bb + k.stop, :], ACT.Exp, scale=0.125)
                            free(bb, 2, ex)
                            AC.wait(ex, E_free.get(ej))
                            for r, k in parts:
                                kc = slice(2 * c2 + k.start, 2 * c2 + k.stop)
                                hi = cp(AC, EH[ej][0:r, kc], E[er][0:r, k])
                            if lows:
                                low(*lows.pop(0))
                            ex = er_free[er] = [None]
                            lows.append((ej, er, c2, hi, E_free.get(ej), ex, parts))
                            exs.append(ex)
                            if pend:
                                pv(*pend[0], c2)
                            yield
                        if pend:
                            pend.pop(0)
                        pend.append((n, par, a, ej, exs))
                        n += 1
                low(*lows.pop(0))
                for part in range(3):
                    pv(*pend[0], part)
                s[u]["sc"] = sc
                vp_free[g] = done_pv["t"]
                if g == 3:
                    done_pv[b] = done_pv["o"]

            def part_c(b):
                O, dn = OT[b % 2], den[b % 2]
                D1(den_t["last"])
                D1(recip(rden[64:80], dn[64:80]))
                D1(ts(DV, rden[64:80], rden[64:80], SEL, ALU.mult))
                D1(cp(DV, rpart[64:80], rden[64:80]))
                rt = tt(DV, rpart[96:112], rden[64:80], rpart[64:80], ALU.subtract)
                yield
                yield
                yield
                PE.wait(rt)
                DV.wait(done_pv[b])
                for a in range(8):
                    bb = banks()
                    t = mm(PS[:, bb, :], sel[64:112, a, :], rpart[64:112], inc=True)
                    DV.wait(t)
                    n = tt(DV, O[:, a, :], O[:, a, :], PS[:, bb, :], ALU.mult)
                    free(bb, 1, n)
                    yield
                yield
                PE.wait(n)
                bo = banks()
                for j in range(4):
                    for a in range(8):
                        t = mm(PS[:, bo, 128 * j:128 * j + 128], O[:, a, 128 * j:128 * j + 128], wo[:, a, :],
                               start=(a == 0), stop=(a == 7), inc=(j == 3 and a == 7))
                ot_free[b % 2] = t
                yield from residual_steps(b, bo, t)

            def stream_p(u):
                if u < 16:
                    yield from project(u // 4, u % 4)
                if u % 4 == 2 and u > 4:
                    yield from part_c(u // 4 - 1)
                if u % 4 == 0 and u > 4:
                    turn(u // 4 - 2)

            DV.wait(zero)

            def finish():
                yield from tail0
                yield from latents(NB - 1)
            tail0 = yield
            weave((project(0, 0), 7), (finish(), 12))
            weave((maxima(0, 0), 20), (project(0, 1), 7))
            for u in range(16):
                b, g = u // 4, u % 4
                streams = [(part_b(b, g), 13), (stream_p(u + 2), 7 + (12 if g == 0 and u else 0))]
                if u < 15:
                    streams.append((maxima((u + 1) // 4, (u + 1) % 4), 26))
                weave(*streams)
                if u == 13 and phases > 2:
                    keep, top[0] = top[0], 0
                    loaded.append(moe_weights(PE.last))
                    top[0] = keep

            def tail():
                yield from part_c(NB - 1)
                for _ in range(6):
                    yield
                turn(NB - 1)
            yield tail()

        def pick(b, lg, n, bits, idx, idxf):
            for j in range(4):
                t = DV.op(lambda e, j=j: e.max(bits[:, j, :], lg[:, j, :]))
            D1(t)
            for j in range(4):
                t = DV.op(lambda e, j=j: e.max_index(idx[:, j, :], bits[:, j, :], lg[:, j, :]))
            D1(t)
            return D1(cp(DV, idxf, idx[:, :, 0:2]))

        loaded = []

        def moe_weights(free_):
            up, gt = take(1024), take(1024)
            sg, su = take(128), take(128)
            rw, rb, iota = take(16), take(16), take(16)
            SP.wait(free_)
            for o, i in ((rw, "m_rw"), (rb[0:1], "m_rb"), (iota, "iota16"), (up, "m_up"), (gt, "m_gate"),
                         (sg, "m_sg"), (su, "m_su")):
                l = dma("w2", o, io[i])
            return up, gt, sg, su, rw, rb, iota, l

        def l0_ffn(tail, layer1):
            up, gt, sg, su, rw, rb, iota, l = loaded[0]
            sel = arena[:, 4100:4612].bitcast(F16).rearrange("p (a n) -> p a n", a=8)
            top[0] = 32420
            dn = take(1152).rearrange("p (a n) -> p a n", a=9)
            ld = dma("w2b", dn, io["m_down"])
            v4 = lambda n, m: take(4 * n * m).rearrange("p (k a n) -> p k a n", k=n, a=4)
            lg = v4(1, 16)[:, 0]
            m8, i8 = v4(1, 8)[:, 0], v4(1, 8)[:, 0].bitcast(U32)
            ixf = v4(1, 2)[:, 0]
            oh = v4(3, 16)
            wt = take(16).rearrange("p (k a) -> p k a", k=4)
            CT = [take(256, F16) for _ in range(2)]
            for i in range(2):
                D1(memset(DV, CT[i], 0.0))
            SG = [take(512) for _ in range(3)]
            Hh = [take(4608).rearrange("p (a n) -> p a n", a=9) for _ in range(2)]
            PE.wait(l)
            DV.wait(l)
            ct_ready, h_free, sg_free = {}, {}, {}
            iob = iota.unsqueeze(1).broadcast_to([128, 4, 16])

            def route(b):
                bb = banks()
                PE.wait(xt_ready[b])
                for j in range(4):
                    o = PS[:, bb, 16 * j:16 * j + 16]
                    mm(o, XT[:, T * b + 128 * j:T * b + 128 * j + 128], rw, stop=False)
                    t = mm(o, ones[0:1, :], rb[0:1], start=False, inc=(j == 3))
                DV.wait(t)
                t = D1(cp(DV, lg, PS[:, bb, 0:64].rearrange("p (a n) -> p a n", a=4)))
                free(bb, 1, t)
                pick(b, lg, 16, m8, i8, ixf)
                t = D1(tt(DV, wt[:, 0, :], m8[:, :, 1], m8[:, :, 0], ALU.subtract))
                AC.wait(t)
                t = act(wt[:, 1, :], wt[:, 0, :], ACT.Exp)
                DV.wait(t)
                D1(ts(DV, wt[:, 0, :], wt[:, 1, :], 1.0, ALU.add))
                D1(recip(wt[:, 2, :], wt[:, 0, :]))
                D1(tt(DV, wt[:, 3, :], wt[:, 1, :], wt[:, 2, :], ALU.mult))
                tt(DV, oh[:, 0], iob, bc(ixf[:, :, 0], 16), ALU.is_equal)
                D1(tt(DV, oh[:, 1], iob, bc(ixf[:, :, 1], 16), ALU.is_equal))
                D1(ts(DV, wt[:, 2:4, :], wt[:, 2:4, :], SEL, ALU.mult))
                tt(DV, oh[:, 0], oh[:, 0], bc(wt[:, 2, :], 16), ALU.mult)
                D1(tt(DV, oh[:, 1], oh[:, 1], bc(wt[:, 3, :], 16), ALU.mult))
                t = D1(tt(DV, oh[:, 2], oh[:, 0], oh[:, 1], ALU.add))
                yield
                bb = banks()
                PE.wait(t)
                for j in range(4):
                    t = tr(PS[0:16, bb, 128 * j:128 * j + 128], oh[:, 2, j, :], j == 3)
                D1(t)
                D1(cp(DV, CT[b % 2][0:16], PS[0:16, bb, :]))
                t = tt(DV, CT[b % 2][32:48], PS[0:16, bb, :], CT[b % 2][0:16], ALU.subtract)
                free(bb, 1, t)
                ct_ready[b] = t

            def experts(b):
                cols = slice(T * b, T * b + T)
                H = Hh[b % 2]
                PE.wait(xt_ready[b])
                nr = iter(())
                for p in range(9):
                    if b and p == 1:
                        rs = down(b - 1)
                    if b and 1 < p < 6:
                        next(rs, None)
                    if p == 2 and b + 1 < NB:
                        nr = route(b + 1)
                    if p in (2, 6):
                        next(nr, None)
                    if b and p == 7:
                        turn(b - 1)
                    i = (9 * b + p) % 3
                    bu = banks(2)
                    c = slice(128 * p, 128 * p + 128)
                    tg = mm(PS[:, bu, :], gt[:, c] if p < 8 else sg, XT[:, cols], inc=True)
                    t = mm(PS[:, bu + 1, :], up[:, c] if p < 8 else su, XT[:, cols], inc=True)
                    AC.wait(tg, sg_free.get(i))
                    a = act(SG[i], PS[:, bu, :], ACT.Silu)
                    DV.wait(a, t, h_free.get(b % 2))
                    if p == 8:
                        t = tt(DV, H[:, p, :], SG[i], PS[:, bu + 1, :], ALU.mult)
                        free(bu, 2, t)
                    else:
                        bw = 6 + p % 2
                        PE.wait(ct_ready[b], freed[bw])
                        w = mm(PS[:, bw, :], sel[0:48, p, :], CT[b % 2][0:48], inc=True)
                        t = D1(tt(DV, SG[i], SG[i], PS[:, bu + 1, :], ALU.mult))
                        free(bu, 2, t)
                        DV.wait(w)
                        t = tt(DV, H[:, p, :], SG[i], PS[:, bw, :], ALU.mult)
                        free(bw, 1, t)
                    sg_free[i] = t
                    yield
                h_ready[b] = t

            def down(b):
                H = Hh[b % 2]
                bo = banks()
                PE.wait(h_ready[b], ld)
                for j in range(4):
                    for p in range(9):
                        t = mm(PS[:, bo, 128 * j:128 * j + 128], H[:, p, 128 * j:128 * j + 128], dn[:, p, :],
                               start=(p == 0), stop=(p == 8), inc=(j == 3 and p == 8))
                h_free[b % 2] = t
                return residual_steps(b, bo, t)

            h_ready = {}

            weave((route(0), 1))
            weave((tail, 19), (experts(0), 9))
            if layer1:
                next(layer1)
            weave((experts(1), 9))
            weave((experts(2), 9), (next(layer1) if layer1 else iter(()), 27))
            weave((experts(3), 9), (next(layer1) if layer1 else iter(()), 11))
            weave((down(NB - 1), 1))
            if layer1:
                weave((next(layer1), 1))
            turn(NB - 1)

        def l1_attn():
            top[0] = 5124
            SP.wait(PE.last, DV.last, AC.last)
            PO.wait(PE.last, DV.last, AC.last)
            wq, wk, wv, wo = take(1024), take(1024), take(1024), take(1024).rearrange("p (a n) -> p a n", a=8)
            wb, bb_ = take(16), take(16)
            maskL, maskU = take(128), take(128)
            for o, i in ((wq, "d_wq"), (wk, "d_wk"), (wv, "d_wv"), (wo, "d_wo"), (wb, "d_wb"), (bb_[0:1], "d_bb"),
                         (maskL, "mask_l"), (maskU, "mask_u")):
                l = dma("w3", o, io[i])
            Kn = [take(4096).rearrange("p (c n) -> p c n", c=4) for _ in range(2)]
            KT = [take(4096).rearrange("p (a n) -> p a n", a=8) for _ in range(2)]
            beta = [take(64).rearrange("p (h c) -> p h c", h=16) for _ in range(2)]
            work[:] = [top[0]]
            GA = take(2048)
            XI = take(2048)
            tmp = take(512)
            sqk = take(512)
            ss = take(64 * 4).rearrange("p (k c h) -> p k c h", k=4, c=4)
            two = range(2)
            KB = take(1024).rearrange("p (t n) -> p t n", t=2)
            kb_zero = memset(PO, KB, 0.0)
            s1, s2 = {}, {}
            sq_read, kb_read = [None], [None]

            def part(gen, n):
                for _ in range(n):
                    if next(gen, StopIteration) is StopIteration:
                        return
                    yield

            def stage1(b):
                i = b % 2
                if b == 0:
                    for e in (PE, DV, AC):
                        e.wait(l)
                prev = s1.get(b - 1, {})
                done = s2.get(b - 2)
                PE.wait(xt_ready[b])
                bbk = banks()
                for c in range(4):
                    o = PS[:, bbk, 16 * c:16 * c + 16]
                    mm(o, XT[:, T * b + 128 * c:T * b + 128 * c + 128], wb, stop=False)
                    t = mm(o, ones[0:1, :], bb_[0:1], start=False, inc=(c == 3))
                AC.wait(t, done)
                t = act(beta[i].rearrange("p h c -> p c h"), PS[:, bbk, 0:64].rearrange("p (c h) -> p c h", c=4), ACT.Sigmoid)
                free(bbk, 1, t)
                bt = t
                AC.wait(done)
                for c in range(4):
                    for j in range(2):
                        bk = banks()
                        t = mm(PS[:, bk, :], XT[:, T * b + 128 * c:T * b + 128 * c + 128],
                               wk[:, 512 * j:512 * j + 512], inc=True)
                        AC.wait(t)
                        k = cp(AC, Kn[i][:, c, 512 * j:512 * j + 512], PS[:, bk, :])
                        AC.wait(sq_read[0])
                        t = act(sqk, PS[:, bk, :], ACT.Square)
                        free(bk, 1, t, k)
                        DV.wait(t)
                        r = sq_read[0] = red(ss[:, 0, c, 8 * j:8 * j + 8], sqk.rearrange("p (h n) -> p h n", h=8), ALU.add)
                        yield
                D1(r)
                fl = [ss[:, k].rearrange("p c h -> p (c h)") for k in range(4)]
                D1(ts(DV, fl[0], fl[0], 1e-24, ALU.max))
                yield
                r = rsqrt(fl[0], fl[1], fl[2], fl[3])
                PO.wait(r, k)
                ts_ = []
                for c in range(4):
                    if c % 2 == 0:
                        yield
                    kc = Kn[i][:, c, :].rearrange("p (h n) -> p h n", h=16)
                    ts_.append(tt((PO, DV)[c % 2], kc, kc, bc(ss[:, 1, c], 64), ALU.mult))
                for _ in range(2):
                    yield
                PE.wait(*ts_)
                G = GA.rearrange("p (h c n) -> p h c n", h=16, c=4)

                def turned_keys(p):
                    bk = banks()
                    for c in range(4):
                        t = tr(PS[:, bk, 128 * c:128 * c + 128], Kn[i][:, c, 128 * p:128 * p + 128], c == 3)
                    AC.wait(t)
                    cp(AC, KT[i][:, p, :], PS[:, bk, :])
                    AC.wait(kb_read[0], kb_zero)
                    for par in range(2):
                        k = cp(AC, KB[64 * par:64 * par + 64, par, :], PS[64 * par:64 * par + 64, bk, :])
                    free(bk, 1, k)
                    return k
                k = turned_keys(0)
                yield
                for p in range(8):
                    PE.wait(k)
                    if p == 0:
                        DV.wait(bt, prev.get("ga_free"))
                    bk = banks(2)
                    for c in range(4):
                        cc = slice(128 * c, 128 * c + 128)
                        t = mm(PS[:, bk + c // 2, 256 * (c % 2):256 * (c % 2) + 256], KT[i][:, p, cc], KB[:, :, cc],
                               inc=(c == 3))
                    kb_read[0] = t
                    if p < 7:
                        k = turned_keys(p + 1)
                    DV.wait(t)
                    for q in range(4):
                        r = slice(32 * q, 32 * q + 32)
                        for par in range(2):
                            src = PS[r, bk:bk + 2, :].rearrange("p k (c h n) -> p (k c) h n", c=2, h=2)[
                                :, :, par, 32 * q:32 * q + 32]
                            g = tt(DV, G[r, 2 * p + par], src, bc(beta[i][r, 2 * p + par, :], 32), ALU.mult)
                    free(bk, 2, g)
                    yield
                    yield
                w = dma("gw", io["s_g"], GA, g, prev.get("grd"))
                sg = io["s_g"].rearrange("(q t) (l u s) -> q l u t s", q=4, l=2, u=32)
                L4 = GA.rearrange("p (l t s) -> p l t s", l=2, t=32)
                for q in range(4):
                    for sl in range(2):
                        rd = dma("gr", L4[32 * q:32 * q + 32, sl], sg[q, sl], w)
                XL = XI.rearrange("p (l s t) -> p l s t", l=2, s=32)
                for sl in range(2):
                    rd = dma("gr", XI[:, 1024 * sl:1024 * sl + 1024], io["eye32"], prev.get("xw"))
                PO.wait(rd)
                for t in range(31, 0, -1):
                    n = 32 - t
                    tm = tmp[:, 0:2 * t * n].rearrange("p (l s t) -> p l s t", l=2, s=t)
                    a = L4[:, :, t, 0:t].unsqueeze(3).broadcast_to([128, 2, t, n])
                    x = XL[:, :, t, t:32].unsqueeze(2).broadcast_to([128, 2, t, n])
                    tt(PO, tm, a, x, ALU.mult)
                    z = tt(PO, XL[:, :, 0:t, t:32], XL[:, :, 0:t, t:32], tm, ALU.subtract)
                xw = dma("xw1", io["s_x"][i], XI, z, s1.get(b - 2, {}).get("xrd"), eng=PO)
                s1[b] = {"ga_free": z, "grd": rd, "xw": xw, "bt": bt, "k": k}

            yield
            yield stage1(0)
            nxt = stage1(1)
            yield part(nxt, 11)
            yield part(nxt, 1)
            top[0], keep = 0, top[0]
            LN_ = [take(2048).rearrange("p (h c n) -> p h c n", h=4, c=4) for _ in two]
            OT = take(1024).rearrange("p (a n) -> p a n", a=2)
            top[0] = keep
            QT = [take(1024).rearrange("p (a n) -> p a n", a=2) for _ in two]
            V = [take(1024).rearrange("p (c n) -> p c n", c=4) for _ in two]
            P = [take(2048).rearrange("p (h c n) -> p h c n", h=4, c=4) for _ in two]
            XE = [take(2048).rearrange("p (h c n) -> p h c n", h=4, c=4) for _ in two]
            BD = take(2048).rearrange("p (k t n) -> p k t n", k=2, t=2)
            S = [take(256).rearrange("p (a n) -> p a n", a=2) for _ in two]
            R, A, B = [take(256) for _ in range(3)]
            before = [PE.last, DV.last, AC.last]
            for e in (PE, DV, AC, SP):
                e.wait(before)
            for t in XE + S + [BD]:
                zero = memset(DV, t, 0.0)

            last = {}

            def prep(u):
                b, g, j, i = u // 4, u % 4, u % 2, (u // 4) % 2
                cols = slice(T * b, T * b + T)
                sx = io["s_x"][i].rearrange("(q v u) (l s t) -> q v l s u t", q=4, v=2, l=2, s=32)
                XEu = XE[j].rearrange("p h c n -> p (h c) n")
                for q in range(4):
                    r = slice(32 * q, 32 * q + 32)
                    xr = dma(f"xer{j}", XEu[r, :, 32 * q:32 * q + 32], sx[q, g % 2, g // 2], s1[b]["xw"], last.get(u - 2), zero)
                s1[b]["xrd"] = xr
                DV.wait(last.get(u - 2))
                mu = maskU.unsqueeze(1).broadcast_to([128, 2, 128])

                def turned(h, ll):
                    PE.wait(ll, xr)
                    bk = banks()
                    for c in range(4):
                        t = mm(PS[:, bk, 128 * c:128 * c + 128], LN_[j][:, h, c, :], XE[j][:, h, c, :], inc=(c == 3))
                    AC.wait(t)
                    n = cp(AC, LN_[j][:, h], PS[:, bk, :].rearrange("p (c n) -> p c n", c=4))
                    free(bk, 1, n)
                    return n
                ll = None
                for a in range(2):
                    AC.wait(bd_read[0], zero, s1[b]["k"], last.get(u - 2))
                    for par in range(2):
                        r = slice(64 * par, 64 * par + 64)
                        cp(AC, BD[r, 0, par, :], KT[i][r, 2 * g + a, :])
                    bk = banks()
                    t = mm(PS[:, bk, :], wq[:, 256 * g + 128 * a:256 * g + 128 * a + 128], XT[:, cols], inc=True)
                    AC.wait(t)
                    for par in range(2):
                        r = slice(64 * par, 64 * par + 64)
                        k = cp(AC, BD[r, 1, par, :], PS[r, bk, :])
                    t = cp(AC, QT[j][:, a, :], PS[:, bk, :])
                    free(bk, 1, t)
                    yield
                    if a == 0:
                        for c2 in range(2):
                            bk = banks()
                            for c in range(2):
                                n = T * b + 128 * (2 * c2 + c)
                                t = mm(PS[:, bk, 256 * c:256 * c + 256], XT[:, n:n + 128],
                                       wv[:, 256 * g:256 * g + 256], inc=(c == 1))
                            AC.wait(t)
                            t = cp(AC, V[j][:, 2 * c2:2 * c2 + 2, :], PS[:, bk, :].rearrange("p (c n) -> p c n", c=2))
                            free(bk, 1, t)
                            yield
                    if a:
                        turned(0, ll)
                        yield
                        turned(1, ll)
                        yield
                    PE.wait(k)
                    for c in range(4):
                        cc = slice(128 * c, 128 * c + 128)
                        bk = 6 + c % 2
                        PE.wait(k, freed[bk])
                        mm(PS[:, bk, 0:256], KT[i][:, 2 * g + a, cc], BD[:, 0, :, cc])
                        yield
                        PE.wait(k)
                        t = bd_read[0] = mm(PS[:, bk, 256:512], KT[i][:, 2 * g + a, cc], BD[:, 1, :, cc], inc=True)
                        ps = PS[:, bk, :].rearrange("p (k t n) -> p k t n", k=2, t=2)
                        DV.wait(t)
                        for par in range(2):
                            h = 2 * a + par
                            ll = stt(LN_[j][:, h, c, :], ps[:, 0, par], beta[i][:, 4 * g + h, c:c + 1],
                                     maskL, ALU.mult, ALU.mult)
                        pp = tt(DV, P[j][:, 2 * a:2 * a + 2, c, :], ps[:, 1], mu, ALU.mult)
                        free(bk, 1, pp)
                        yield
                turned(2, ll)
                yield
                n = turned(3, ll)
                ready[u] = [n, pp]

            bd_read = [None]
            ready = {}

            def chain(u):
                b, g, j, i = u // 4, u % 4, u % 2, (u // 4) % 2
                v3 = lambda x: x.rearrange("p (h n) -> p h n", h=4)
                st_ready = None
                PE.wait(ready[u])
                for c in range(4):
                    bcol = bc(beta[i][:, 4 * g:4 * g + 4, c], 64)
                    if c:
                        bk = banks()
                        PE.wait(st_ready)
                        for a in range(2):
                            t = mm(PS[:, bk, 128 * a:128 * a + 128], KT[i][:, 2 * g + a, 128 * c:128 * c + 128],
                                   S[j][:, a, :], inc=(a == 1))
                        DV.wait(t)
                        t = D1(tt(DV, R, V[j][:, c, :], PS[:, bk, 0:256], ALU.subtract))
                        free(bk, 1, t)
                        t = tt(DV, v3(R), v3(R), bcol, ALU.mult)
                    else:
                        t = tt(DV, v3(R), v3(V[j][:, c, :]), bcol, ALU.mult)
                    yield
                    bk = banks()
                    PE.wait(t)
                    for h in range(4):
                        t = mm(PS[:, bk, 64 * h:64 * h + 64], XE[j][:, h, c, :], R[:, 64 * h:64 * h + 64], inc=(h == 3))
                    DV.wait(t)
                    t = cp(DV, A, PS[:, bk, 0:256])
                    free(bk, 1, t)
                    src = A
                    for k in range(3):
                        yield
                        bk = banks()
                        PE.wait(t)
                        for h in range(4):
                            t = mm(PS[:, bk, 64 * h:64 * h + 64], LN_[j][:, h, c, :], src[:, 64 * h:64 * h + 64],
                                   inc=(h == 3))
                        D1(t)
                        t = tt(DV, B, A, PS[:, bk, 0:256], ALU.subtract)
                        free(bk, 1, t)
                        src = B
                    yield
                    PE.wait(t)
                    if c < 3:
                        bk = banks()
                        for h in range(4):
                            par, a = h % 2, h // 2
                            t = mm(PS[64 * par:64 * par + 64, bk, 64 * a:64 * a + 64],
                                   Kn[i][:, c, 64 * (4 * g + h):64 * (4 * g + h) + 64],
                                   B[:, 64 * h:64 * h + 64], inc=(h == 3))
                    bo = banks()
                    for a in range(2):
                        if c:
                            mm(PS[:, bo, 128 * a:128 * a + 128], S[j][:, a, :], QT[j][:, a, 128 * c:128 * c + 128], stop=False)
                        for par in range(2):
                            h = 2 * a + par
                            to = mm(PS[64 * par:64 * par + 64, bo, 128 * a:128 * a + 128], B[:, 64 * h:64 * h + 64],
                                    P[j][:, h, c, :], start=(c == 0), inc=(h == 3))
                    if c < 3:
                        DV.wait(to)
                        for par in range(2):
                            r = slice(64 * par, 64 * par + 64)
                            so = S[j][r, :, 64 * par:64 * par + 64]
                            ps = PS[r, bk, 0:128].rearrange("p (a n) -> p a n", a=2)
                            t = cp(DV, so, ps) if c == 0 else tt(DV, so, so, ps, ALU.add)
                        free(bk, 1, t)
                        st_ready = t
                    AC.wait(to, last.get(u - 1))
                    ot = cp(AC, OT[:, :, 128 * c:128 * c + 128], PS[:, bo, 0:256].rearrange("p (a n) -> p a n", a=2))
                    free(bo, 1, ot)
                    yield
                    D1(t)
                PE.wait(ot)
                bo = banks()
                for k in range(4):
                    for a in range(2):
                        t = mm(PS[:, bo, 128 * k:128 * k + 128], OT[:, a, 128 * k:128 * k + 128], wo[:, 2 * g + a, :],
                               start=(a == 0), stop=(a == 1), inc=(k == 3 and a == 1))
                last[u] = [t, DV.last]
                if g < 3:
                    xb = X[:, 4 * b:4 * b + 4, :]
                    DV.wait(t, x_ready[b], xt_ready[b])
                    t = tt(DV, xb, xb, PS[:, bo, :].rearrange("p (a b) -> p a b", a=4), ALU.add)
                    free(bo, 1, t)
                    x_ready[b] = t
                elif b < NB - 1:
                    s2[b] = [t, DV.last]
                    residual(b, bo, t)
                else:
                    rest.append((bo, t))

            def late_turn(b):
                yield
                turn(b)
            weave((prep(0), 1))
            for u in range(16):
                b, g = u // 4, u % 4
                if u == 12 and phases > 4:
                    for e in (PE, DV, AC):
                        SP.wait(e.last)
                    loaded.append(last_weights())
                if g == 0 and b:
                    nxt = stage1(b + 1) if b + 1 < NB else iter(())
                streams = [(chain(u), 26)]
                if u + 1 < 16:
                    streams.append((prep(u + 1), 24))
                if g < 2:
                    streams.append((part(nxt, 18 if g == 0 else 100), 20))
                if g == 1 and b:
                    streams.append((late_turn(b - 1), 4))
                if u > 13 and phases > 4:
                    if u == 14:
                        for e in (PE, DV, AC):
                            e.wait(PE.last, DV.last, AC.last, PO.last, s1[NB - 1]["xw"], s1[NB - 1]["xrd"])
                        attend, xg = l1_xattn()
                        rest.append(attend)
                    streams.append((part(xg, 13) if u == 14 else xg, 14))
                weave(*streams)
            yield

        rest, work = [], []

        def last_weights():
            keep = top[0]
            top[0] = 9508
            w1 = take(4096).rearrange("p (e n) -> p e n", e=8)
            top[0] = 17700
            wx, wy, wv, cT = take(128), take(128), take(128), take(NB * TC)
            bxy, bv = take(2), take(128)
            mc, mr = take(8), take(NB * TC)
            b1, wo, rw = take(512), take(512).rearrange("p (a n) -> p a n", a=4), take(8)
            bo, gb, iota = take(128), take(256), take(16)
            sel16 = take(512, F16).rearrange("p (e n) -> p e n", e=8)
            assert top[0] <= 21796
            for o, i in ((wx, "y_wx"), (wy, "y_wy"), (wv, "y_wv"), (cT, "ctx_T"), (bxy, "y_bxy"), (bv[0:1], "y_bv"),
                         (mc.bitcast(I32), "mask_c"), (mr[0:1].bitcast(I32), "mask_r"),
                         (w1, "f_w1"), (b1[0:8], "f_b1"), (wo, "f_wo"), (rw, "f_rw"), (bo[0:1], "f_bo"),
                         (gb[0:1], "f_gb"), (iota, "iota16"), (sel16[0:8], "sel8")):
                l = dma("w4", o, io[i])
            top[0] = keep
            return (wx, wy, wv, cT, bxy, bv, mc, mr), (w1, b1, wo, rw, bo, gb, iota, sel16), l

        def l1_xattn():
            (wx, wy, wv, cT, bxy, bv, mc, mr), _, l = loaded[1]
            keep, top[0] = top[0], work[0]
            mcf, mrf = take(8).rearrange("p (b c) -> p b c", b=4), take(NB * TC)
            Kp = take(NB * TC)
            Vp = take(NB * 2 * 129).rearrange("p (b c n) -> p b c n", b=4, c=2)
            Qp = [take(512) for _ in range(2)]
            E = [take(1024).rearrange("p (c n) -> p c n", c=2) for _ in range(2)]
            mx = [take(8).rearrange("p (k q) -> p k q", k=2) for _ in range(2)]
            mrow = [take(512) for _ in range(2)]
            rd = take(4)
            sizes = [128, 26]
            scale = float(D) ** -0.5
            assert top[0] <= 32420
            top[0] = keep

            def first():
                DV.wait(l)
                PE.wait(l)
                ts(DV, mcf.rearrange("p b c -> p (b c)"), mc.bitcast(I32), 1.0, ALU.is_equal, -1e30, ALU.mult)
                t = ts(DV, mrf[0:1], mr[0:1].bitcast(I32), 1.0, ALU.is_equal, -1e30, ALU.mult)
                vm = DV.op(lambda e: e.memset(Vp[:, :, :, 128:129], 1.0))
                for k in range(2):
                    bk = banks()
                    c = slice(308 * k, 308 * k + 308)
                    t = mm(PS[:, bk, 0:308], wy, cT[:, c], inc=True)
                    DV.wait(t)
                    t = ts(DV, Kp[:, c], PS[:, bk, 0:308], bxy[:, 1:2], ALU.add)
                    free(bk, 1, t)
                for b in range(NB):
                    yield
                    bk = banks()
                    for c in range(2):
                        n = sizes[c]
                        o = PS[0:n, bk, 128 * c:128 * c + 128]
                        mm(o, cT[:, TC * b + 128 * c:TC * b + 128 * c + n], wv, stop=False)
                        t = mm(o, ones[0:1, 0:n], bv[0:1], start=False, inc=True)
                    DV.wait(t)
                    for c in range(2):
                        n = sizes[c]
                        t = cp(DV, Vp[0:n, b, c, 0:128], PS[0:n, bk, 128 * c:128 * c + 128])
                    free(bk, 1, t)
                PE.wait(t, DV.last)
                AC.wait(t)
                for b in range(3):
                    yield from part_a(b)

            r = {}

            def part_a(b):
                i = b % 2
                bk = banks()
                PE.wait(xt_ready[b])
                t = mm(PS[:, bk, :], wx, XT[:, T * b:T * b + T], inc=True)
                DV.wait(t, r.get(b - 2))
                q = ts(DV, Qp[i], PS[:, bk, :], bxy[:, 0:1], ALU.add)
                free(bk, 1, q)
                yield
                bk = banks(2)
                PE.wait(q)
                kb = slice(TC * b, TC * b + TC)
                for j in range(4):
                    o = PS[:, bk + j // 2, TC * (j % 2):TC * (j % 2) + TC]
                    mm(o, Qp[i][:, 128 * j:128 * j + 128], Kp[:, kb], stop=False)
                    t = mm(o, ones[0:1, :], mrf[0:1, kb], start=False, inc=(j == 3))
                DV.wait(t)
                t = D1(red(mx[i][:, 0, :].rearrange("p (a q) -> p a q", a=2),
                           PS[:, bk:bk + 2, 0:2 * TC].rearrange("p a (q n) -> p a q n", q=2), ALU.max))
                free(bk, 2, t)
                t = ts(DV, mx[i][:, 1, :], mx[i][:, 0, :], -1.0, ALU.mult)
                yield
                bk = banks()
                PE.wait(t)
                for j in range(4):
                    t = mm(PS[0:1, bk, 128 * j:128 * j + 128], mx[i][:, 1, j:j + 1], ident[:], inc=(j == 3))
                D1(t)
                t = cp(DV, mrow[i][0:1], PS[0:1, bk, :])
                free(bk, 1, t)
                yield
                bk = banks(2)
                PE.wait(t)
                for c in range(2):
                    n = sizes[c]
                    mm(PS[0:n, bk + c, :], Kp[:, TC * b + 128 * c:TC * b + 128 * c + n], Qp[i], stop=False)
                    t = mm(PS[0:n, bk + c, :], ones[0:1, 0:n], mrow[i][0:1], start=False, inc=True)
                AC.wait(t, r.get(b - 2))
                for c in range(2):
                    n = sizes[c]
                    t = act(E[i][0:n, c, :], PS[0:n, bk + c, :], ACT.Exp, scale=scale, bias=mcf[0:n, b, c:c + 1])
                free(bk, 2, t)
                yield
                bk = banks(2)
                PE.wait(t)
                for j in range(4):
                    for c in range(2):
                        n = sizes[c]
                        t = mm(PS[:, bk + j // 2, 129 * (j % 2):129 * (j % 2) + 129], E[i][0:n, c, 128 * j:128 * j + 128],
                               Vp[0:n, b, c, :], start=(c == 0), stop=(c == 1), inc=(j == 3 and c == 1))
                r[b] = t
                DV.wait(t, x_ready[b], xt_ready[b])
                den = PS[:, bk:bk + 2, 0:258].rearrange("p a (q n) -> p a q n", q=2)[:, :, :, 128]
                D1(recip(rd.rearrange("p (a q) -> p a q", a=2), den))
                for j in range(4):
                    t = stt(X[:, 4 * b + j, :], PS[:, bk + j // 2, 129 * (j % 2):129 * (j % 2) + 128], rd[:, j:j + 1],
                            X[:, 4 * b + j, :], ALU.mult, ALU.add)
                free(bk, 2, t)
                D1(t)
                x_ready[b] = yield from normalize_steps(X[:, 4 * b:4 * b + 4, :], 1e-5, k=7)
                for _ in range(2):
                    yield
                turn(b)
            return part_a, first()

        def l1_ffn(attend):
            _, (w1, b1, wo, rw, bo, gb, iota, sel16), l = loaded[1]
            top[0] = 32420
            gam = take(256)
            lg = take(32).rearrange("p (a n) -> p a n", a=4)
            m8, i8 = take(32).rearrange("p (a n) -> p a n", a=4), take(32).rearrange("p (a n) -> p a n", a=4).bitcast(U32)
            ixf = take(8).rearrange("p (a n) -> p a n", a=4)
            oh = take(32).rearrange("p (a n) -> p a n", a=4)
            MT = [take(512) for _ in range(2)]
            M16 = [take(256, F16) for _ in range(2)]
            XM = [take(4096).rearrange("p (e n) -> p e n", e=8) for _ in range(2)]
            XY = [take(512) for _ in range(2)]
            HT = [take(2048).rearrange("p (a n) -> p a n", a=4) for _ in range(2)]
            DV.wait(l)
            PE.wait(l)
            bk = banks()
            t = mm(PS[:, bk, 0:256], ones[0:1, :], gb[0:1], inc=True)
            DV.wait(t)
            t = cp(DV, gam, PS[:, bk, 0:256])
            free(bk, 1, t)
            D1(t)
            g3 = gam[:, 0:128].unsqueeze(1).broadcast_to([128, 4, 128])
            b3 = gam[:, 128:256].unsqueeze(1).broadcast_to([128, 4, 128])
            iob = iota[:, 0:8].unsqueeze(1).broadcast_to([128, 4, 8])
            xm_free, ht_free = {}, {}

            def route(b):
                i = b % 2
                bk = banks()
                PE.wait(xt_ready[b])
                for j in range(4):
                    t = mm(PS[:, bk, 8 * j:8 * j + 8], XT[:, T * b + 128 * j:T * b + 128 * j + 128], rw, inc=(j == 3))
                D1(t)
                t = D1(cp(DV, lg, PS[:, bk, 0:32].rearrange("p (a n) -> p a n", a=4)))
                free(bk, 1, t)
                pick(b, lg, 8, m8, i8, ixf)
                t = D1(tt(DV, oh, iob, bc(ixf[:, :, 0], 8), ALU.is_equal))
                yield
                bk = banks()
                PE.wait(t)
                for j in range(4):
                    t = tr(PS[0:8, bk, 128 * j:128 * j + 128], oh[:, j, :], j == 3)
                DV.wait(t, xm_free.get(i))
                cp(DV, MT[i][0:8], PS[0:8, bk, :])
                m = cp(DV, M16[i][0:8], PS[0:8, bk, :])
                free(bk, 1, m)
                for e in range(8):
                    if e % 2 == 0:
                        yield
                    bk = banks()
                    PE.wait(m)
                    t = mm(PS[:, bk, :], sel16[0:8, e, :], M16[i][0:8], inc=True)
                    DV.wait(t)
                    t = tt(DV, XM[i][:, e, :], XT[:, T * b:T * b + T], PS[:, bk, :], ALU.mult)
                    free(bk, 1, t)
                xm_ready[b] = t

            xm_ready = {}

            def hidden(b):
                i = b % 2
                PE.wait(xm_ready[b])
                for a in range(4):
                    bk = 6 + a % 2
                    PE.wait(freed[bk])
                    c = slice(128 * a, 128 * a + 128)
                    for e in range(8):
                        if e % 2 == 0:
                            yield
                        mm(PS[:, bk, :], w1[:, e, c], XM[i][:, e, :], start=(e == 0), stop=False)
                    t = mm(PS[:, bk, :], b1[0:8, c], MT[i][0:8], start=False, inc=True)
                    AC.wait(t, ht_free.get(i))
                    h = act(HT[i][:, a, :], PS[:, bk, :], ACT.Gelu)
                    free(bk, 1, h)
                xm_free[i] = t
                yield
                yield
                bk = banks()
                PE.wait(h)
                for j in range(4):
                    o = PS[:, bk, 128 * j:128 * j + 128]
                    for a in range(4):
                        mm(o, HT[i][:, a, 128 * j:128 * j + 128], wo[:, a, :], start=(a == 0), stop=False)
                    t = mm(o, ones[0:1, :], bo[0:1], start=False, inc=(j == 3))
                ht_free[i] = t
                xb = X[:, 4 * b:4 * b + 4, :]
                Y = XY[i].rearrange("p (a n) -> p a n", a=4)
                DV.wait(t, x_ready[b])
                t = D1(tt(DV, Y, xb, PS[:, bk, :].rearrange("p (a b) -> p a b", a=4), ALU.add))
                free(bk, 1, t)
                normalize(Y, 1e-12)
                D1(tt(DV, Y, Y, g3, ALU.mult))
                D1(tt(DV, Y, Y, b3, ALU.add))
                D1(tt(DV, xb, xb, Y, ALU.add))
                t = normalize(xb, 1e-5)
                x_ready[b] = t
                done.append(dma(f"out{b}", io["out"][:, 4 * b:4 * b + 4, :], xb, t))

            def late(b):
                x_ready[b] = yield from normalize_steps(X[:, 4 * b:4 * b + 4, :], 1e-5, k=7)
                for _ in range(2):
                    yield
                turn(b)
                yield
                yield from attend(b)
            weave((route(0), 6))

            def after(n, gen):
                for _ in range(n):
                    yield
                yield from gen
            for b in range(NB):
                streams = [(hidden(b), 19)]
                if b + 1 < NB:
                    streams.append((after(8, route(b + 1)), 16))
                if b == 0:
                    streams.append((after(0, late(NB - 1)), 16))
                weave(*streams)

        cross = l0_xattn()
        tail = l0_attn(cross)
        barrier()
        next(cross)
        tail = cross.send(tail)
        if phases == 2:
            weave((tail, 1))
        barrier()
        layer1 = l1_attn() if phases > 3 else None
        if phases > 2:
            l0_ffn(tail, layer1)
        if phases > 3:
            next(layer1)
        barrier()
        done = []
        if phases > 4:
            add(NB - 1, *rest[1])
            l1_ffn(rest[0])
        else:
            if phases == 4:
                residual(NB - 1, *rest[0])
                turn(NB - 1)
            barrier()
            done.append(dma("out", io["out"], X[:]))
        SP.wait(*done)

        block = ctx.enter_context(nc.Block())

        @block.tensor
        def _(e):
            for f in PE.q:
                f(e)

        @block.vector
        def _(e):
            for f in DV.q:
                f(e)

        @block.scalar
        def _(e):
            for f in AC.q:
                f(e)

        @block.gpsimd
        def _(e):
            for f in PO.q:
                f(e)

        @block.sync
        def _(e):
            for f in SP.q:
                f(e)


OUTS = ["out"]
SCRATCH = {"s_g": ([128, 2048], F32), "s_x": ([2, 128, 2048], F32), "s_xq": ([2, 2, 128, 2, 512], F16), "s_xk": ([2, 2, 128, 2, 666], F16), "s_xm": ([4, 512], F16),
           "s_qk0": ([2, 2, 128, 512], F16), "s_m0": ([16, 512], F16)}
PHASES = 6


def kernel(**inputs):
    import concourse.bacc as bacc
    from concourse.bass_utils import run_bass_kernel_spmd

    a = {k: np.asarray(v) for k, v in inputs.items()}
    x = a["x"].reshape(NB * T, D)
    arrays = {
        "x_tm": x.reshape(NT, 128, D).transpose(1, 0, 2),
        "x_T": x.T,
        "ident": np.eye(128, dtype=np.float32),
        "qkv_w": a["L0_attn_qkv_weight"].T,
        "qkv_m": a["L0_attn_qkv_weight_mask"].T,
        "ow": a["L0_attn_out_weight"].T,
        "om": a["L0_attn_out_weight_mask"].T,
        "ob": a["L0_attn_out_bias"][None],
        "obm": a["L0_attn_out_bias_mask"][None],
    }
    ctx_pad = np.zeros((NB, 256, D), np.float32)
    ctx_pad[:, :TC] = a["ctx_1024"]
    sel = np.zeros((112, 8, 2, 64), np.float16)
    for r in (0, 32, 64, 96):
        for h in range(16):
            sel[r + h, h // 2, h % 2] = 1.0 / SEL
    arrays |= {
        "ctx_tm": ctx_pad.reshape(8, 128, D).transpose(1, 0, 2),
        "x_wq": a["L0_xattn_Wq"],
        "x_wk": a["L0_xattn_Wkv"][:, :1024],
        "x_wv": a["L0_xattn_Wkv"][:, 1024:],
        "x_wo": a["L0_xattn_Wo"].reshape(8, 128, D).transpose(1, 0, 2),
        "x_ln": np.stack([a["L0_xattn_ln1_g"], a["L0_xattn_ln1_b"], a["L0_xattn_ln2_g"], a["L0_xattn_ln2_b"]], 1),
        "sel16": sel.reshape(112, 8, 128),
        "zeros": np.zeros((8, 512), np.float16),
        "ones16": np.ones((8, 512), np.float16),
    }
    def experts(w):
        return w.transpose(1, 0, 2).reshape(D, -1)
    down = np.concatenate([a["L0_ffn_down_proj"].reshape(8, 128, D), a["L0_ffn_sh_down"].T[None]])
    mask = np.zeros((NB, 256), np.int32)
    mask[:, :TC] = a["mask_BxS2_ik1"]
    ii = np.arange(128)
    arrays |= {
        "m_up": experts(a["L0_ffn_up_proj"]),
        "m_gate": experts(a["L0_ffn_gate_proj"]),
        "m_down": down.transpose(1, 0, 2),
        "m_sg": a["L0_ffn_sh_gate"].T,
        "m_su": a["L0_ffn_sh_up"].T,
        "m_rw": a["L0_ffn_router_w"].T,
        "m_rb": a["L0_ffn_router_bias"][None],
        "iota16": np.tile(np.arange(16, dtype=np.float32), (128, 1)),
        "d_wq": a["L1_attn_Wq"],
        "d_wk": a["L1_attn_Wk"],
        "d_wv": a["L1_attn_Wv"],
        "d_wo": a["L1_attn_Wout"].reshape(8, 128, D).transpose(1, 0, 2),
        "d_wb": a["L1_attn_Wbeta"],
        "d_bb": a["L1_attn_b_beta"][None],
        "mask_l": (ii[None, :] // 32 < ii[:, None] // 32).astype(np.float32),
        "mask_u": (ii[:, None] <= ii[None, :]).astype(np.float32),
        "eye32": np.tile(np.eye(32, dtype=np.float32).reshape(1, 1024), (128, 1)),
        "y_wx": a["L1_xattn_Wx"].T,
        "y_wy": a["L1_xattn_Wy"].T,
        "y_wv": a["L1_xattn_Wv"].T,
        "ctx_T": a["ctx_1024"].reshape(NB * TC, D).T,
        "y_bxy": np.stack([a["L1_xattn_bx"], a["L1_xattn_by"]], 1),
        "y_bv": a["L1_xattn_bv"][None],
        "mask_c": mask.reshape(8, 128).T,
        "mask_r": a["mask_BxS2_ik1"].reshape(1, NB * TC),
        "f_w1": a["L1_ffn_W1"].transpose(1, 0, 2),
        "f_b1": a["L1_ffn_b1"],
        "f_wo": a["L1_ffn_Wo"].reshape(4, 128, D).transpose(1, 0, 2),
        "f_rw": a["L1_ffn_Wr"].T,
        "f_bo": a["L1_ffn_bo"][None],
        "f_gb": np.concatenate([a["L1_ffn_gamma"], a["L1_ffn_beta"]])[None],
        "sel8": np.repeat(np.eye(8, dtype=np.float16), 128, axis=1).reshape(8, 8, 128),
    }
    arrays = {k: np.ascontiguousarray(v) for k, v in arrays.items()}
    nc = bacc.Bacc("TRN2", target_bir_lowering=False, num_devices=1)
    io = {k: nc.dram_tensor(k, v.shape, mybir.dt.from_np(v.dtype), kind="ExternalInput").ap()
          for k, v in arrays.items()}
    io["out"] = nc.dram_tensor("out", [128, NT, 128], F32, kind="ExternalOutput").ap()
    for k, (shape, dt) in SCRATCH.items():
        io[k] = nc.dram_tensor(k, shape, dt).ap()
    build(nc, io, PHASES)
    r = run_bass_kernel_spmd(nc, [arrays], core_ids=[0])
    out = r.results[0]["out"]
    return np.ascontiguousarray(out.transpose(1, 0, 2)).reshape(NB, T, D)
```
